# Optimizing a Trainium2 kernel written in Bass

```python
import numpy as np
import jax
import jax.numpy as jnp

def _softmax(x, axis=-1):
    return jax.nn.softmax(x, axis=axis)

def _gelu(x):
    return jax.nn.gelu(x, approximate=True)

def _silu(x):
    return jax.nn.silu(x)

def _sigmoid(x):
    return jax.nn.sigmoid(x)

def _layernorm(x, axis=-1, eps=1e-05):
    m = jnp.mean(x, axis=axis, keepdims=True)
    v = jnp.var(x, axis=axis, keepdims=True)
    return (x - m) / jnp.sqrt(v + eps)

def _scatter_add(tgt, idx, src, axis=0):
    return tgt.at[idx].add(src)

def _segment_sum(src, seg, n):
    return jax.ops.segment_sum(src, seg, n)
kernel_name = 'mk_conv_attn_hybrid_d4_conv_nhwc1024_r4_eb88f5'

def setup_inputs(seed: int=0):
    np.random.seed(seed)
    _w = jnp.asarray

    def _rec_inputs():
        import jax
        import jax.numpy as jnp
        _gk = jax.random.key(seed)
        x = -0.0003929 + 0.9999 * jax.random.normal(jax.random.fold_in(_gk, 1), (8, 16, 32, 256), jnp.float32)
        return x
    x = _rec_inputs()

    def _L0_conv_setup():
        import jax, jax.numpy as jnp
        import numpy as np
        IN_DIM = 256
        LATENT = IN_DIM // 2
        B, T, N = (8, 16, 32)
        BN_EPS = 1e-05
        key = jax.random.key(seed)
        ks = jax.random.split(key, 5)
        std = np.sqrt(2.0 / IN_DIM)
        std_w = np.sqrt(2.0 / LATENT)
        x = jax.random.normal(ks[0], (B, T, N, IN_DIM), dtype=jnp.float32)
        Wt = jax.random.normal(ks[1], (LATENT, IN_DIM), dtype=jnp.float32) * std
        Wp = jax.random.normal(ks[2], (LATENT, IN_DIM), dtype=jnp.float32) * std
        Wg = jax.random.normal(ks[3], (LATENT, IN_DIM), dtype=jnp.float32) * std
        Ww = jax.random.normal(ks[4], (IN_DIM, LATENT), dtype=jnp.float32) * std_w
        gamma = jnp.ones((IN_DIM,), dtype=jnp.float32)
        beta = jnp.zeros((IN_DIM,), dtype=jnp.float32)
        return {'x': x, 'Wt': Wt, 'Wp': Wp, 'Wg': Wg, 'Ww': Ww, 'gamma': gamma, 'beta': beta}
    _L0_conv_all = _L0_conv_setup()
    _L0_conv_in = {k: v for k, v in _L0_conv_all.items() if k in ('Wt', 'Wp', 'Wg', 'Ww', 'gamma', 'beta')}
    del _L0_conv_all

    def _L1_conv_setup():
        import jax, jax.numpy as jnp
        import numpy as np
        IN_DIM = 256
        LATENT = IN_DIM // 2
        B, T, N = (8, 16, 32)
        BN_EPS = 1e-05
        key = jax.random.key(seed)
        ks = jax.random.split(key, 5)
        std = np.sqrt(2.0 / IN_DIM)
        std_w = np.sqrt(2.0 / LATENT)
        x = jax.random.normal(ks[0], (B, T, N, IN_DIM), dtype=jnp.float32)
        Wt = jax.random.normal(ks[1], (LATENT, IN_DIM), dtype=jnp.float32) * std
        Wp = jax.random.normal(ks[2], (LATENT, IN_DIM), dtype=jnp.float32) * std
        Wg = jax.random.normal(ks[3], (LATENT, IN_DIM), dtype=jnp.float32) * std
        Ww = jax.random.normal(ks[4], (IN_DIM, LATENT), dtype=jnp.float32) * std_w
        gamma = jnp.ones((IN_DIM,), dtype=jnp.float32)
        beta = jnp.zeros((IN_DIM,), dtype=jnp.float32)
        return {'x': x, 'Wt': Wt, 'Wp': Wp, 'Wg': Wg, 'Ww': Ww, 'gamma': gamma, 'beta': beta}
    _L1_conv_all = _L1_conv_setup()
    _L1_conv_in = {k: v for k, v in _L1_conv_all.items() if k in ('Wt', 'Wp', 'Wg', 'Ww', 'gamma', 'beta')}
    del _L1_conv_all

    def _L2_attn_setup():
        import jax, jax.numpy as jnp
        import numpy as np
        HID = 256
        NH = 16
        NKV = 4
        HD = 16
        B = 2
        S = 512
        SCALE = 1.0 / HD ** 0.5
        key = jax.random.key(seed)
        k1, k2, k3 = jax.random.split(key, 3)
        qkv_out = (NH + 2 * NKV) * HD
        return {'hidden_states': jax.random.normal(k1, (B, S, HID), dtype=jnp.float32), 'W_qkv': jax.random.normal(k2, (HID, qkv_out), dtype=jnp.float32) * 0.02, 'W_o': jax.random.normal(k3, (HID, HID), dtype=jnp.float32) * 0.02}
    _L2_attn_all = _L2_attn_setup()
    _L2_attn_in = {k: v for k, v in _L2_attn_all.items() if k in ('W_qkv', 'W_o')}
    del _L2_attn_all

    def _L2_ffn_setup():
        import jax, jax.numpy as jnp
        import numpy as np
        import math
        B, T, C = (4, 512, 256)
        E, K = (8, 2)
        EH, SH = (512, 1024)
        CAP_FACTOR = 1.25
        SCALING = 1.0
        FC_MULT = 1.0

        def _capacity(N, k):
            avg = math.ceil(N * k / E)
            return max(int(math.ceil(avg * CAP_FACTOR)), 1)
        key = jax.random.key(seed)
        ks = jax.random.split(key, 6)
        sd = 0.02
        return {'x': jax.random.normal(ks[0], (B, T, C), jnp.float32), 'proj_w': jax.random.normal(ks[1], (E, C), jnp.float32) * sd, 'proj_b': jnp.zeros((E,), jnp.float32), 'expert_bias': jnp.zeros((E,), jnp.float32), 'fc1_w': jax.random.normal(ks[2], (E, EH, C), jnp.float32) * sd, 'fc1_b': jnp.zeros((E, EH), jnp.float32), 'fc2_w': jax.random.normal(ks[3], (E, C, EH), jnp.float32) * sd, 'fc2_b': jnp.zeros((E, C), jnp.float32), 'sh1_w': jax.random.normal(ks[4], (SH, C), jnp.float32) * sd, 'sh1_b': jnp.zeros((SH,), jnp.float32), 'sh2_w': jax.random.normal(ks[5], (C, SH), jnp.float32) * sd, 'sh2_b': jnp.zeros((C,), jnp.float32)}
    _L2_ffn_all = _L2_ffn_setup()
    _L2_ffn_in = {k: v for k, v in _L2_ffn_all.items() if k in ('proj_w', 'proj_b', 'expert_bias', 'fc1_w', 'fc1_b', 'fc2_w', 'fc2_b', 'sh1_w', 'sh1_b', 'sh2_w', 'sh2_b')}
    del _L2_ffn_all

    def _L3_attn_setup():
        import jax, jax.numpy as jnp
        import numpy as np
        NH = 16
        NKV = 4
        D = 16
        BLK = 16
        KSEL = 16
        THETA = 10000.0

        def _rotate_half(x):
            x1, x2 = jnp.split(x, 2, axis=-1)
            return jnp.concatenate([-x2, x1], axis=-1)
        key = jax.random.key(seed)
        ks = jax.random.split(key, 8)
        B, S, Hm = (2, 512, 256)
        s = 0.02
        return {'hidden_states': jax.random.normal(ks[0], (B, S, Hm), jnp.float32), 'Wq': jax.random.normal(ks[1], (NH * D, Hm), jnp.float32) * s, 'Wk': jax.random.normal(ks[2], (NKV * D, Hm), jnp.float32) * s, 'Wv': jax.random.normal(ks[3], (NKV * D, Hm), jnp.float32) * s, 'Wo': jax.random.normal(ks[4], (Hm, NH * D), jnp.float32) * s, 'Wkc': jax.random.normal(ks[5], (D // 4, D), jnp.float32) * s, 'Wg_slc': jax.random.normal(ks[6], (NH, Hm), jnp.float32) * s, 'Wg_swa': jax.random.normal(ks[7], (NH, Hm), jnp.float32) * s}
    _L3_attn_all = _L3_attn_setup()
    _L3_attn_in = {k: v for k, v in _L3_attn_all.items() if k in ('Wq', 'Wk', 'Wv', 'Wo', 'Wkc', 'Wg_slc', 'Wg_swa')}
    del _L3_attn_all

    def _L3_ffn_setup():
        import jax, jax.numpy as jnp
        import numpy as np
        E = 8
        K = 2
        D = 256
        FF = 1024
        S, B = (512, 4)
        key = jax.random.key(seed)
        ks = jax.random.split(key, 5)
        scale_in = 0.02
        return {'x': jax.random.normal(ks[0], (S, B, D), dtype=jnp.float32), 'w1': jax.random.normal(ks[1], (E, D, FF), dtype=jnp.float32) * scale_in, 'b1': jnp.zeros((E, FF), dtype=jnp.float32), 'w2': jax.random.normal(ks[2], (E, FF, D), dtype=jnp.float32) * scale_in, 'b2': jnp.zeros((E, D), dtype=jnp.float32), 'gate_w': jax.random.normal(ks[3], (D, E), dtype=jnp.float32) * scale_in, 'gate_b': jnp.zeros((E,), dtype=jnp.float32), 'expert_biases': jnp.zeros((E,), dtype=jnp.float32)}
    _L3_ffn_all = _L3_ffn_setup()
    _L3_ffn_in = {k: v for k, v in _L3_ffn_all.items() if k in ('w1', 'b1', 'w2', 'b2', 'gate_w', 'gate_b', 'expert_biases')}
    del _L3_ffn_all
    return {'x': x, 'L0_conv_Wt': _L0_conv_in['Wt'], 'L0_conv_Wp': _L0_conv_in['Wp'], 'L0_conv_Wg': _L0_conv_in['Wg'], 'L0_conv_Ww': _L0_conv_in['Ww'], 'L0_conv_gamma': _L0_conv_in['gamma'], 'L0_conv_beta': _L0_conv_in['beta'], 'L1_conv_Wt': _L1_conv_in['Wt'], 'L1_conv_Wp': _L1_conv_in['Wp'], 'L1_conv_Wg': _L1_conv_in['Wg'], 'L1_conv_Ww': _L1_conv_in['Ww'], 'L1_conv_gamma': _L1_conv_in['gamma'], 'L1_conv_beta': _L1_conv_in['beta'], 'L2_attn_W_qkv': _L2_attn_in['W_qkv'], 'L2_attn_W_o': _L2_attn_in['W_o'], 'L2_ffn_proj_w': _L2_ffn_in['proj_w'], 'L2_ffn_proj_b': _L2_ffn_in['proj_b'], 'L2_ffn_expert_bias': _L2_ffn_in['expert_bias'], 'L2_ffn_fc1_w': _L2_ffn_in['fc1_w'], 'L2_ffn_fc1_b': _L2_ffn_in['fc1_b'], 'L2_ffn_fc2_w': _L2_ffn_in['fc2_w'], 'L2_ffn_fc2_b': _L2_ffn_in['fc2_b'], 'L2_ffn_sh1_w': _L2_ffn_in['sh1_w'], 'L2_ffn_sh1_b': _L2_ffn_in['sh1_b'], 'L2_ffn_sh2_w': _L2_ffn_in['sh2_w'], 'L2_ffn_sh2_b': _L2_ffn_in['sh2_b'], 'L3_attn_Wq': _L3_attn_in['Wq'], 'L3_attn_Wk': _L3_attn_in['Wk'], 'L3_attn_Wv': _L3_attn_in['Wv'], 'L3_attn_Wo': _L3_attn_in['Wo'], 'L3_attn_Wkc': _L3_attn_in['Wkc'], 'L3_attn_Wg_slc': _L3_attn_in['Wg_slc'], 'L3_attn_Wg_swa': _L3_attn_in['Wg_swa'], 'L3_ffn_w1': _L3_ffn_in['w1'], 'L3_ffn_b1': _L3_ffn_in['b1'], 'L3_ffn_w2': _L3_ffn_in['w2'], 'L3_ffn_b2': _L3_ffn_in['b2'], 'L3_ffn_gate_w': _L3_ffn_in['gate_w'], 'L3_ffn_gate_b': _L3_ffn_in['gate_b'], 'L3_ffn_expert_biases': _L3_ffn_in['expert_biases']}

def reference(x, L0_conv_Wt, L0_conv_Wp, L0_conv_Wg, L0_conv_Ww, L0_conv_gamma, L0_conv_beta, L1_conv_Wt, L1_conv_Wp, L1_conv_Wg, L1_conv_Ww, L1_conv_gamma, L1_conv_beta, L2_attn_W_qkv, L2_attn_W_o, L2_ffn_proj_w, L2_ffn_proj_b, L2_ffn_expert_bias, L2_ffn_fc1_w, L2_ffn_fc1_b, L2_ffn_fc2_w, L2_ffn_fc2_b, L2_ffn_sh1_w, L2_ffn_sh1_b, L2_ffn_sh2_w, L2_ffn_sh2_b, L3_attn_Wq, L3_attn_Wk, L3_attn_Wv, L3_attn_Wo, L3_attn_Wkc, L3_attn_Wg_slc, L3_attn_Wg_swa, L3_ffn_w1, L3_ffn_b1, L3_ffn_w2, L3_ffn_b2, L3_ffn_gate_w, L3_ffn_gate_b, L3_ffn_expert_biases):
    import jax
    import jax.numpy as jnp

    def _L0_conv_ref(x, Wt, Wp, Wg, Ww, gamma, beta):
        import jax, jax.numpy as jnp
        import numpy as np
        IN_DIM = 256
        LATENT = IN_DIM // 2
        B, T, N = (8, 16, 32)
        BN_EPS = 1e-05
        Bv, Tv, Nv, C = x.shape
        th = jnp.einsum('btnc,lc->btnl', x, Wt)
        ph = jnp.einsum('btnc,lc->btnl', x, Wp)
        g = jnp.einsum('btnc,lc->btnl', x, Wg)
        sw = jnp.einsum('bikl,bijl->bijk', ph, th)
        spatio = jnp.einsum('bijk,bikl->bijl', sw, g) / Nv
        tw = jnp.einsum('btjl,bijl->bijt', ph, th)
        temporal = jnp.einsum('bijt,btjl->bijl', tw, g) / Tv
        st = (spatio + temporal) / (Tv + Nv)
        out = jnp.einsum('bijl,cl->bijc', st, Ww) + x
        mean = out.mean(axis=(0, 1, 2))
        var = out.var(axis=(0, 1, 2))
        return (out - mean) * jax.lax.rsqrt(var + BN_EPS) * gamma + beta

    def _L1_conv_ref(x, Wt, Wp, Wg, Ww, gamma, beta):
        import jax, jax.numpy as jnp
        import numpy as np
        IN_DIM = 256
        LATENT = IN_DIM // 2
        B, T, N = (8, 16, 32)
        BN_EPS = 1e-05
        Bv, Tv, Nv, C = x.shape
        th = jnp.einsum('btnc,lc->btnl', x, Wt)
        ph = jnp.einsum('btnc,lc->btnl', x, Wp)
        g = jnp.einsum('btnc,lc->btnl', x, Wg)
        sw = jnp.einsum('bikl,bijl->bijk', ph, th)
        spatio = jnp.einsum('bijk,bikl->bijl', sw, g) / Nv
        tw = jnp.einsum('btjl,bijl->bijt', ph, th)
        temporal = jnp.einsum('bijt,btjl->bijl', tw, g) / Tv
        st = (spatio + temporal) / (Tv + Nv)
        out = jnp.einsum('bijl,cl->bijc', st, Ww) + x
        mean = out.mean(axis=(0, 1, 2))
        var = out.var(axis=(0, 1, 2))
        return (out - mean) * jax.lax.rsqrt(var + BN_EPS) * gamma + beta

    def _L2_attn_ref(hidden_states, W_qkv, W_o):
        import jax, jax.numpy as jnp
        import numpy as np
        HID = 256
        NH = 16
        NKV = 4
        HD = 16
        B = 2
        S = 512
        SCALE = 1.0 / HD ** 0.5
        b, s, _ = hidden_states.shape
        rep = NH // NKV
        qkv = hidden_states @ W_qkv
        q, k, v = jnp.split(qkv, [NH * HD, (NH + NKV) * HD], axis=-1)
        q = q.reshape(b, s, NH, HD).transpose(0, 2, 1, 3)
        k = k.reshape(b, s, NKV, HD).transpose(0, 2, 1, 3)
        v = v.reshape(b, s, NKV, HD).transpose(0, 2, 1, 3)
        qg = q.reshape(b, NKV, rep, s, HD)
        scores = jnp.einsum('bgrqd,bgkd->bgrqk', qg, k) * SCALE
        causal = jnp.triu(jnp.ones((s, s), dtype=bool), k=1)
        scores = jnp.where(causal, jnp.finfo(scores.dtype).min, scores)
        attn = jax.nn.softmax(scores, axis=-1)
        out = jnp.einsum('bgrqk,bgkd->bgrqd', attn, v)
        out = out.reshape(b, NH, s, HD).transpose(0, 2, 1, 3).reshape(b, s, NH * HD)
        return out @ W_o

    def _L2_ffn_ref(x, proj_w, proj_b, expert_bias, fc1_w, fc1_b, fc2_w, fc2_b, sh1_w, sh1_b, sh2_w, sh2_b):
        import jax, jax.numpy as jnp
        import numpy as np
        import math
        B, T, C = (4, 512, 256)
        E, K = (8, 2)
        EH, SH = (512, 1024)
        CAP_FACTOR = 1.25
        SCALING = 1.0
        FC_MULT = 1.0

        def _capacity(N, k):
            avg = math.ceil(N * k / E)
            return max(int(math.ceil(avg * CAP_FACTOR)), 1)
        Bx, Tx, Cx = x.shape
        N = Bx * Tx
        xf = x.reshape(N, Cx)
        z = xf @ proj_w.T + proj_b
        s = jax.nn.sigmoid(z) + expert_bias
        logits = jnp.log(jnp.clip(s, 1e-12)) * SCALING
        probs = jax.nn.softmax(logits, axis=-1)
        topk_w, topk_idx = jax.lax.top_k(probs, K)
        topk_w = topk_w / jnp.clip(topk_w.sum(-1, keepdims=True), 1e-12)
        pair_e = topk_idx.reshape(-1)
        pair_w = topk_w.reshape(-1)
        pair_tok = jnp.repeat(jnp.arange(N), K)
        cap = _capacity(N, K)
        assigned = pair_e[None, :] == jnp.arange(E)[:, None]
        wmat = jnp.where(assigned, pair_w[None, :], -jnp.inf)
        kept_w, kept_pair = jax.lax.top_k(wmat, cap)
        valid = kept_w > -jnp.inf
        kept_w = jnp.where(valid, kept_w, 0.0)
        kept_tok = pair_tok[kept_pair]
        xe = xf[kept_tok]
        h = jax.nn.gelu(jnp.einsum('ecd,ehd->ech', xe, fc1_w) + fc1_b[:, None, :], approximate=False)
        oe = jnp.einsum('ech,edh->ecd', h, fc2_w) + fc2_b[:, None, :]
        contrib = oe * kept_w[..., None]
        y = jnp.zeros((N, Cx), x.dtype).at[kept_tok.reshape(-1)].add(contrib.reshape(-1, Cx))
        sh = jax.nn.gelu(xf @ sh1_w.T + sh1_b, approximate=False) @ sh2_w.T + sh2_b
        return ((sh + y) * FC_MULT).reshape(Bx, Tx, Cx)

    def _L3_attn_ref(hidden_states, Wq, Wk, Wv, Wo, Wkc, Wg_slc, Wg_swa):
        import jax, jax.numpy as jnp
        import numpy as np
        NH = 16
        NKV = 4
        D = 16
        BLK = 16
        KSEL = 16
        THETA = 10000.0

        def _rotate_half(x):
            x1, x2 = jnp.split(x, 2, axis=-1)
            return jnp.concatenate([-x2, x1], axis=-1)
        B, S, Hm = hidden_states.shape
        g_slc = jax.nn.sigmoid(hidden_states @ Wg_slc.T)
        g_swa = jax.nn.sigmoid(hidden_states @ Wg_swa.T)
        q = (hidden_states @ Wq.T).reshape(B, S, NH, D)
        k = (hidden_states @ Wk.T).reshape(B, S, NKV, D)
        v = (hidden_states @ Wv.T).reshape(B, S, NKV, D)
        inv_freq = 1.0 / THETA ** (jnp.arange(0, D, 2, dtype=jnp.float32) / D)
        freqs = jnp.arange(S, dtype=jnp.float32)[:, None] * inv_freq
        emb = jnp.concatenate([freqs, freqs], axis=-1)
        cos = jnp.cos(emb)[None, :, None, :]
        sin = jnp.sin(emb)[None, :, None, :]
        q = q * cos + _rotate_half(q) * sin
        k = k * cos + _rotate_half(k) * sin
        groups = NH // NKV
        k = jnp.repeat(k, groups, axis=2)
        v = jnp.repeat(v, groups, axis=2)
        nb = S // BLK
        kc = k @ Wkc.T
        k_block_mean = kc.reshape(B, nb, BLK, NH, D // 4).mean(axis=2)
        qc = q @ Wkc.T
        block_scores = jnp.einsum('bshd,bnhd->bhsn', qc, k_block_mean)
        block_scores = block_scores / jnp.sqrt(jnp.float32(D // 4))
        pos_blocks = jnp.arange(S) // BLK
        bmask = jnp.arange(nb)[None, :] <= pos_blocks[:, None]
        block_scores = jnp.where(bmask[None, None], block_scores, -jnp.inf)
        _, top_idx = jax.lax.top_k(block_scores, min(KSEL, nb))
        top_idx = jnp.sort(top_idx, axis=-1)
        del top_idx
        scale = 1.0 / jnp.sqrt(jnp.float32(D))
        scores = jnp.einsum('bqhd,bkhd->bhqk', q, k) * scale
        cmask = jnp.tril(jnp.ones((S, S), dtype=bool))
        scores = jnp.where(cmask[None, None], scores, -jnp.inf)
        p = jax.nn.softmax(scores, axis=-1)
        attn = jnp.einsum('bhqk,bkhd->bqhd', p, v)
        out = attn * (g_slc + g_swa)[..., None]
        out = out.reshape(B, S, NH * D)
        return out @ Wo.T

    def _L3_ffn_ref(x, w1, b1, w2, b2, gate_w, gate_b, expert_biases):
        import jax, jax.numpy as jnp
        import numpy as np
        E = 8
        K = 2
        D = 256
        FF = 1024
        S, B = (512, 4)
        s, b, d = x.shape
        xf = x.reshape(-1, d)
        scores = xf @ gate_w + gate_b
        gate_probs = jax.nn.sigmoid(scores)
        gate_logits = scores + expert_biases
        _, topk_idx = jax.lax.top_k(gate_logits, K)
        top_k_probs = jnp.take_along_axis(gate_probs, topk_idx, axis=-1)
        top_k_probs = top_k_probs / top_k_probs.sum(axis=-1, keepdims=True)
        combine = (jax.nn.one_hot(topk_idx, E, dtype=xf.dtype) * top_k_probs[..., None]).sum(axis=1)
        out = jnp.zeros_like(xf)
        for e in range(E):
            h = jax.nn.relu(xf @ w1[e] + b1[e])
            out = out + combine[:, e:e + 1] * (h @ w2[e] + b2[e])
        return out.reshape(s, b, d)

    def _gn(v, G=32, eps=1e-05):
        B_, H_, W_, C_ = v.shape
        g = v.reshape(B_, H_, W_, G, C_ // G)
        m = jnp.mean(g, axis=(1, 2, 4), keepdims=True)
        s = jnp.var(g, axis=(1, 2, 4), keepdims=True)
        return ((g - m) / jnp.sqrt(s + eps)).reshape(v.shape)

    def _ln_c(v, eps=1e-06):
        m = jnp.mean(v, axis=-1, keepdims=True)
        s = jnp.var(v, axis=-1, keepdims=True)
        return (v - m) / jnp.sqrt(s + eps)

    def _ln_t(v, eps=1e-05):
        m = jnp.mean(v, axis=-1, keepdims=True)
        s = jnp.var(v, axis=-1, keepdims=True)
        return (v - m) / jnp.sqrt(s + eps)

    def _to_tokens(v):
        B_, H_, W_, C_ = v.shape
        return v.reshape(B_, H_ * W_, C_)

    def _from_tokens(t, like):
        return t.reshape(like.shape)
    x = _L0_conv_ref(x, L0_conv_Wt, L0_conv_Wp, L0_conv_Wg, L0_conv_Ww, L0_conv_gamma, L0_conv_beta)
    x = _L1_conv_ref(x, L1_conv_Wt, L1_conv_Wp, L1_conv_Wg, L1_conv_Ww, L1_conv_gamma, L1_conv_beta)
    t = _to_tokens(x)
    t = t + _L2_attn_ref(_ln_t(t), L2_attn_W_qkv, L2_attn_W_o)
    t = t + _L2_ffn_ref(_ln_t(t), L2_ffn_proj_w, L2_ffn_proj_b, L2_ffn_expert_bias, L2_ffn_fc1_w, L2_ffn_fc1_b, L2_ffn_fc2_w, L2_ffn_fc2_b, L2_ffn_sh1_w, L2_ffn_sh1_b, L2_ffn_sh2_w, L2_ffn_sh2_b)
    t = t + _L3_attn_ref(_ln_t(t), L3_attn_Wq, L3_attn_Wk, L3_attn_Wv, L3_attn_Wo, L3_attn_Wkc, L3_attn_Wg_slc, L3_attn_Wg_swa)
    t = t + _L3_ffn_ref(_ln_t(t), L3_ffn_w1, L3_ffn_b1, L3_ffn_w2, L3_ffn_b2, L3_ffn_gate_w, L3_ffn_gate_b, L3_ffn_expert_biases)
    x = _from_tokens(t, x)
    return x

_drawn_inputs = setup_inputs


def setup_inputs(seed=0):
    import zlib

    import numpy as np

    out = dict(_drawn_inputs(seed))
    spreads = {'L0_conv_gamma': (1.0, 0.2),
     'L0_conv_beta': (0.0, 0.1),
     'L1_conv_gamma': (1.0, 0.2),
     'L1_conv_beta': (0.0, 0.1),
     'L2_ffn_proj_b': (0.0, 0.1),
     'L2_ffn_expert_bias': (0.0, 0.1),
     'L2_ffn_fc1_b': (0.0, 0.428),
     'L2_ffn_fc2_b': (0.0, 0.1),
     'L2_ffn_sh1_b': (0.0, 0.1),
     'L2_ffn_sh2_b': (0.0, 0.1),
     'L3_ffn_b1': (0.0, 0.28),
     'L3_ffn_b2': (0.0, 0.1),
     'L3_ffn_gate_b': (0.0, 0.1),
     'L3_ffn_expert_biases': (0.0, 0.1)}
    factors = {'L2_attn_W_qkv': 2.938,
     'L2_attn_W_o': 2.759,
     'L3_attn_Wq': 8.0,
     'L3_attn_Wk': 8.0,
     'L3_attn_Wg_slc': 8.0,
     'L3_attn_Wg_swa': 8.0}
    for name, (base, spread) in spreads.items():
        noise = np.random.default_rng([zlib.crc32(name.encode()), seed]).standard_normal(out[name].shape)
        drawn = base * np.exp(spread * noise) if base else spread * noise
        out[name] = jnp.asarray(drawn.astype(out[name].dtype))
    for name, factor in factors.items():
        out[name] = (out[name] * factor).astype(out[name].dtype)
    return out
```

```python
from contextlib import ExitStack

import numpy as np

import concourse.bass as bass
from concourse import mybir

F32 = mybir.dt.float32
BF16 = mybir.dt.bfloat16
I32 = mybir.dt.int32
U32 = mybir.dt.uint32
ALU = mybir.AluOpType
ACT = mybir.ActivationFunctionType
AX = mybir.AxisListType
ds = bass.ds

P = 128
B, T, N, C = 8, 16, 32, 256
LAT = C // 2
S = T * N
TOK = B * S
KC = C // P
NT = TOK // P
TB = S // P
NH, NKV, HD = 16, 4, 16
GR = NH // NKV
E = 8
CAP = 1280
SLOT_TILES = 2 * TOK // P + E
SLOTS = SLOT_TILES * P
BN_EPS = 1e-5
LN_EPS = 1e-5


def host_constants():
    tok = np.arange(S)
    same_time = tok[:, None] // N == tok[None, :] // N
    same_joint = tok[:, None] % N == tok[None, :] % N
    mix = (same_time / np.float32(N) + same_joint / np.float32(T)) / np.float32(T + N)
    mix = mix.astype(np.float32).reshape(TB, P, S).transpose(1, 0, 2)
    q, k = np.arange(P)[:, None], np.arange(P)[None, :]
    inv = np.float32(1.0) / np.float32(10000.0) ** (np.arange(0, HD, 2, dtype=np.float32) / np.float32(HD))
    freqs = np.arange(S, dtype=np.float32)[:, None] * inv.astype(np.float32)
    emb = np.concatenate([freqs, freqs], axis=-1)
    width_of = (np.arange(P) % (GR * HD) // GR, np.arange(P) % HD)
    step_of = (GR, 1)
    rope = np.stack([f(emb).T[w] for w in width_of for f in (np.cos, np.sin)], 1)
    swap = np.zeros((P, 2, P), np.float32)
    for j, (w, step) in enumerate(zip(width_of, step_of)):
        for r in range(P):
            if w[r] < HD // 2:
                swap[r + step * HD // 2, j, r] = -1.0
            else:
                swap[r - step * HD // 2, j, r] = 1.0
    return {
        "c_ident": np.eye(P, dtype=np.float32),
        "c_mix": np.ascontiguousarray(mix),
        "c_causal": np.where(k > q, np.float32(-1e30), np.float32(0)).astype(np.float32),
        "c_rope": np.ascontiguousarray(rope.astype(np.float32)),
        "c_swap": swap,
        "c_before": (q < k).astype(np.float32),
        "c_expert": np.ascontiguousarray(np.broadcast_to(np.arange(E, dtype=np.float32), (P, E))),
        "c_tilestart": np.ascontiguousarray(np.broadcast_to(
            np.arange(SLOT_TILES, dtype=np.float32) * P, (P, SLOT_TILES))),
        "c_bits": np.ascontiguousarray(np.broadcast_to(
            (1 << np.arange(29, -1, -1)).astype(np.int32)[:, None], (P, 30, E))),
        "c_lane": np.ascontiguousarray(np.broadcast_to(np.arange(P, dtype=np.float32), (P, P))),
    }


class Order:

    def __init__(self, engine, semaphore, base=0):
        self.engine, self.semaphore, self.base, self.n = engine, semaphore, base, 0

    def did(self, instruction):
        instruction.then_inc(self.semaphore, 1)
        self.n += 1
        return self.n

    def wait(self):
        self.engine.wait_ge(self.semaphore, self.base + self.n)


class Net:

    def __init__(self, nc, ctx, dram):
        self.nc, self.ctx, self.dram = nc, ctx, dram
        self.part, self.sems = 0, []
        self.going = self.sem("going0")
        self.ident = self.sb("ident", [P, P], F32)
        self.x = self.sb("x_tokens", [P, NT, C], F32)
        self.xT = None

    def hold_channels(self, tag, ctx):
        self.xT = self.sb(f"{tag}_x_channels", [P, KC, TOK], F32, ctx)

    def go_on(self, engine):
        engine.sem_inc(self.going, 1)

    def sb(self, name, shape, dt, ctx=None):
        return (ctx or self.ctx).enter_context(self.nc.sbuf_tensor(name, shape, dt))

    def ps(self, name, shape, dt, ctx):
        return ctx.enter_context(self.nc.psum_tensor(name, shape, dt))

    def sem(self, name):
        semaphore = self.nc.alloc_semaphore(name=name)
        self.sems.append(semaphore)
        return semaphore

    def clear_semaphores(self):
        self.nc.clear_and_free_semaphores(self.sems)
        self.nc.all_engine_barrier()
        self.part += 1
        self.sems = []
        self.going = self.sem(f"going{self.part}")


def load_tokens(net):
    nc = net.nc
    with ExitStack() as ctx:
        ring = [net.sb(f"load_ring{p}", [P, TB, C], F32, ctx) for p in range(2)]
        turned = net.ps("load_turned", [P, 2, KC, S], F32, ctx)
        const_in = net.sem("load_const_in")
        loaded = [net.sem(f"load_loaded{p}") for p in range(2)]
        turned_ready = net.sem("load_turned_ready")
        copied_a = net.sem("load_copied_a")
        copied_v = net.sem("load_copied_v")
        x_tiles = net.dram["x"].rearrange("b t n c -> (b t n) c").rearrange("(u p) c -> p u c", p=P)
        with nc.Block() as block:
            @block.sync
            def _(sp):
                sp.dma_start(net.ident[:, :], net.dram["c_ident"]).then_inc(const_in, 16)

                def load(b, p):
                    sp.dma_start(ring[p][:, :, :], x_tiles[:, ds(b * TB, TB), :]).then_inc(loaded[p], 16)
                load(0, 0)
                load(1, 1)
                with sp.Fori(1, B // 2) as i:
                    for p in range(2):
                        sp.wait_ge(turned_ready, i * 2 + p - 1)
                        net.go_on(sp)
                        load(i * 2 + p, p)

            @block.tensor
            def _(pe):
                pe.wait_ge(const_in, 16)

                def turn(b, p, first):
                    if not first:
                        pe.wait_ge(copied_a, b - 1)
                        pe.wait_ge(copied_v, b - 1)
                    for c in range(KC):
                        for t in range(TB):
                            last = pe.transpose(turned[:, p, c, t * P:(t + 1) * P],
                                                ring[p][:, t, c * P:(c + 1) * P], net.ident[:, :])
                    last.then_inc(turned_ready, 1)
                for p in range(2):
                    pe.wait_ge(loaded[p], 16)
                    turn(p, p, True)
                with pe.Fori(1, B // 2) as i:
                    for p in range(2):
                        pe.wait_ge(loaded[p], i * 16 + 16)
                        turn(i * 2 + p, p, False)

            @block.scalar
            def _(act):
                with act.Fori(0, B // 2) as i:
                    for p in range(2):
                        act.wait_ge(turned_ready, i * 2 + p + 1)
                        act.activation(net.xT[:, 0, ds((i * 2 + p) * S, S)], turned[:, p, 0, :],
                                       ACT.Copy).then_inc(copied_a, 1)

            @block.vector
            def _(dve):
                with dve.Fori(0, B // 2) as i:
                    for p in range(2):
                        dve.wait_ge(turned_ready, i * 2 + p + 1)
                        dve.tensor_copy(net.xT[:, 1, ds((i * 2 + p) * S, S)],
                                        turned[:, p, 1, :]).then_inc(copied_v, 1)


def inverse_root(net, eng_steps, dve, var, root, out, tmp, sqrt_asked, sqrt_done, asked):
    s = eng_steps
    s.wait()
    dve.tensor_copy(root, var).then_inc(sqrt_asked, 1)
    dve.wait_ge(sqrt_done, asked)
    s.did(dve.reciprocal(out, root))
    s.wait()
    s.did(dve.tensor_tensor(tmp, out, out, ALU.mult))
    s.wait()
    s.did(dve.tensor_tensor(tmp, tmp, var, ALU.mult))
    s.wait()
    s.did(dve.tensor_scalar(tmp, tmp, -0.5, 1.5, ALU.mult, ALU.add))
    s.wait()
    s.did(dve.tensor_tensor(out, out, tmp, ALU.mult))


def conv_block(net, layer, to_tokens):
    nc = net.nc
    n_ = f"L{layer}"
    with ExitStack() as ctx:
        sb = lambda name, shape, dt=F32: net.sb(f"{n_}_{name}", shape, dt, ctx)
        sem = lambda name: net.sem(f"{n_}_{name}")
        w_in = sb("w_in", [P, 3, C])
        ww_in = sb("ww_in", [P, KC, LAT])
        affine = sb("affine", [P, 2, KC])
        wT = sb("wT", [P, KC, 3, LAT])
        wwT = sb("wwT", [P, C])
        mix = sb("mix", [P, TB, S])
        xb = [sb(f"xb{p}", [P, KC, S]) for p in range(2)]
        theta = [sb(f"theta{p}", [P, S]) for p in range(2)]
        phi = [sb(f"phi{p}", [P, S]) for p in range(2)]
        g = [sb(f"g{p}", [P, TB, LAT]) for p in range(2)]
        mixed = [sb(f"mixed{p}", [P, TB, S]) for p in range(2)]
        st = [sb(f"st{p}", [P, S]) for p in range(2)]
        stats = sb("stats", [P, KC, B, 6])
        norm = sb("norm", [P, 12, KC])
        mv = sb("mv", [P, KC, 2])
        turned = net.ps(f"{n_}_ps_turned", [P, S], F32, ctx)
        ps_phi = net.ps(f"{n_}_ps_phi", [P, S], F32, ctx)
        ps_g = net.ps(f"{n_}_ps_g", [P, TB, LAT], F32, ctx)
        ps_s = net.ps(f"{n_}_ps_s", [P, 2, S], F32, ctx)
        ps_st = net.ps(f"{n_}_ps_st", [P, S], F32, ctx)
        ps_out = net.ps(f"{n_}_ps_out", [P, KC, S], F32, ctx)
        ps_theta = turned

        w_loaded = sem("w_loaded")
        mix_loaded = sem("mix_loaded")
        affine_loaded = sem("affine_loaded")
        w_turned = sem("w_turned")
        w_ready = sem("w_ready")
        xb_ready = sem("xb_ready")
        projected = sem("projected")
        proj_copied = sem("proj_copied")
        scored = sem("scored")
        masked = sem("masked")
        st_ready = sem("st_ready")
        st_copied = sem("st_copied")
        out_ready = sem("out_ready")
        out_added = sem("out_added")
        stats_step = sem("stats_step")
        sqrt_asked, sqrt_done = sem("sqrt_asked"), sem("sqrt_done")
        norm_step = sem("norm_step")
        norm_ready = sem("norm_ready")
        bn_done_a, bn_done_v = sem("bn_done_a"), sem("bn_done_v")
        bn_turned = sem("bn_turned")
        bn_copied_a, bn_copied_v = sem("bn_copied_a"), sem("bn_copied_v")

        mean, var, root, inv, scale, shift, tmp = (norm[:, j, :] for j in range(7))

        with nc.Block() as block:
            @block.sync
            def _(sp):
                for j, w in enumerate(("Wt", "Wp", "Wg")):
                    sp.dma_start(w_in[:, j, :], net.dram[f"L{layer}_conv_{w}"]).then_inc(w_loaded, 16)
                sp.dma_start(ww_in[:, :, :], net.dram[f"L{layer}_conv_Ww"].rearrange("(k p) l -> p k l", p=P)
                             ).then_inc(w_loaded, 16)
                sp.dma_start(mix[:, :, :], net.dram["c_mix"]).then_inc(mix_loaded, 16)
                for j, w in enumerate(("gamma", "beta")):
                    for c in range(KC):
                        sp.dma_start(affine[:, j, c:c + 1],
                                     net.dram[f"L{layer}_conv_{w}"][c * P:(c + 1) * P].rearrange("(p a) -> p a", a=1)
                                     ).then_inc(affine_loaded, 16)

            @block.tensor
            def _(pe):
                pe.wait_ge(w_loaded, 64)
                for j in range(3):
                    for k in range(KC):
                        bank, at = ((ps_s[:, 0, :], 2 * j + k) if 2 * j + k < 4 else (ps_s[:, 1, :], 2 * j + k - 4))
                        pe.transpose(bank[:, at * P:(at + 1) * P], w_in[:, j, k * P:(k + 1) * P], net.ident[:, :])
                for c in range(KC):
                    last = pe.transpose(ps_s[:, 1, (2 + c) * P:(3 + c) * P], ww_in[:, c, :], net.ident[:, :])
                last.then_inc(w_turned, 1)
                pe.wait_ge(w_ready, 2)

                def project(b, p, first):
                    pe.wait_ge(xb_ready, b + 1)
                    for j, out in enumerate((ps_theta, ps_phi)):
                        if not first:
                            pe.wait_ge(proj_copied, b * 3 + j - 2)
                        for k in range(KC):
                            last = pe.matmul(out[:, :], wT[:, k, j, :], xb[p][:, k, :], start=k == 0, stop=k == KC - 1)
                        last.then_inc(projected, 1)
                    if not first:
                        pe.wait_ge(proj_copied, b * 3)
                    for t in range(TB):
                        for k in range(KC):
                            last = pe.matmul(ps_g[:, t, :], xb[p][:, k, t * P:(t + 1) * P], wT[:, k, 2, :],
                                             start=k == 0, stop=k == KC - 1)
                    last.then_inc(projected, 1)

                def score(b, p, first):
                    pe.wait_ge(proj_copied, b * 3 + 2)
                    for kb in range(TB):
                        if not (first and kb < 2):
                            pe.wait_ge(masked, b * TB + kb - 1)
                        pe.matmul(ps_s[:, kb % 2, :], phi[p][:, kb * P:(kb + 1) * P], theta[p][:, :],
                                  start=True, stop=True).then_inc(scored, 1)

                def output(b, p, first):
                    pe.wait_ge(proj_copied, b * 3 + 3)
                    pe.wait_ge(masked, b * TB + TB)
                    if not first:
                        pe.wait_ge(st_copied, b)
                    for kb in range(TB):
                        last = pe.matmul(ps_st[:, :], g[p][:, kb, :], mixed[p][:, kb, :],
                                         start=kb == 0, stop=kb == TB - 1)
                    last.then_inc(st_ready, 1)
                    pe.wait_ge(st_copied, b + 1)
                    if not first:
                        pe.wait_ge(out_added, b * KC)
                    for c in range(KC):
                        pe.matmul(ps_out[:, c, :], wwT[:, c * P:(c + 1) * P], st[p][:, :],
                                  start=True, stop=True).then_inc(out_ready, 1)

                project(0, 0, True)
                score(0, 0, True)
                project(1, 1, False)
                score(1, 1, False)
                output(0, 0, True)
                with pe.Fori(1, B // 2) as i:
                    for p in range(2):
                        project(i * 2 + p, p, False)
                        score(i * 2 + p, p, False)
                        output(i * 2 + p - 1, 1 - p, False)
                output(B - 1, 1, False)
                if to_tokens:
                    def turn(b, p, first):
                        pe.wait_ge(bn_done_a, b + 1)
                        pe.wait_ge(bn_done_v, b + 1)
                        if not first:
                            pe.wait_ge(bn_copied_a, b - 1)
                            pe.wait_ge(bn_copied_v, b - 1)
                        dst = (ps_out, ps_s)[p]
                        for t in range(TB):
                            for c in range(KC):
                                last = pe.transpose(dst[:, t // 2, (t % 2) * C + c * P:(t % 2) * C + (c + 1) * P],
                                                    xb[p][:, c, t * P:(t + 1) * P], net.ident[:, :])
                        last.then_inc(bn_turned, 1)
                    turn(0, 0, True)
                    turn(1, 1, True)
                    with pe.Fori(1, B // 2) as i:
                        for p in range(2):
                            turn(i * 2 + p, p, False)

            @block.scalar
            def _(act):
                def fetch(b, p, first):
                    if not first:
                        act.wait_ge(projected, b * 3 - 3)
                    act.activation(xb[p][:, :, :], net.xT[:, :, ds(b * S, S)], ACT.Copy).then_inc(xb_ready, 1)

                def copy_projections(b, p, first):
                    for j, (src, dst) in enumerate(((ps_theta, theta), (ps_phi, phi), (ps_g, g))):
                        act.wait_ge(projected, b * 3 + j + 1)
                        if j == 0 and not first:
                            act.wait_ge(st_ready, b - 1)
                        act.activation(dst[p][:], src[:], ACT.Copy).then_inc(proj_copied, 1)

                def copy_st(b, p):
                    act.wait_ge(st_ready, b + 1)
                    act.activation(st[p][:, :], ps_st[:, :], ACT.Copy).then_inc(st_copied, 1)
                act.wait_ge(w_ready, 2)
                fetch(0, 0, True)
                fetch(1, 1, True)
                copy_projections(0, 0, True)
                copy_projections(1, 1, True)
                fetch(2, 0, False)
                copy_st(0, 0)
                with act.Fori(1, B // 2 - 1) as i:
                    for p in range(2):
                        copy_projections(i * 2 + p, p, False)
                        fetch(i * 2 + p + 1, 1 - p, False)
                        copy_st(i * 2 + p - 1, 1 - p)
                copy_projections(B - 2, 0, False)
                fetch(B - 1, 1, False)
                copy_st(B - 3, 1)
                copy_projections(B - 1, 1, False)
                copy_st(B - 2, 0)
                copy_st(B - 1, 1)
                act.wait_ge(sqrt_asked, 1)
                act.activation(root, root, ACT.Sqrt).then_inc(sqrt_done, 1)
                act.wait_ge(norm_ready, 1)
                if not to_tokens:
                    act.activation(net.xT[:, 0, :], net.xT[:, 0, :], ACT.Identity, bias=shift[:, 0:1],
                                   scale=scale[:, 0:1]).then_inc(bn_done_a, 1)
                else:
                    def norm0(b, p, first):
                        if not first:
                            act.wait_ge(bn_turned, b - 1)
                        act.activation(xb[p][:, 0, :], net.xT[:, 0, ds(b * S, S)], ACT.Identity,
                                       bias=shift[:, 0:1], scale=scale[:, 0:1]).then_inc(bn_done_a, 1)

                    def take(b, p):
                        act.wait_ge(bn_turned, b + 1)
                        act.activation(net.x[:, ds(b * TB, 2), :], (ps_out, ps_s)[p][:, 0, :].rearrange(
                            "p (t c) -> p t c", c=C), ACT.Copy).then_inc(bn_copied_a, 1)
                    norm0(0, 0, True)
                    norm0(1, 1, True)
                    with act.Fori(1, B // 2) as i:
                        for p in range(2):
                            take(i * 2 + p - 2, p)
                            norm0(i * 2 + p, p, False)
                    take(B - 2, 0)
                    take(B - 1, 1)

            @block.vector
            def _(dve):
                dve.wait_ge(w_turned, 1)
                dve.tensor_copy(wT[:, :, :, :].rearrange("p k j l -> p j k l")[:, 0:2, :, :],
                                ps_s[:, 0, :].rearrange("p (j k l) -> p j k l", j=2, k=KC)).then_inc(w_ready, 1)
                dve.tensor_copy(wT[:, :, 2, :], ps_s[:, 1, 0:2 * P].rearrange("p (k l) -> p k l", k=KC))
                dve.tensor_copy(wwT[:, :], ps_s[:, 1, 2 * P:4 * P]).then_inc(w_ready, 1)
                dve.wait_ge(mix_loaded, 16)

                def mask(b, p, first):
                    if not first:
                        dve.wait_ge(st_ready, b - 1)
                    for kb in range(TB):
                        dve.wait_ge(scored, b * TB + kb + 1)
                        dve.tensor_tensor(mixed[p][:, kb, :], ps_s[:, kb % 2, :], mix[:, kb, :],
                                          ALU.mult).then_inc(masked, 1)

                def add(b, p):
                    for c in range(KC):
                        dve.wait_ge(out_ready, b * KC + c + 1)
                        x_c = net.xT[:, c, ds(b * S, S)]
                        dve.tensor_tensor(x_c, ps_out[:, c, :], x_c, ALU.add).then_inc(out_added, 1)
                        dve.wait_ge(out_added, b * KC + c + 1)
                        dve.bn_stats(stats[:, c, ds(b, 1), :], x_c).then_inc(stats_step, 1)
                mask(0, 0, True)
                mask(1, 1, True)
                add(0, 0)
                with dve.Fori(1, B // 2) as i:
                    for p in range(2):
                        mask(i * 2 + p, p, False)
                        add(i * 2 + p - 1, 1 - p)
                add(B - 1, 1)
                s = Order(dve, norm_step)
                dve.wait_ge(affine_loaded, 64)
                dve.wait_ge(stats_step, B * KC)
                for c in range(KC):
                    s.did(dve.bn_aggr(mv[:, c, :], stats[:, c, :, :].rearrange("p b f -> p (b f)")))
                s.wait()
                s.did(dve.tensor_copy(mean, mv[:, :, 0]))
                s.did(dve.tensor_scalar(var, mv[:, :, 1], BN_EPS, None, ALU.add))
                inverse_root(net, s, dve, var, root, inv, tmp, sqrt_asked, sqrt_done, 1)
                s.wait()
                s.did(dve.tensor_tensor(scale, inv, affine[:, 0, :], ALU.mult))
                s.wait()
                s.did(dve.tensor_tensor(tmp, mean, scale, ALU.mult))
                s.wait()
                dve.tensor_tensor(shift, affine[:, 1, :], tmp, ALU.subtract).then_inc(norm_ready, 1)
                dve.wait_ge(norm_ready, 1)
                if not to_tokens:
                    dve.tensor_scalar(net.xT[:, 1, :], net.xT[:, 1, :], scale[:, 1:2], shift[:, 1:2],
                                      ALU.mult, ALU.add).then_inc(bn_done_v, 1)
                else:
                    def norm1(b, p, first):
                        if not first:
                            dve.wait_ge(bn_turned, b - 1)
                        dve.tensor_scalar(xb[p][:, 1, :], net.xT[:, 1, ds(b * S, S)], scale[:, 1:2], shift[:, 1:2],
                                          ALU.mult, ALU.add).then_inc(bn_done_v, 1)

                    def take(b, p):
                        dve.wait_ge(bn_turned, b + 1)
                        dve.tensor_copy(net.x[:, ds(b * TB + 2, 2), :], (ps_out, ps_s)[p][:, 1, :].rearrange(
                            "p (t c) -> p t c", c=C)).then_inc(bn_copied_v, 1)
                    norm1(0, 0, True)
                    norm1(1, 1, True)
                    with dve.Fori(1, B // 2) as i:
                        for p in range(2):
                            take(i * 2 + p - 2, p)
                            norm1(i * 2 + p, p, False)
                    take(B - 2, 0)
                    take(B - 1, 1)


def conv_layers(net):
    with ExitStack() as ctx:
        net.hold_channels("conv", ctx)
        load_tokens(net)
        conv_block(net, 0, False)
        conv_block(net, 1, True)


def layer_norm(net, tag, to_dram=None):
    nc = net.nc
    with ExitStack() as ctx:
        sb = lambda name, shape, dt=F32: net.sb(f"{tag}_{name}", shape, dt, ctx)
        sem = lambda name: net.sem(f"{tag}_{name}")
        stats = sb("stats", [P, NT, 6])
        mv = sb("mv", [P, NT, 2])
        var, root, rstd, tmp = (sb(n, [P, NT]) for n in ("var", "root", "rstd", "tmp"))
        normed = [sb(f"normed{p}", [P, TB, C]) for p in range(2)]
        turned = net.ps(f"{tag}_turned", [P, 2, KC, S], F32, ctx)
        stats_step, aggr_step, step = sem("stats_step"), sem("aggr_step"), sem("step")
        sqrt_asked, sqrt_done = sem("sqrt_asked"), sem("sqrt_done")
        normed_ready = sem("normed_ready")
        turned_ready = sem("turned_ready")
        copied = sem("copied")
        stored = [sem(f"stored{p}") for p in range(2)]
        with nc.Block() as block:
            @block.vector
            def _(dve):
                with dve.Fori(0, B) as b:
                    for t in range(TB):
                        dve.bn_stats(stats[:, ds(b * TB + t, 1), :], net.x[:, ds(b * TB + t, 1), :]
                                     ).then_inc(stats_step, 1)
                dve.wait_ge(stats_step, NT)
                for t in range(NT):
                    dve.bn_aggr(mv[:, t, :], stats[:, t, :]).then_inc(aggr_step, 1)
                dve.wait_ge(aggr_step, NT)
                s = Order(dve, step)
                s.did(dve.tensor_scalar(var[:, :], mv[:, :, 1], LN_EPS, None, ALU.add))
                inverse_root(net, s, dve, var[:, :], root[:, :], rstd[:, :], tmp[:, :], sqrt_asked, sqrt_done, 1)
                s.wait()

                def normalise(b, p, first):
                    if not first:
                        dve.wait_ge(turned_ready, b - 1)
                        if to_dram is not None:
                            dve.wait_ge(stored[p], (b - p) * 8)
                    for t in range(TB):
                        last = dve.tensor_scalar(normed[p][:, t, :], net.x[:, ds(b * TB + t, 1), :],
                                                 mv[:, ds(b * TB + t, 1), 0], rstd[:, ds(b * TB + t, 1)],
                                                 ALU.subtract, ALU.mult)
                    last.then_inc(normed_ready, 1)
                normalise(0, 0, True)
                normalise(1, 1, True)
                with dve.Fori(1, B // 2) as i:
                    for p in range(2):
                        normalise(i * 2 + p, p, False)

            @block.tensor
            def _(pe):
                def turn(b, p, first):
                    pe.wait_ge(normed_ready, b + 1)
                    if not first:
                        pe.wait_ge(copied, b - 1)
                    for c in range(KC):
                        for t in range(TB):
                            last = pe.transpose(turned[:, p, c, t * P:(t + 1) * P],
                                                normed[p][:, t, c * P:(c + 1) * P], net.ident[:, :])
                    last.then_inc(turned_ready, 1)
                turn(0, 0, True)
                turn(1, 1, True)
                with pe.Fori(1, B // 2) as i:
                    for p in range(2):
                        turn(i * 2 + p, p, False)

            @block.scalar
            def _(act):
                act.wait_ge(sqrt_asked, 1)
                act.activation(root[:, :], root[:, :], ACT.Sqrt).then_inc(sqrt_done, 1)
                with act.Fori(0, B // 2) as i:
                    for p in range(2):
                        act.wait_ge(turned_ready, i * 2 + p + 1)
                        act.activation(net.xT[:, :, ds((i * 2 + p) * S, S)], turned[:, p, :, :],
                                       ACT.Copy).then_inc(copied, 1)

            if to_dram is not None:
                rows = to_dram.rearrange("(u p) c -> p u c", p=P)

                @block.sync
                def _(sp):
                    with sp.Fori(0, B // 2) as i:
                        for p in range(2):
                            sp.wait_ge(normed_ready, i * 2 + p + 1)
                            net.go_on(sp)
                            sp.dma_start(rows[:, ds((i * 2 + p) * TB, TB), :], normed[p][:, :, :]
                                         ).then_inc(stored[p], 16)
                    for p in range(2):
                        sp.wait_ge(stored[p], 16 * B // 2)


def project_qkv(net, layer, scratch, values, gates):
    nc = net.nc
    rotary = layer == 3
    tag = f"L{layer}_qkv"
    regions = ((slice(0, P), slice(0, 2)), (slice(0, NKV * HD), slice(2, 3)))
    with ExitStack() as ctx:
        sb = lambda name, shape, dt=F32: net.sb(f"{tag}_{name}", shape, dt, ctx)
        sem = lambda name: net.sem(f"{tag}_{name}")
        w = sb("w", [P, KC, 3 * P + 32])
        w_plain = None if rotary else sb("w_plain", [P, KC, 3 * P])
        full = [sb(f"full{p}", [P, 3, S]) for p in range(2)]
        parts = [sb(f"parts{p}", [P, 3, 3, S], BF16) for p in range(2)]
        rest = sb("rest", [P, 3, S])
        proj = net.ps(f"{tag}_proj", [P, 3, S], F32, ctx)
        small = net.ps(f"{tag}_small", [P, TB, P], F32, ctx)
        w_loaded = sem("w_loaded")
        w_turned, w_ready = sem("w_turned"), sem("w_ready")
        projected = sem("projected")
        copied = sem("copied")
        turned_ready = sem("turned_ready")
        values_ready = sem("values_ready")
        hi_ready = sem("hi_ready")
        mid_ready = sem("mid_ready")
        rest_ready = sem("rest_ready")
        lo_ready = sem("lo_ready")
        written = [sem(f"written{p}") for p in range(2)]
        if rotary:
            w_in = sb("w_in", [P, 3, C])
            wg_in = sb("wg_in", [32, C])
            rope = sb("rope", [P, 4, S])
            swap = sb("swap", [P, 2, P])
            cosd = sb("cosd", [P, 3, S])
            sind = sb("sind", [P, 3, S])
            rot = [sb(f"rot{p}", [P, 3, S]) for p in range(2)]
            gate_row = [sb(f"gate_row{p}", [32, S]) for p in range(2)]
            gate_e = sb("gate_e", [P, TB, 32])
            gate_s = sb("gate_s", [P, TB, 32])
            swapped = net.ps(f"{tag}_swapped", [P, 3, S], F32, ctx)
            gate_ps = net.ps(f"{tag}_gate", [32, S], F32, ctx)
            swapped_ready = sem("swapped_ready")
            cos_ready = sem("cos_ready")
            sin_ready = sem("sin_ready")
            rot_ready = sem("rot_ready")
            gate_exp = sem("gate_exp")
            gate_step = sem("gate_step")
            gates_done = sem("gates_done")
        source = rot if rotary else full
        source_ready = rot_ready if rotary else copied

        with nc.Block() as block:
            @block.sync
            def _(sp):
                if not rotary:
                    sp.dma_start(w_plain[:, :, :], net.dram["L2_attn_W_qkv"].rearrange("(k p) n -> p k n", p=P)
                                 ).then_inc(w_loaded, 16)
                else:
                    sp.dma_start(w_in[:, 0:2, :], net.dram["L3_attn_Wq"].rearrange("(j p) c -> p j c", p=P)
                                 ).then_inc(w_loaded, 16)
                    sp.dma_start(w_in[0:64, 2, :], net.dram["L3_attn_Wk"]).then_inc(w_loaded, 16)
                    sp.dma_start(w_in[64:128, 2, :], net.dram["L3_attn_Wv"]).then_inc(w_loaded, 16)
                    sp.dma_start(wg_in[0:16, :], net.dram["L3_attn_Wg_slc"]).then_inc(w_loaded, 16)
                    sp.dma_start(wg_in[16:32, :], net.dram["L3_attn_Wg_swa"]).then_inc(w_loaded, 16)
                    sp.dma_start(rope[:, :, :], net.dram["c_rope"]).then_inc(w_loaded, 16)
                    sp.dma_start(swap[:, :, :], net.dram["c_swap"]).then_inc(w_loaded, 16)
                with sp.Fori(0, B // 2) as i:
                    for p in range(2):
                        b = i * 2 + p
                        sp.wait_ge(lo_ready, b + 1)
                        sp.wait_ge(mid_ready, b + 1)
                        net.go_on(sp)
                        for c in range(2):
                            for g in range(2):
                                sp.dma_start(scratch["q"][ds(b * NKV + 2 * c + g, 1), :, :].rearrange(
                                    "u (a r) t -> r (u a) t", a=3), parts[p][64 * g:64 * g + 64, c, :, :]
                                    ).then_inc(written[p], 16)
                        sp.dma_start(scratch["k"][:, ds(b * NKV * HD, NKV * HD), :].rearrange("a r t -> r a t"),
                                     parts[p][0:64, 2, :, :]).then_inc(written[p], 16)
                for p in range(2):
                    sp.wait_ge(written[p], 5 * 16 * B // 2)

            @block.tensor
            def _(pe):
                if rotary:
                    pe.wait_ge(w_loaded, 7 * 16)
                    for k in range(KC):
                        for j in range(3):
                            pe.transpose(swapped[:, k, j * P:(j + 1) * P], w_in[:, j, k * P:(k + 1) * P],
                                         net.ident[:, :])
                        last = pe.transpose(swapped[:, k, 3 * P:3 * P + 32], wg_in[:, k * P:(k + 1) * P],
                                            net.ident[0:32, 0:32])
                    last.then_inc(w_turned, 1)
                pe.wait_ge(w_ready, 1)

                def project(b, first):
                    if not first:
                        pe.wait_ge(copied, b)
                    for j in range(3):
                        for k in range(KC):
                            last = pe.matmul(proj[:, j, :], w[:, k, j * P:(j + 1) * P], net.xT[:, k, ds(b * S, S)],
                                             start=k == 0, stop=k == KC - 1)
                    if rotary:
                        for k in range(KC):
                            last = pe.matmul(gate_ps[:, :], w[:, k, 3 * P:3 * P + 32], net.xT[:, k, ds(b * S, S)],
                                             start=k == 0, stop=k == KC - 1)
                    last.then_inc(projected, 1)

                def turn(b, p, first):
                    pe.wait_ge(copied, b + 1)
                    if not first:
                        pe.wait_ge(values_ready, b)
                        if rotary:
                            pe.wait_ge(gate_exp, b)
                    for t in range(TB):
                        last = pe.transpose(small[:, t, :], full[p][:, 2, t * P:(t + 1) * P], net.ident[:, :])
                        if rotary:
                            last = pe.transpose(small[:, t, 0:32], gate_row[p][:, t * P:(t + 1) * P],
                                                net.ident[0:32, 0:32])
                    last.then_inc(turned_ready, 1)
                    if rotary:
                        if not first:
                            pe.wait_ge(sin_ready, b)
                        for j in range(3):
                            last = pe.matmul(swapped[:, j, :], swap[:, j // 2, :], full[p][:, j, :], start=True, stop=True)
                        last.then_inc(swapped_ready, 1)
                project(0, True)
                project(1, False)
                turn(0, 0, True)
                with pe.Fori(1, B // 2) as i:
                    for p in range(2):
                        project(i * 2 + p, False)
                        turn(i * 2 + p - 1, 1 - p, False)
                turn(B - 1, 1, False)

            @block.scalar
            def _(act):
                def copy(b, p, first):
                    act.wait_ge(projected, b + 1)
                    if not first:
                        act.wait_ge(turned_ready, b - 1)
                        if rotary:
                            act.wait_ge(swapped_ready, b - 1)
                            act.wait_ge(cos_ready, b - 1)
                        else:
                            act.wait_ge(rest_ready, b - 1)
                    if rotary:
                        act.activation(gate_row[p][:, :], gate_ps[:, :], ACT.Copy)
                    act.activation(full[p][:, :, :], proj[:, :, :], ACT.Copy).then_inc(copied, 1)

                def split(b, p, first, early):
                    act.wait_ge(source_ready, b + 1)
                    if not early:
                        act.wait_ge(written[p], (b - p) * 40)
                    for rows, chunks in regions:
                        last = act.activation(parts[p][rows, chunks, 0, :], source[p][rows, chunks, :], ACT.Copy)
                    last.then_inc(hi_ready, 1)
                    act.wait_ge(rest_ready, b + 1)
                    for rows, chunks in regions:
                        last = act.activation(parts[p][rows, chunks, 1, :], rest[rows, chunks, :], ACT.Copy)
                    last.then_inc(mid_ready, 1)
                    if rotary:
                        act.wait_ge(values_ready, b + 1)
                        if not first:
                            act.wait_ge(gates_done, b)
                        act.activation(gate_e[:, :, :], small[:, :, 0:32], ACT.Exp, scale=-1.0).then_inc(gate_exp, 1)
                copy(0, 0, True)
                copy(1, 1, True)
                split(0, 0, True, True)
                copy(2, 0, False)
                split(1, 1, False, True)
                copy(3, 1, False)
                with act.Fori(1, B // 2 - 1) as i:
                    for p in range(2):
                        split(i * 2 + p, p, False, False)
                        copy(i * 2 + p + 2, p, False)
                split(B - 2, 0, False, False)
                split(B - 1, 1, False, False)

            @block.vector
            def _(dve):
                if rotary:
                    dve.wait_ge(w_turned, 1)
                    plain, end = swapped, 3 * P + 32
                else:
                    dve.wait_ge(w_loaded, 16)
                    plain, end = w_plain, 3 * P
                for k in range(KC):
                    dve.tensor_copy(w[:, k, 0:2 * P].rearrange("p (g d h) -> p g d h", g=NKV, h=GR),
                                    plain[:, k, 0:2 * P].rearrange("p (g h d) -> p g d h", g=NKV, h=GR))
                dve.tensor_copy(w[:, :, 2 * P:end], plain[:, 0:KC, 2 * P:end]).then_inc(w_ready, 1)

                def per_element(b, p, first):
                    if rotary:
                        dve.wait_ge(swapped_ready, b + 1)
                        if not first:
                            dve.wait_ge(rot_ready, b)
                        sin_q = rope[:, 1:2, :].to_broadcast([P, 2, S])
                        dve.tensor_tensor(sind[:, 0:2, :], swapped[:, 0:2, :], sin_q, ALU.mult)
                        dve.tensor_tensor(sind[0:64, 2, :], swapped[0:64, 2, :], rope[0:64, 3, :],
                                          ALU.mult).then_inc(sin_ready, 1)
                    dve.wait_ge(hi_ready, b + 1)
                    if not first:
                        dve.wait_ge(lo_ready, b)
                        dve.wait_ge(mid_ready, b)
                    for rows, chunks in regions:
                        last = dve.tensor_tensor(rest[rows, chunks, :], source[p][rows, chunks, :],
                                                 parts[p][rows, chunks, 0, :], ALU.subtract)
                    last.then_inc(rest_ready, 1)
                    dve.wait_ge(turned_ready, b + 1)
                    dve.tensor_copy(values[:, ds(b * NKV, NKV), :, :],
                                    small[:, :, 64:128].rearrange("p t (g d) -> p g t d", g=NKV)
                                    ).then_inc(values_ready, 1)
                    dve.wait_ge(mid_ready, b + 1)
                    for rows, chunks in regions:
                        last = dve.tensor_tensor(parts[p][rows, chunks, 2, :], rest[rows, chunks, :],
                                                 parts[p][rows, chunks, 1, :], ALU.subtract)
                    last.then_inc(lo_ready, 1)
                    if rotary:
                        dve.wait_ge(gate_exp, b + 1)
                        s = Order(dve, gate_step, b * 2)
                        s.did(dve.tensor_scalar(gate_s[:, :, :], gate_e[:, :, :], 1.0, None, ALU.add))
                        s.wait()
                        s.did(dve.reciprocal(gate_s[:, :, :], gate_s[:, :, :]))
                        s.wait()
                        dve.tensor_tensor(gates[:, ds(b * NKV, NKV), :, :],
                                          gate_s[:, :, 0:16].rearrange("p t (g h) -> p g t h", g=NKV),
                                          gate_s[:, :, 16:32].rearrange("p t (g h) -> p g t h", g=NKV),
                                          ALU.add).then_inc(gates_done, 1)
                per_element(0, 0, True)
                per_element(1, 1, False)
                with dve.Fori(1, B // 2) as i:
                    for p in range(2):
                        per_element(i * 2 + p, p, False)

            if rotary:
                @block.gpsimd
                def _(pool):
                    def turn_positions(b, p, first, early):
                        pool.wait_ge(copied, b + 1)
                        if not first:
                            pool.wait_ge(rot_ready, b)
                        pool.tensor_tensor(cosd[:, 0:2, :], full[p][:, 0:2, :],
                                           rope[:, 0:1, :].to_broadcast([P, 2, S]), ALU.mult)
                        pool.tensor_tensor(cosd[0:64, 2, :], full[p][0:64, 2, :], rope[0:64, 2, :],
                                           ALU.mult).then_inc(cos_ready, 1)
                        pool.wait_ge(cos_ready, b + 1)
                        pool.wait_ge(sin_ready, b + 1)
                        if not early:
                            pool.wait_ge(rest_ready, b - 1)
                        pool.tensor_tensor(rot[p][:, 0:2, :], cosd[:, 0:2, :], sind[:, 0:2, :], ALU.add)
                        pool.tensor_tensor(rot[p][0:64, 2, :], cosd[0:64, 2, :], sind[0:64, 2, :],
                                           ALU.add).then_inc(rot_ready, 1)
                    pool.wait_ge(w_loaded, 7 * 16)
                    turn_positions(0, 0, True, True)
                    turn_positions(1, 1, False, True)
                    with pool.Fori(1, B // 2) as i:
                        for p in range(2):
                            turn_positions(i * 2 + p, p, False, False)


def attention(net, layer, scratch, values, gates, out):
    nc = net.nc
    tag = f"L{layer}_attn"
    U = B * NKV
    scale = float(HD) ** -0.5
    order = [("A", 0), ("B", 0), ("A", 1), ("B", 1), ("C", 0), ("A", 2), ("B", 2), ("A", 3), ("B", 3), ("C", 2)]
    place = {("A", r): r for r in range(GR)} | {("B", r): GR + r for r in range(GR)} | {("C", 0): 8, ("C", 2): 9}
    UN = len(order)
    with ExitStack() as ctx:
        sb = lambda name, shape, dt=F32: net.sb(f"{tag}_{name}", shape, dt, ctx)
        sem = lambda name: net.sem(f"{tag}_{name}")
        q = [sb(f"q{j}", [P, GR, S], BF16) for j in range(4)]
        k = [sb(f"k{j}", [P, S], BF16) for j in range(4)]
        v = [sb(f"v{j}", [P, TB, 32]) for j in range(4)]
        probs = [sb(f"probs{j}", [P, UN, S]) for j in range(2)]
        ident16 = sb("ident16", [P, P], BF16)
        causal = sb("causal", [P, P])
        causal16 = sb("causal16", [P, P], BF16)
        top = [sb(f"top{j}", [P, GR, TB]) for j in range(2)]
        top_rows = [sb(f"top_rows{j}", [GR * TB, 2, P], BF16) for j in range(2)]
        oT = [sb(f"oT{j}", [P, S]) for j in range(2)]
        inv = sb("inv", [P, TB, GR])
        ps_m = net.ps(f"{tag}_ps_m", [P, 2, S], F32, ctx)
        ps_t = net.ps(f"{tag}_ps_t", [P, 2, S], F32, ctx)
        ps_v = net.ps(f"{tag}_ps_v", [P, 2, S], F32, ctx)
        ps_o = net.ps(f"{tag}_ps_o", [P, TB, P], F32, ctx)
        ps_top = net.ps(f"{tag}_ps_top", [P, S], F32, ctx)
        const_in = sem("const_in")
        const_ready = sem("const_ready")
        v_const = sem("v_const")
        loaded = [sem(f"loaded{j}") for j in range(4)]
        tops_in = [sem(f"tops_in{j}") for j in range(4)]
        m_scored = sem("m_scored")
        m_reduced = sem("m_reduced")
        top_turned = sem("top_turned")
        top_hi = sem("top_hi")
        top_ready = sem("top_ready")
        t_scored = sem("t_scored")
        exped = sem("exped")
        v_ready = sem("v_ready")
        probs_ready = sem("probs_ready")
        pv_done = sem("pv_done")
        oT_ready = sem("oT_ready")
        o_turned = sem("o_turned")
        inv_step = sem("inv_step")
        o_done = sem("o_done")

        with nc.Block() as block:
            @block.sync
            def _(sp):
                sp.dma_start(causal[:, :], net.dram["c_causal"]).then_inc(const_in, 16)

                def load(u, j):
                    for at, n in ((0, 3), (3, 2), (5, 1)):
                        sp.dma_start(q[j][at * HD:(at + n) * HD, :, :],
                                     scratch["q"][ds(u, 1), 0:n * HD * GR, :].rearrange("u (p h) t -> (u p) h t", h=GR)
                                     ).then_inc(loaded[j], 16)
                    for part, at, n in ((0, 0, 3), (1, 3, 2), (2, 5, 1)):
                        sp.dma_start(k[j][at * HD:(at + n) * HD, :],
                                     scratch["k"][part:part + 1, ds(u * HD, HD), :].broadcast_to([n, HD, S])
                                     ).then_inc(loaded[j], 16)

                def put_tops(u, j, first):
                    sp.wait_ge(top_ready, u + 1)
                    net.go_on(sp)
                    if not first:
                        sp.wait_ge(t_scored, (u - 3) * UN)
                    for a in range(2):
                        sp.dma_start(q[j][6 * HD + a:6 * HD + a + 1, :, :], top_rows[j % 2][:, a, :]
                                     ).then_inc(tops_in[j], 16)

                def unit(u, j, more=True):
                    if more:
                        sp.wait_ge(t_scored, u * UN)
                        net.go_on(sp)
                        load(u + 3, (j + 3) % 4)
                    put_tops(u + 1, (j + 1) % 4, False)
                for j in range(4):
                    load(j, j)
                put_tops(0, 0, True)
                put_tops(1, 1, True)
                for u in (1, 2):
                    sp.wait_ge(t_scored, u * UN)
                    load(u + 3, (u + 3) % 4)
                    put_tops(u + 1, u + 1, True)
                sp.wait_ge(t_scored, 3 * UN)
                load(6, 2)
                put_tops(4, 0, False)
                sp.wait_ge(t_scored, 4 * UN)
                load(7, 3)
                put_tops(5, 1, False)
                with sp.Fori(1, U // 4 - 1) as i:
                    for j in range(1, 5):
                        unit(i * 4 + j, j % 4)
                unit(U - 3, 1, False)
                unit(U - 2, 2, False)

            @block.gpsimd
            def _(pool):
                pool.wait_ge(v_const, 12)

                def keep_causal(block, columns):
                    return pool.affine_select(out=block, in_=block, compare_op=ALU.is_ge, fill=0.0, base=0,
                                              pattern=columns, channel_multiplier=-1)

                def unit(u, j, first):
                    if not first:
                        pool.wait_ge(pv_done, u - 3)
                    pool.tensor_copy(v[j][:, :, 0:HD], values[:, ds(u, 1), :, :]).then_inc(v_ready, 1)
                    pool.wait_ge(exped, u * UN + UN)
                    net.go_on(pool)
                    pr = probs[j % 2]
                    keep_causal(pr[:, 0:GR, 0:P], [[0, GR], [1, P]])
                    keep_causal(pr[:, GR:2 * GR, 0:P], [[0, GR], [1, P]])
                    keep_causal(pr[:, GR:2 * GR, 3 * P:4 * P], [[0, GR], [1, P]])
                    keep_causal(pr[:, 8:10, :].rearrange("p c (r q) -> p (c r) q", r=2)[:, :, 0:P],
                                [[0, GR], [1, P]]).then_inc(probs_ready, 1)
                for u in range(4):
                    unit(u, u, True)
                with pool.Fori(1, U // 4) as i:
                    for j in range(4):
                        unit(i * 4 + j, j, False)

            @block.tensor
            def _(pe):
                pe.wait_ge(const_ready, 2)
                pe.wait_ge(v_const, 12)

                def max_unit(u, j, n, first):
                    kind, r = order[n]
                    if n == 0:
                        pe.wait_ge(loaded[j], (u - j) * 24 + 96)
                    if not (first and n < 2):
                        pe.wait_ge(m_reduced, u * UN + n - 1)
                    bank = ps_m[:, n % 2, :]
                    pieces = {"A": [(r, 3, 0)], "B": [(r, 2, 0), (r, 0, 3 * P)], "C": [(r, 1, 0), (r + 1, 1, 2 * P)]}
                    for head, qb, at in pieces[kind]:
                        width = (qb + 1) * P
                        pe.matmul(bank[:, at:at + width], q[j][0:96, head, qb * P:(qb + 1) * P], k[j][0:96, 0:width],
                                  start=True, stop=False)
                        last = pe.matmul(bank[:, at + width - P:at + width], ident16[:, :], causal16[:, :],
                                         start=False, stop=True)
                    last.then_inc(m_scored, 1)

                def exp_unit(u, j, n, first):
                    kind, r = order[n]
                    if n == 0:
                        pe.wait_ge(tops_in[j], (u - j) * 8 + 32)
                    if not (first and n < 2):
                        pe.wait_ge(exped, u * UN + n - 1)
                    bank = ps_t[:, n % 2, :]
                    pieces = {"A": [(r, 0, 0)], "B": [(r, 1, 0), (r, 3, 3 * P)], "C": [(r, 2, 0), (r + 1, 2, 2 * P)]}
                    for head, kb, at in pieces[kind]:
                        width = (TB - kb) * P
                        last = pe.matmul(bank[:, at:at + width], k[j][0:98, kb * P:(kb + 1) * P],
                                         q[j][0:98, head, kb * P:S], start=True, stop=True)
                    last.then_inc(t_scored, 1)

                def turn_tops(u, j):
                    pe.wait_ge(m_reduced, u * UN + UN)
                    pe.transpose(ps_top[0:GR * TB, 0:P], top[j % 2][:, :, :].rearrange("p h t -> p (h t)"),
                                 net.ident[:, :]).then_inc(top_turned, 1)

                def weigh_values(u, j, first):
                    pe.wait_ge(probs_ready, u + 1)
                    pe.wait_ge(v_ready, u + 1)
                    if not first:
                        pe.wait_ge(oT_ready, u - 1)
                    pr = probs[j % 2]
                    for kb in range(TB):
                        for r in range(GR):
                            src = {0: pr[:, r, :], 1: pr[:, GR + r, 0:3 * P],
                                   2: pr[:, 8 + r // 2, (r % 2) * 2 * P:(r % 2 + 1) * 2 * P],
                                   3: pr[:, GR + r, 3 * P:4 * P]}[kb]
                            last = pe.matmul(ps_v[32 * r:32 * r + 32, j % 2, kb * P:S], v[j][:, kb, :], src,
                                             start=kb == 0, stop=kb == TB - 1, tile_position=(0, 32 * r))
                    last.then_inc(pv_done, 1)

                def turn_out(u, j, first):
                    pe.wait_ge(oT_ready, u + 1)
                    if not first:
                        pe.wait_ge(o_done, u)
                    for t in range(TB):
                        last = pe.transpose(ps_o[:, t, :], oT[j % 2][:, t * P:(t + 1) * P], net.ident[:, :])
                    last.then_inc(o_turned, 1)

                def unit(u, j, maxima=True, weigh=True, turn=True, first=False, first_turn=False, first_weigh=False):
                    for n in range(UN):
                        if maxima:
                            max_unit(u + 1, (j + 1) % 4, n, False)
                        exp_unit(u, j, n, first)
                        if n == 4 and turn:
                            turn_out(u - 2, (j + 2) % 4, first_turn)
                    if maxima:
                        turn_tops(u + 1, (j + 1) % 4)
                    if weigh:
                        weigh_values(u - 1, (j + 3) % 4, first_weigh)
                for n in range(UN):
                    max_unit(0, 0, n, True)
                turn_tops(0, 0)
                unit(0, 0, weigh=False, turn=False, first=True)
                unit(1, 1, turn=False, first_weigh=True)
                unit(2, 2, first_turn=True, first_weigh=True)
                unit(3, 3)
                unit(4, 0)
                with pe.Fori(1, U // 4 - 1) as i:
                    for j in range(1, 5):
                        unit(i * 4 + j, j % 4)
                unit(U - 3, 1)
                unit(U - 2, 2)
                unit(U - 1, 3, maxima=False)
                turn_out(U - 2, 2, False)
                weigh_values(U - 1, 3, False)
                turn_out(U - 1, 3, False)

            @block.scalar
            def _(act):
                def exponentials(u, j, first, mid=None):
                    if not first:
                        act.wait_ge(pv_done, u - 1)
                    for n, unit in enumerate(order):
                        act.wait_ge(t_scored, u * UN + n + 1)
                        act.activation(probs[j % 2][:, place[unit], :], ps_t[:, n % 2, :], ACT.Exp,
                                       scale=scale).then_inc(exped, 1)

                def copy_out(u, j, first):
                    act.wait_ge(pv_done, u + 1)
                    if not first:
                        act.wait_ge(o_turned, u - 1)
                    act.activation(oT[j % 2][:, :], ps_v[:, j % 2, :], ACT.Copy).then_inc(oT_ready, 1)
                exponentials(0, 0, True)
                exponentials(1, 1, True)
                copy_out(0, 0, True)
                exponentials(2, 2, False)
                copy_out(1, 1, True)
                exponentials(3, 3, False)
                copy_out(2, 2, False)
                with act.Fori(1, U // 4) as i:
                    for j in range(4):
                        exponentials(i * 4 + j, j, False)
                        copy_out(i * 4 + j - 1, (j + 3) % 4, False)
                copy_out(U - 1, 3, False)

            @block.vector
            def _(dve):
                for j in range(4):
                    dve.memset(k[j][96:98, :], -1.0).then_inc(v_const, 1)
                    dve.memset(v[j][:, :, :], 0.0).then_inc(v_const, 1)
                dve.wait_ge(v_const, 8)
                for j in range(4):
                    dve.memset(v[j][:, :, HD:HD + 1], 1.0).then_inc(v_const, 1)
                dve.tensor_copy(ident16[:, :], net.ident[:, :]).then_inc(const_ready, 1)
                dve.wait_ge(const_in, 16)
                dve.tensor_copy(causal16[:, :], causal[:, :]).then_inc(const_ready, 1)

                def reduce(u, j, n, first):
                    kind, r = order[n]
                    if n == 0 and not first:
                        dve.wait_ge(top_turned, u - 1)
                    dve.wait_ge(m_scored, u * UN + n + 1)
                    bank, t = ps_m[:, n % 2, :], top[j % 2]
                    if kind == "A":
                        last = dve.tensor_reduce(t[:, r, 3:4], bank, AX.X, ALU.max)
                    elif kind == "B":
                        dve.tensor_reduce(t[:, r, 2:3], bank[:, 0:3 * P], AX.X, ALU.max)
                        last = dve.tensor_reduce(t[:, r, 0:1], bank[:, 3 * P:4 * P], AX.X, ALU.max)
                    else:
                        last = dve.tensor_reduce(t[:, r:r + 2, 1], bank.rearrange("p (h k) -> p h k", h=2),
                                                 AX.X, ALU.max)
                    last.then_inc(m_reduced, 1)

                def split_tops(u, j, first):
                    dve.wait_ge(top_turned, u + 1)
                    if not first:
                        dve.wait_ge(tops_in[(j + 2) % 4], (u - 2 - (j + 2) % 4) * 8 + 32)
                    rows, src = top_rows[j % 2], ps_top[0:GR * TB, 0:P]
                    dve.tensor_copy(rows[:, 0, :], src).then_inc(top_hi, 1)
                    dve.wait_ge(top_hi, u + 1)
                    dve.tensor_tensor(rows[:, 1, :], src, rows[:, 0, :], ALU.subtract).then_inc(top_ready, 1)

                def normalise(u, first):
                    dve.wait_ge(o_turned, u + 1)
                    heads = ps_o[:, :, :].rearrange("p t (h c) -> p t h c", h=GR)
                    n = 2 if layer == 3 else 1
                    if not first:
                        dve.wait_ge(o_done, u)
                    dve.reciprocal(inv[:, :, :], heads[:, :, :, HD]).then_inc(inv_step, 1)
                    dve.wait_ge(inv_step, u * n + 1)
                    if layer == 3:
                        dve.tensor_tensor(inv[:, :, :], inv[:, :, :], gates[:, ds(u, 1), :, :].rearrange(
                            "p u t h -> p (u t) h"), ALU.mult).then_inc(inv_step, 1)
                        dve.wait_ge(inv_step, u * n + 2)
                    dve.tensor_tensor(out[:, ds(u, 1), :, :].rearrange("p u t (h d) -> p (u t) h d", h=GR),
                                      heads[:, :, :, 0:HD],
                                      inv[:, :, :].unsqueeze(3).to_broadcast([P, TB, GR, HD]),
                                      ALU.mult).then_inc(o_done, 1)

                def unit(u, j, maxima=True, turn=True, first=False, first_norm=False):
                    for n in range(UN):
                        if maxima:
                            reduce(u + 1, (j + 1) % 4, n, first)
                        if n == 5 and turn:
                            normalise(u - 2, first_norm)
                    if maxima:
                        split_tops(u + 1, (j + 1) % 4, first)
                for n in range(UN):
                    reduce(0, 0, n, True)
                split_tops(0, 0, True)
                unit(0, 0, turn=False, first=True)
                unit(1, 1, turn=False)
                unit(2, 2, first_norm=True)
                unit(3, 3)
                unit(4, 0)
                with dve.Fori(1, U // 4 - 1) as i:
                    for j in range(1, 5):
                        unit(i * 4 + j, j % 4)
                unit(U - 3, 1)
                unit(U - 2, 2)
                unit(U - 1, 3, maxima=False)
                normalise(U - 2, False)
                normalise(U - 1, False)


def project_out(net, layer, heads):
    nc = net.nc
    tag = f"L{layer}_wo"
    with ExitStack() as ctx:
        sb = lambda name, shape, dt=F32: net.sb(f"{tag}_{name}", shape, dt, ctx)
        sem = lambda name: net.sem(f"{tag}_{name}")
        w_in = sb("w_in", [P, KC, C])
        w = sb("w", [P, KC, C]) if layer == 3 else w_in
        rows = [sb(f"rows{p}", [P, TB, C]) for p in range(2)]
        rowsT = [sb(f"rowsT{p}", [P, KC, S]) for p in range(2)]
        turned = net.ps(f"{tag}_turned", [P, KC, S], F32, ctx)
        w_ps = net.ps(f"{tag}_w_ps", [P, KC, C], F32, ctx)
        proj = [net.ps(f"{tag}_proj{p}", [P, TB, C], F32, ctx) for p in range(2)]
        w_loaded, w_turned, w_ready = sem("w_loaded"), sem("w_turned"), sem("w_ready")
        rows_ready = sem("rows_ready")
        turned_ready = sem("turned_ready")
        copied = sem("copied")
        projected = sem("projected")
        added = sem("added")
        with nc.Block() as block:
            @block.sync
            def _(sp):
                src = net.dram["L2_attn_W_o" if layer == 2 else "L3_attn_Wo"]
                sp.dma_start(w_in[:, :, :], src.rearrange("(k p) c -> p k c", p=P)).then_inc(w_loaded, 16)

            @block.tensor
            def _(pe):
                pe.wait_ge(w_loaded, 16)
                if layer == 3:
                    for k in range(KC):
                        for j in range(KC):
                            last = pe.transpose(w_ps[:, k, j * P:(j + 1) * P], w_in[:, j, k * P:(k + 1) * P],
                                                net.ident[:, :])
                    last.then_inc(w_turned, 1)
                    pe.wait_ge(w_ready, 1)

                def turn(b, p, first):
                    pe.wait_ge(rows_ready, b + 1)
                    if not first:
                        pe.wait_ge(copied, b)
                    for c in range(KC):
                        for t in range(TB):
                            last = pe.transpose(turned[:, c, t * P:(t + 1) * P], rows[p][:, t, c * P:(c + 1) * P],
                                                net.ident[:, :])
                    last.then_inc(turned_ready, 1)

                def project(b, p, first):
                    pe.wait_ge(copied, b + 1)
                    if not first:
                        pe.wait_ge(added, b - 1)
                    for t in range(TB):
                        for k in range(KC):
                            last = pe.matmul(proj[p][:, t, :], rowsT[p][:, k, t * P:(t + 1) * P], w[:, k, :],
                                             start=k == 0, stop=k == KC - 1)
                    last.then_inc(projected, 1)
                turn(0, 0, True)
                turn(1, 1, False)
                project(0, 0, True)
                turn(2, 0, False)
                project(1, 1, True)
                with pe.Fori(1, B // 2 - 1) as i:
                    for p in range(2):
                        turn(i * 2 + p + 1, 1 - p, False)
                        project(i * 2 + p, p, False)
                turn(B - 1, 1, False)
                project(B - 2, 0, False)
                project(B - 1, 1, False)

            @block.scalar
            def _(act):
                def gather(b, p, first):
                    if not first:
                        act.wait_ge(turned_ready, b - 1)
                    act.activation(rows[p][:, :, :].rearrange("p t (g c) -> p g t c", g=NKV),
                                   heads[:, ds(b * NKV, NKV), :, :], ACT.Copy).then_inc(rows_ready, 1)

                def copy(b, p, first):
                    act.wait_ge(turned_ready, b + 1)
                    if not first:
                        act.wait_ge(projected, b - 1)
                    act.activation(rowsT[p][:, :, :], turned[:, :, :], ACT.Copy).then_inc(copied, 1)
                gather(0, 0, True)
                gather(1, 1, True)
                copy(0, 0, True)
                copy(1, 1, True)
                with act.Fori(1, B // 2) as i:
                    for p in range(2):
                        gather(i * 2 + p, p, False)
                        copy(i * 2 + p, p, False)

            @block.vector
            def _(dve):
                if layer == 3:
                    dve.wait_ge(w_turned, 1)
                    dve.tensor_copy(w[:, :, :], w_ps[:, :, :]).then_inc(w_ready, 1)
                with dve.Fori(0, B // 2) as i:
                    for p in range(2):
                        b = i * 2 + p
                        dve.wait_ge(projected, b + 1)
                        x_b = net.x[:, ds(b * TB, TB), :]
                        dve.tensor_tensor(x_b, proj[p][:, :, :], x_b, ALU.add).then_inc(added, 1)


def attention_block(net, layer):
    with ExitStack() as ctx:
        values = net.sb(f"L{layer}_values", [P, B * NKV, TB, HD], F32, ctx)
        heads = net.sb(f"L{layer}_heads", [P, B * NKV, TB, GR * HD], F32, ctx)
        gates = net.sb(f"L{layer}_gates", [P, B * NKV, TB, GR], F32, ctx) if layer == 3 else None
        scratch = {"q": net.nc.dram_tensor(f"L{layer}_q_parts", (B * NKV, 3 * GR * HD, S), BF16).ap(),
                   "k": net.nc.dram_tensor(f"L{layer}_k_parts", (3, B * NKV * HD, S), BF16).ap()}
        with ExitStack() as early:
            net.hold_channels(f"L{layer}_attn", early)
            layer_norm(net, f"L{layer}_ln")
            project_qkv(net, layer, scratch, values, gates)
        attention(net, layer, scratch, values, gates, heads)
        project_out(net, layer, heads)


class Tables:

    def __init__(self, net, tag, ctx):
        self.take = net.sb(f"{tag}_take", [P, SLOT_TILES], I32, ctx)
        self.give = net.sb(f"{tag}_give", [P, SLOT_TILES], I32, ctx)
        self.weight = net.sb(f"{tag}_weight", [P, SLOT_TILES], F32, ctx)
        self.expert = net.sb(f"{tag}_expert", [P, SLOT_TILES], I32, ctx)


def route(net, layer, xT, tables):
    nc = net.nc
    tag = f"L{layer}_route"
    with ExitStack() as ctx:
        sb = lambda name, shape, dt=F32: net.sb(f"{tag}_{name}", shape, dt, ctx)
        sem = lambda name: net.sem(f"{tag}_{name}")
        by_tile = [P, NT, E]
        by_expert = [P, E, NT]
        w_in = sb("w_in", [E, C])
        w = sb("w", [P, KC, E])
        bias_col = sb("bias_col", [E, 1])
        bias_row = sb("bias_row", [P, E])
        z_row = [sb(f"z_row{p}", [E, S]) for p in range(2)]
        z, sig, key, score, first, second, chosen, tmp, weights = (
            sb(n, by_tile) for n in ("z", "sig", "key", "score", "first", "second", "chosen", "tmp", "weights"))
        best, where_, total, slot, wslot, token1 = (
            sb("best", [P, NT]), sb("where", [P, NT]), sb("total", [P, NT]),
            sb("slot", [P, 2, NT]), sb("wslot", [P, 2, NT]), sb("token1", [P, NT]))
        slot_i, high_i, low_i = (sb(n, [P, 2, NT], I32) for n in ("slot_i", "high_i", "low_i"))
        high, low = sb("high", [P, 2, NT]), sb("low", [P, 2, NT])
        chosen16 = sb("chosen16", by_tile, BF16)
        before, before16 = sb("before", [P, P]), sb("before16", [P, P], BF16)
        ones16, ones = sb("ones16", [P, P], BF16), sb("ones", [P, NT])
        lane, expert_no, tile_start = sb("lane", [P, P]), sb("expert_no", [P, E]), sb("tile_start", [P, SLOT_TILES])
        less8 = sb("less8", [P, E])
        per_tile, upto, ranks = sb("per_tile", by_expert), sb("upto", by_expert), sb("ranks", by_expert)
        small = sb("small", [P, 8, E])
        padded_i = sb("padded_i", [P, E], I32)
        tile_cmp, tile_exp = sb("tile_cmp", [P, SLOT_TILES, E]), sb("tile_exp", [P, SLOT_TILES])
        left = [[sb(f"left{p}{c}", [P, P]) for c in range(2)] for p in range(2)]
        right = [[sb(f"right{p}{c}", [P, 2, P]) for c in range(2)] for p in range(2)]
        table_rows = sb("table_rows", [P, 2, P])
        table = sb("table", [P, 2, SLOT_TILES])
        empty = sb("empty", [P, SLOT_TILES])
        lane_col = sb("lane_col", [P, 1])
        if layer == 2:
            bits = sb("bits", [P, 30, E], I32)
            floor_, candidate, gain = (sb(n, [P, E], I32) for n in ("floor", "candidate", "gain"))
            rated, over = sb("rated", by_expert), sb("over", by_expert)
            level, level16 = sb("level", by_expert), sb("level16", by_expert, BF16)
            count16 = sb("count16", [P, E], BF16)
        ps_z = net.ps(f"{tag}_ps_z", [P, 2, S], F32, ctx)
        ps_t = net.ps(f"{tag}_ps_t", [P, 2, S], F32, ctx)
        ps_c = net.ps(f"{tag}_ps_c", [P, 2, S], F32, ctx)
        ps_k = net.ps(f"{tag}_ps_k", [P, S], F32, ctx)
        ps_tab = net.ps(f"{tag}_ps_tab", [P, S], F32, ctx)
        loaded = sem("loaded")
        w_turned, w_ready = sem("w_turned"), sem("w_ready")
        z_ready = sem("z_ready")
        z_copied = sem("z_copied")
        z_turned = sem("z_turned")
        z_in = sem("z_in")
        const_ready = sem("const_ready")
        exp_done = sem("exp_done")
        step = sem("step")
        loop_step = sem("loop_step")
        counts_asked, counted = sem("counts_asked"), sem("counted")
        level_asked, level_counted = sem("level_asked"), sem("level_counted")
        sides_ready = sem("sides_ready")
        sides_used = sem("sides_used")
        table_ready, table_copied, table_turned = sem("table_ready"), sem("table_copied"), sem("table_turned")
        dram = net.dram
        w_name = "L2_ffn_proj_w" if layer == 2 else "L3_ffn_gate_w"
        b_name = "L2_ffn_proj_b" if layer == 2 else "L3_ffn_gate_b"
        e_name = "L2_ffn_expert_bias" if layer == 2 else "L3_ffn_expert_biases"
        n_loaded = 7 + (1 if layer == 2 else 0)

        with nc.Block() as block:
            @block.sync
            def _(sp):
                if layer == 2:
                    sp.dma_start(w_in[:, :], dram[w_name]).then_inc(loaded, 16)
                    sp.dma_start(bits[:, :, :], dram["c_bits"]).then_inc(loaded, 16)
                else:
                    sp.dma_start(w[:, :, :], dram[w_name].rearrange("(k p) e -> p k e", p=P)).then_inc(loaded, 16)
                sp.dma_start(bias_col[:, :], dram[b_name].rearrange("(e a) -> e a", a=1)).then_inc(loaded, 16)
                sp.dma_start(bias_row[:, :], dram[e_name].partition_broadcast(P)).then_inc(loaded, 16)
                sp.dma_start(before[:, :], dram["c_before"]).then_inc(loaded, 16)
                sp.dma_start(expert_no[:, :], dram["c_expert"]).then_inc(loaded, 16)
                sp.dma_start(tile_start[:, :], dram["c_tilestart"]).then_inc(loaded, 16)
                sp.dma_start(lane[:, :], dram["c_lane"]).then_inc(loaded, 16)

            @block.tensor
            def _(pe):
                pe.wait_ge(loaded, 16 * n_loaded)
                if layer == 2:
                    for k in range(KC):
                        last = pe.transpose(ps_k[:, k * E:(k + 1) * E], w_in[:, k * P:(k + 1) * P],
                                            net.ident[0:E, 0:E])
                    last.then_inc(w_turned, 1)
                    pe.wait_ge(w_ready, 1)

                def logits(b, p, first):
                    if not first:
                        pe.wait_ge(z_copied, b - 1)
                        net.go_on(pe)
                    for k in range(KC):
                        last = pe.matmul(ps_z[0:E, p, :], w[:, k, :], xT[:, k, ds(b * S, S)],
                                         start=k == 0, stop=k == KC - 1)
                    last.then_inc(z_ready, 1)

                def turn(b, p, first):
                    pe.wait_ge(z_copied, b + 1)
                    if not first:
                        pe.wait_ge(z_in, b - 1)
                    net.go_on(pe)
                    for t in range(TB):
                        last = pe.transpose(ps_t[:, p, t * E:(t + 1) * E], z_row[p][:, t * P:(t + 1) * P],
                                            net.ident[0:E, 0:E])
                    last.then_inc(z_turned, 1)
                logits(0, 0, True)
                logits(1, 1, True)
                turn(0, 0, True)
                logits(2, 0, False)
                turn(1, 1, True)
                with pe.Fori(1, B // 2 - 1) as i:
                    for p in range(2):
                        logits(i * 2 + p + 1, 1 - p, False)
                        turn(i * 2 + p, p, False)
                logits(B - 1, 1, False)
                turn(B - 2, 0, False)
                turn(B - 1, 1, False)

                pe.wait_ge(counts_asked, 1)
                pairs = chosen16[:, :, :].rearrange("p t e -> p (t e)")
                pe.matmul(ps_c[:, 0, 0:NT * E], before16[:, :], pairs, start=True, stop=True)
                pe.matmul(ps_c[:, 1, 0:NT * E], ones16[:, :], pairs, start=True, stop=True).then_inc(counted, 1)
                if layer == 2:
                    with pe.Fori(0, 31) as i:
                        pe.wait_ge(level_asked, i + 1)
                        net.go_on(pe)
                        pe.matmul(ps_k[:, 0:E], ones16[:, :], count16[:, :], start=True, stop=True
                                  ).then_inc(level_counted, 1)
                    pe.wait_ge(level_asked, 32)
                    pairs = level16[:, :, :].rearrange("p e t -> p (e t)")
                    pe.matmul(ps_z[:, 0, 0:NT * E], before16[:, :], pairs, start=True, stop=True)
                    pe.matmul(ps_z[:, 1, 0:NT * E], ones16[:, :], pairs, start=True, stop=True
                              ).then_inc(level_counted, 1)

                def place(t, p, first, last_one):
                    for c in range(2):
                        pe.wait_ge(sides_ready, t * 2 + c + 1)
                        pe.matmul(ps_tab[:, 0:2 * P], left[p][c][:, :], right[p][c][:, :, :],
                                  start=first and c == 0, stop=last_one and c == 1).then_inc(sides_used, 1)
                place(0, 0, True, False)
                with pe.Fori(0, NT // 2 - 1) as i:
                    place(i * 2 + 1, 1, False, False)
                    place(i * 2 + 2, 0, False, False)
                place(NT - 1, 1, False, True)
                pe.wait_ge(table_copied, 1)
                for j in range(2):
                    last = pe.transpose(ps_t[:, 0, j * P:(j + 1) * P], table_rows[:, j, :], net.ident[:, :])
                last.then_inc(table_turned, 1)

            @block.scalar
            def _(act):
                act.wait_ge(loaded, 16 * n_loaded)

                def copy(b, p, first):
                    act.wait_ge(z_ready, b + 1)
                    if not first:
                        act.wait_ge(z_turned, b - 1)
                    act.activation(z_row[p][:, :], ps_z[0:E, p, :], ACT.Identity, bias=bias_col[:, 0:1]
                                   ).then_inc(z_copied, 1)
                copy(0, 0, True)
                copy(1, 1, True)
                with act.Fori(1, B // 2) as i:
                    for p in range(2):
                        copy(i * 2 + p, p, False)
                act.wait_ge(z_in, B)
                act.activation(sig[:, :, :], z[:, :, :], ACT.Exp, scale=-1.0).then_inc(exp_done, 1)

            @block.vector
            def _(dve):
                s = Order(dve, step)
                did, wait = s.did, s.wait
                if layer == 2:
                    dve.wait_ge(w_turned, 1)
                    dve.tensor_copy(w[:, :, :], ps_k[:, 0:KC * E].rearrange("p (k e) -> p k e", k=KC)
                                    ).then_inc(w_ready, 1)
                dve.wait_ge(loaded, 16 * n_loaded)
                did(dve.memset(ones[:, :], 1.0))
                did(dve.memset(ones16[:, :], 1.0))
                did(dve.tensor_copy(before16[:, :], before[:, :]))
                did(dve.tensor_scalar(less8[:, :], expert_no[:, :], float(-E), None, ALU.add))
                with dve.Fori(0, B // 2) as i:
                    for p in range(2):
                        b = i * 2 + p
                        dve.wait_ge(z_turned, b + 1)
                        dve.tensor_copy(z[:, ds(b * TB, TB), :], ps_t[:, p, 0:TB * E].rearrange(
                            "p (t e) -> p t e", e=E)).then_inc(z_in, 1)

                def over_experts(column):
                    return column.unsqueeze(2).to_broadcast(by_tile)

                def over_tiles(row):
                    return row.unsqueeze(1).to_broadcast(by_tile)

                def by_e(row):
                    return row.unsqueeze(2).to_broadcast(by_expert)

                did(dve.tensor_reduce(total[:, 0:1], before[:, :], AX.X, ALU.add))
                wait()
                did(dve.tensor_scalar(lane_col[:, :], total[:, 0:1], -1.0, float(P - 1), ALU.mult, ALU.add))
                dve.wait_ge(z_in, B)
                dve.wait_ge(exp_done, 1)
                did(dve.tensor_scalar(sig[:, :, :], sig[:, :, :], 1.0, None, ALU.add))
                wait()
                did(dve.reciprocal(sig[:, :, :], sig[:, :, :]))
                wait()
                if layer == 2:
                    did(dve.tensor_tensor(score[:, :, :], sig[:, :, :], over_tiles(bias_row[:, :]), ALU.add))
                    wait()
                    did(dve.tensor_scalar(score[:, :, :], score[:, :, :], 1e-12, None, ALU.max))
                    wait()
                    did(dve.tensor_reduce(total[:, :], score[:, :, :], AX.X, ALU.add))
                    wait()
                    did(dve.reciprocal(total[:, :], total[:, :]))
                    wait()
                    did(dve.tensor_tensor(score[:, :, :], score[:, :, :], over_experts(total[:, :]), ALU.mult))
                    wait()
                    did(dve.tensor_copy(key[:, :, :], score[:, :, :]))
                    prob = score
                else:
                    did(dve.tensor_tensor(key[:, :, :], z[:, :, :], over_tiles(bias_row[:, :]), ALU.add))
                    prob = sig
                for n, one_hot in enumerate((first, second)):
                    wait()
                    did(dve.tensor_reduce(best[:, :], key[:, :, :], AX.X, ALU.max))
                    wait()
                    did(dve.tensor_tensor(tmp[:, :, :], key[:, :, :], over_experts(best[:, :]), ALU.is_equal))
                    wait()
                    did(dve.tensor_tensor(tmp[:, :, :], tmp[:, :, :], over_tiles(less8[:, :]), ALU.mult))
                    wait()
                    did(dve.tensor_reduce(where_[:, :], tmp[:, :, :], AX.X, ALU.min))
                    wait()
                    did(dve.tensor_tensor(one_hot[:, :, :], over_tiles(less8[:, :]), over_experts(where_[:, :]),
                                          ALU.is_equal))
                    if n == 0:
                        wait()
                        did(dve.scalar_tensor_tensor(key[:, :, :], one_hot[:, :, :], -3e38, key[:, :, :],
                                                     ALU.mult, ALU.add))
                wait()
                did(dve.tensor_tensor(chosen[:, :, :], first[:, :, :], second[:, :, :], ALU.add))
                wait()
                dve.tensor_copy(chosen16[:, :, :], chosen[:, :, :]).then_inc(counts_asked, 1)
                did(dve.tensor_tensor(weights[:, :, :], prob[:, :, :], chosen[:, :, :], ALU.mult))
                wait()
                did(dve.tensor_reduce(total[:, :], weights[:, :, :], AX.X, ALU.add))
                wait()
                if layer == 2:
                    did(dve.tensor_scalar(total[:, :], total[:, :], 1e-12, None, ALU.max))
                    wait()
                did(dve.reciprocal(total[:, :], total[:, :]))
                wait()
                did(dve.tensor_tensor(weights[:, :, :], weights[:, :, :], over_experts(total[:, :]), ALU.mult))

                dve.wait_ge(counted, 1)
                did(dve.tensor_copy(per_tile[:, :, :], ps_c[:, 1, 0:NT * E].rearrange("p (t e) -> p e t", e=E)))
                wait()

                def running(out, per):
                    for e in range(E):
                        last = dve.tensor_tensor_scan(out[:, e, :], ones[:, :], per[:, e, :], 0.0, ALU.mult, ALU.add)
                        did(last)
                running(upto, per_tile)
                wait()
                did(dve.tensor_tensor(ranks[:, :, :], upto[:, :, :], per_tile[:, :, :], ALU.subtract))
                did(dve.tensor_scalar(small[:, 0, :], upto[:, :, NT - 1], float(P - 1), None, ALU.add))
                wait()
                did(dve.tensor_copy(padded_i[:, :], small[:, 0, :]))
                wait()
                did(dve.tensor_scalar(padded_i[:, :], padded_i[:, :], -P, None, ALU.bitwise_and))
                wait()
                did(dve.tensor_copy(small[:, 1, :], padded_i[:, :]))
                wait()
                did(dve.tensor_tensor_scan(small[:, 2, :], ones[:, 0:E], small[:, 1, :], 0.0, ALU.mult, ALU.add))
                wait()
                did(dve.tensor_tensor(small[:, 3, :], small[:, 2, :], small[:, 1, :], ALU.subtract))
                did(dve.tensor_tensor(tile_cmp[:, :, :], tile_start[:, :].unsqueeze(2).to_broadcast([P, SLOT_TILES, E]),
                                      small[:, 2, :].unsqueeze(1).to_broadcast([P, SLOT_TILES, E]), ALU.is_ge))
                wait()
                did(dve.tensor_tensor(ranks[:, :, :], ranks[:, :, :], by_e(small[:, 3, :]), ALU.add))
                did(dve.tensor_reduce(tile_exp[:, :], tile_cmp[:, :, :], AX.X, ALU.add))
                wait()
                did(dve.tensor_scalar(tile_exp[:, :], tile_exp[:, :], float(E - 1), None, ALU.min))
                did(dve.tensor_tensor(key[:, :, :], ps_c[:, 0, 0:NT * E].rearrange("p (t e) -> p t e", e=E),
                                      ranks[:, :, :].rearrange("p e t -> p t e"), ALU.add))
                wait()
                did(dve.tensor_copy(tables.expert[:, :], tile_exp[:, :]))
                for c, one_hot in enumerate((first, second)):
                    wait()
                    did(dve.tensor_tensor(tmp[:, :, :], key[:, :, :], one_hot[:, :, :], ALU.mult))
                    wait()
                    did(dve.tensor_reduce(slot[:, c, :], tmp[:, :, :], AX.X, ALU.add))
                wait()
                did(dve.tensor_copy(slot_i[:, :, :], slot[:, :, :]))
                wait()
                did(dve.tensor_scalar(high_i[:, :, :], slot_i[:, :, :], 7, None, ALU.logical_shift_right))
                did(dve.tensor_scalar(low_i[:, :, :], slot_i[:, :, :], P - 1, None, ALU.bitwise_and))
                wait()
                did(dve.tensor_copy(high[:, :, :], high_i[:, :, :]))
                did(dve.tensor_copy(low[:, :, :], low_i[:, :, :]))

                if layer == 2:
                    did(dve.scalar_tensor_tensor(rated[:, :, :], chosen[:, :, :].rearrange("p t e -> p e t"), -1.0,
                                                 weights[:, :, :].rearrange("p t e -> p e t"), ALU.add, ALU.add))
                    did(dve.memset(floor_[:, :], 0))
                    wait()
                    STEPS = 5
                    with dve.Fori(0, 30) as i:
                        o = Order(dve, loop_step, i * STEPS)
                        o.did(dve.tensor_tensor(candidate[:, :], floor_[:, :], bits[:, ds(i, 1), :], ALU.bitwise_or))
                        o.wait()
                        o.did(dve.tensor_tensor(over[:, :, :], rated[:, :, :], by_e(candidate[:, :].bitcast(F32)),
                                                ALU.is_ge))
                        o.wait()
                        with nc.allow_low_precision(reason="counts up to 32 are exact"):
                            dve.tensor_reduce(count16[:, :], over[:, :, :], AX.X, ALU.add).then_inc(level_asked, 1)
                        dve.wait_ge(level_counted, i + 1)
                        o.did(dve.tensor_scalar(small[:, 4, :], ps_k[:, 0:E], float(CAP), None, ALU.is_ge))
                        o.wait()
                        o.did(dve.tensor_tensor(gain[:, :], small[:, 4, :], bits[:, ds(i, 1), :], ALU.mult))
                        o.wait()
                        o.did(dve.tensor_tensor(floor_[:, :], floor_[:, :], gain[:, :], ALU.bitwise_or))
                        o.wait()
                        assert o.n == STEPS
                    floor_f = by_e(floor_[:, :].bitcast(F32))
                    did(dve.tensor_tensor(over[:, :, :], rated[:, :, :], floor_f, ALU.is_gt))
                    did(dve.tensor_tensor(level[:, :, :], rated[:, :, :], floor_f, ALU.is_equal))
                    wait()
                    with nc.allow_low_precision(reason="counts up to 32 are exact"):
                        dve.tensor_reduce(count16[:, :], over[:, :, :], AX.X, ALU.add).then_inc(level_asked, 1)
                    dve.tensor_copy(level16[:, :, :], level[:, :, :]).then_inc(level_asked, 1)
                    dve.wait_ge(level_counted, 31)
                    did(dve.tensor_scalar(small[:, 5, :], ps_k[:, 0:E], -1.0, float(CAP), ALU.mult, ALU.add))
                    dve.wait_ge(level_counted, 32)
                    did(dve.tensor_copy(per_tile[:, :, :], ps_z[:, 1, 0:NT * E].rearrange("p (e t) -> p e t", e=E)))
                    wait()
                    running(upto, per_tile)
                    wait()
                    did(dve.tensor_tensor(upto[:, :, :], upto[:, :, :], per_tile[:, :, :], ALU.subtract))
                    wait()
                    did(dve.tensor_tensor(upto[:, :, :], upto[:, :, :], ps_z[:, 0, 0:NT * E].rearrange(
                        "p (e t) -> p e t", e=E), ALU.add))
                    wait()
                    did(dve.tensor_tensor(upto[:, :, :], upto[:, :, :], by_e(small[:, 5, :]), ALU.is_lt))
                    wait()
                    did(dve.tensor_tensor(level[:, :, :], level[:, :, :], upto[:, :, :], ALU.mult))
                    wait()
                    did(dve.tensor_tensor(over[:, :, :], over[:, :, :], level[:, :, :], ALU.add))
                    wait()
                    did(dve.tensor_tensor(weights[:, :, :], weights[:, :, :], over[:, :, :].rearrange(
                        "p e t -> p t e"), ALU.mult))
                for c, one_hot in enumerate((first, second)):
                    wait()
                    did(dve.tensor_tensor(tmp[:, :, :], weights[:, :, :], one_hot[:, :, :], ALU.mult))
                    wait()
                    did(dve.tensor_reduce(wslot[:, c, :], tmp[:, :, :], AX.X, ALU.add))
                wait()

                def sides(t, p, first_):
                    for c in range(2):
                        if not first_:
                            dve.wait_ge(sides_used, t * 2 + c - 3)
                        dve.tensor_scalar(left[p][c][:, :], lane[:, :], high[:, c, ds(t, 1)], None, ALU.is_equal)
                        dve.tensor_scalar(right[p][c][:, 0, :], lane[:, :], low[:, c, ds(t, 1)],
                                          token1[:, ds(t, 1)], ALU.is_equal, ALU.mult)
                        dve.tensor_scalar(right[p][c][:, 1, :], lane[:, :], low[:, c, ds(t, 1)],
                                          wslot[:, c, ds(t, 1)], ALU.is_equal, ALU.mult).then_inc(sides_ready, 1)
                did(dve.tensor_scalar(token1[:, :], upto[:, 0, :], 0.0, None, ALU.mult))
                wait()
                did(dve.tensor_tensor_scan(token1[:, :], ones[:, :], ones[:, :], -1.0, ALU.mult, ALU.add))
                wait()
                did(dve.tensor_scalar(token1[:, :], token1[:, :], float(P), lane_col[:, 0:1], ALU.mult, ALU.add))
                wait()
                did(dve.tensor_scalar(token1[:, :], token1[:, :], 1.0, None, ALU.add))
                wait()
                sides(0, 0, True)
                sides(1, 1, True)
                with dve.Fori(1, NT // 2) as i:
                    for p in range(2):
                        sides(i * 2 + p, p, False)
                dve.wait_ge(sides_used, 2 * NT)
                dve.tensor_copy(table_rows[:, :, :], ps_tab[:, 0:2 * P].rearrange("p (j l) -> p j l", j=2)
                                ).then_inc(table_copied, 1)
                dve.wait_ge(table_turned, 1)
                did(dve.tensor_copy(table[:, :, :], ps_t[:, 0, 0:2 * P].rearrange("p (j t) -> p j t", j=2)[
                    :, :, 0:SLOT_TILES]))
                wait()
                did(dve.tensor_copy(tables.weight[:, :], table[:, 1, :]))
                did(dve.tensor_scalar(empty[:, :], table[:, 0, :], 0.0, None, ALU.is_equal))
                wait()
                did(dve.tensor_scalar(table[:, 1, :], table[:, 0, :], -1.0, 0.0, ALU.add, ALU.max))
                did(dve.tensor_scalar(tile_exp[:, :], empty[:, :], lane_col[:, 0:1], None, ALU.mult))
                wait()
                did(dve.tensor_copy(tables.take[:, :], table[:, 1, :]))
                did(dve.scalar_tensor_tensor(empty[:, :], empty[:, :], float(TOK), table[:, 1, :],
                                             ALU.mult, ALU.add))
                wait()
                did(dve.tensor_tensor(empty[:, :], empty[:, :], tile_exp[:, :], ALU.add))
                wait()
                did(dve.tensor_copy(tables.give[:, :], empty[:, :]))
                wait()


def shared_expert(net, xT, w1, w2, biases):
    nc = net.nc
    tag = "L2_shared"
    FC = 8
    with ExitStack() as ctx:
        sb = lambda name, shape, dt=F32: net.sb(f"{tag}_{name}", shape, dt, ctx)
        sem = lambda name: net.sem(f"{tag}_{name}")
        act_out = [sb(f"hidden{p}", [P, FC, S]) for p in range(2)]
        b2 = sb("b2", [P, C])
        hidden = net.ps(f"{tag}_hidden_ps", [P, 2, S], F32, ctx)
        out = net.ps(f"{tag}_out_ps", [P, 2, TB, C], F32, ctx)
        b_in = sem("b_in")
        hidden_ready = sem("hidden_ready")
        gelu_done = sem("gelu_done")
        out_ready = sem("out_ready")
        added = sem("added")
        with nc.Block() as block:
            @block.sync
            def _(sp):
                sp.dma_start(b2[:, :], net.dram["L2_ffn_sh2_b"].partition_broadcast(P)).then_inc(b_in, 16)

            @block.tensor
            def _(pe):
                def up(b, p, first):
                    for j in range(FC):
                        if not (first and j < 2):
                            pe.wait_ge(gelu_done, b * FC + j - 1)
                        for k in range(KC):
                            last = pe.matmul(hidden[:, j % 2, :], w1[:, k, j * P:(j + 1) * P], xT[:, k, ds(b * S, S)],
                                             start=k == 0, stop=k == KC - 1)
                        last.then_inc(hidden_ready, 1)

                def down(b, p, first):
                    pe.wait_ge(gelu_done, b * FC + FC)
                    if not first:
                        pe.wait_ge(added, b * 2 - 2)
                    for t in range(TB):
                        for j in range(FC):
                            last = pe.matmul(out[:, p, t, :], act_out[p][:, j, t * P:(t + 1) * P], w2[:, j, :],
                                             start=j == 0, stop=j == FC - 1)
                    last.then_inc(out_ready, 1)
                up(0, 0, True)
                up(1, 1, False)
                down(0, 0, True)
                up(2, 0, False)
                down(1, 1, True)
                with pe.Fori(1, B // 2 - 1) as i:
                    for p in range(2):
                        up(i * 2 + p + 1, 1 - p, False)
                        down(i * 2 + p, p, False)
                up(B - 1, 1, False)
                down(B - 2, 0, False)
                down(B - 1, 1, False)

            @block.scalar
            def _(act):
                def gelus(b, p, first):
                    if not first:
                        act.wait_ge(out_ready, b - 1)
                    for j in range(FC):
                        act.wait_ge(hidden_ready, b * FC + j + 1)
                        act.activation(act_out[p][:, j, :], hidden[:, j % 2, :], ACT.Gelu,
                                       bias=biases[:, j:j + 1]).then_inc(gelu_done, 1)
                gelus(0, 0, True)
                gelus(1, 1, True)
                with act.Fori(1, B // 2) as i:
                    for p in range(2):
                        gelus(i * 2 + p, p, False)

            @block.vector
            def _(dve):
                dve.wait_ge(b_in, 16)
                with dve.Fori(0, B // 2) as i:
                    for p in range(2):
                        b = i * 2 + p
                        dve.wait_ge(out_ready, b + 1)
                        x_b = net.x[:, ds(b * TB, TB), :]
                        dve.tensor_tensor(x_b, out[:, p, :, :], x_b, ALU.add).then_inc(added, 1)
                        dve.wait_ge(added, b * 2 + 1)
                        dve.tensor_tensor(x_b, x_b, b2[:, :].unsqueeze(1).to_broadcast([P, TB, C]),
                                          ALU.add).then_inc(added, 1)


def turn_weights(net, w1, w2, sh1, sh2):
    nc = net.nc
    tag = "L2_turn"
    with ExitStack() as ctx:
        sem = lambda name: net.sem(f"{tag}_{name}")
        up = [net.sb(f"{tag}_up{p}", [P, 4, C], F32, ctx) for p in range(2)]
        down = [net.sb(f"{tag}_down{p}", [P, KC, 4 * P], F32, ctx) for p in range(2)]
        ps_up = net.ps(f"{tag}_ps_up", [P, 2, KC, 4 * P], F32, ctx)
        ps_down = net.ps(f"{tag}_ps_down", [P, 2, 4, C], F32, ctx)
        loaded = [sem(f"loaded{p}") for p in range(2)]
        turned = sem("turned")
        up_copied, down_copied = sem("up_copied"), sem("down_copied")
        U = E + 2
        dram = net.dram
        fc1 = dram["L2_ffn_fc1_w"].rearrange("e (j p) c -> e p j c", p=P)
        fc2 = dram["L2_ffn_fc2_w"].rearrange("e (k p) h -> e p k h", p=P)
        sh1_in = dram["L2_ffn_sh1_w"].rearrange("(u j p) c -> u p j c", p=P, u=2)
        sh2_in = dram["L2_ffn_sh2_w"].rearrange("(k p) (u h) -> u p k h", p=P, u=2)
        with nc.Block() as block:
            @block.sync
            def _(sp):
                def load(u, p, up_in, down_in):
                    sp.dma_start(up[p][:, :, :], up_in).then_inc(loaded[p], 16)
                    sp.dma_start(down[p][:, :, :], down_in).then_inc(loaded[p], 16)
                for u in range(2):
                    load(u, u, fc1[u], fc2[u])
                with sp.Fori(1, E // 2) as i:
                    for p in range(2):
                        u = i * 2 + p
                        sp.wait_ge(turned, u * 2 - 2)
                        net.go_on(sp)
                        load(u, p, fc1[ds(u, 1)].rearrange("e p j c -> p (e j) c"),
                             fc2[ds(u, 1)].rearrange("e p k h -> p (e k) h"))
                for h in range(2):
                    sp.wait_ge(turned, (E + h) * 2 - 2)
                    load(E + h, h, sh1_in[h], sh2_in[h])

            @block.tensor
            def _(pe):
                def turn(u, p, first):
                    pe.wait_ge(loaded[p], (u - p) * 16 + 32)
                    if not first:
                        pe.wait_ge(up_copied, u - 1)
                    for k in range(KC):
                        for j in range(4):
                            last = pe.transpose(ps_up[:, p, k, j * P:(j + 1) * P], up[p][:, j, k * P:(k + 1) * P],
                                                net.ident[:, :])
                    last.then_inc(turned, 1)
                    if not first:
                        pe.wait_ge(down_copied, u - 1)
                    for j in range(4):
                        for k in range(KC):
                            last = pe.transpose(ps_down[:, p, j, k * P:(k + 1) * P], down[p][:, k, j * P:(j + 1) * P],
                                                net.ident[:, :])
                    last.then_inc(turned, 1)
                turn(0, 0, True)
                turn(1, 1, True)
                with pe.Fori(1, U // 2) as i:
                    for p in range(2):
                        turn(i * 2 + p, p, False)

            @block.scalar
            def _(act):
                with act.Fori(0, E // 2) as i:
                    for p in range(2):
                        act.wait_ge(turned, (i * 2 + p) * 2 + 1)
                        act.activation(w1[:, :, ds(i * 2 + p, 1), :].rearrange("p k e h -> p k (e h)"),
                                       ps_up[:, p, :, :], ACT.Copy).then_inc(up_copied, 1)
                for h in range(2):
                    act.wait_ge(turned, (E + h) * 2 + 1)
                    act.activation(sh1[:, :, h * 4 * P:(h + 1) * 4 * P], ps_up[:, h, :, :], ACT.Copy
                                   ).then_inc(up_copied, 1)

            @block.vector
            def _(dve):
                with dve.Fori(0, E // 2) as i:
                    for p in range(2):
                        dve.wait_ge(turned, (i * 2 + p) * 2 + 2)
                        dve.tensor_copy(w2[:, ds(i * 2 + p, 1), :, :].rearrange("p e j c -> p (e j) c"),
                                        ps_down[:, p, :, :]).then_inc(down_copied, 1)
                for h in range(2):
                    dve.wait_ge(turned, (E + h) * 2 + 2)
                    dve.tensor_copy(sh2[:, h * 4:(h + 1) * 4, :], ps_down[:, h, :, :]).then_inc(down_copied, 1)


def experts(net, layer, rows, total, w1, w2, b1, b2, tables):
    nc = net.nc
    tag = f"L{layer}_experts"
    FF = w1.shape[3]
    FC = FF // P
    FN = FF // 512
    func = ACT.Gelu if layer == 2 else ACT.Relu
    with ExitStack() as ctx:
        sb = lambda name, shape, dt=F32: net.sb(f"{tag}_{name}", shape, dt, ctx)
        sem = lambda name: net.sem(f"{tag}_{name}")
        token = [sb(f"token{j}", [P, C]) for j in range(4)]
        take = [sb(f"take{j}", [P, 1], I32) for j in range(4)]
        give = [sb(f"give{j}", [P, 1], I32) for j in range(2)]
        tokenT = [sb(f"tokenT{j}", [P, KC, P]) for j in range(2)]
        hidden = sb("hidden", [P, FF])
        hiddenT = sb("hiddenT", [P, FC, P])
        biased = [sb(f"biased{j}", [P, C]) for j in range(2)]
        result = [sb(f"result{j}", [P, C]) for j in range(2)]
        ps_x = net.ps(f"{tag}_ps_x", [P, KC, P], F32, ctx)
        ps_h = net.ps(f"{tag}_ps_h", [P, FN, 512], F32, ctx)
        ps_t = net.ps(f"{tag}_ps_t", [P, FC, P], F32, ctx)
        ps_y = [net.ps(f"{tag}_ps_y{j}", [P, 512], F32, ctx) for j in range(2)]
        take_ready = sem("take_ready")
        give_ready = sem("give_ready")
        zero = sb("zero", [P, C])
        zeroed = sem("zeroed")
        total_stored = sem("total_stored")
        gathered = [sem(f"gathered{j}") for j in range(4)]
        added = [sem(f"added{j}") for j in range(2)]
        x_turned = sem("x_turned")
        x_copied = sem("x_copied")
        h_ready = sem("h_ready")
        h_copied = sem("h_copied")
        h_turned = sem("h_turned")
        f_done = sem("f_done")
        y_ready = sem("y_ready")
        biased_ready = sem("biased_ready")
        y_done = sem("y_done")
        NS = SLOT_TILES

        def expert_of(engine, i):
            return engine.value_load(tables.expert[0:1, ds(i, 1)], min_val=0, max_val=E - 1)

        with nc.Block() as block:
            @block.sync
            def _(sp):
                sp.dma_start(total[0:TOK, :].rearrange("(u p) c -> p u c", p=P), net.x[:, :, :]
                             ).then_inc(total_stored, 16)
                sp.wait_ge(zeroed, 1)
                sp.dma_start(total[TOK:TOK + P, :], zero[:, :]).then_inc(total_stored, 16)
                sp.wait_ge(total_stored, 32)

            @block.gpsimd
            def _(pool):
                def gather(i, j, first):
                    if not first:
                        pool.wait_ge(x_turned, i - 3)
                        net.go_on(pool)
                    pool.tensor_copy(take[j][:, :], tables.take[:, ds(i, 1)]).then_inc(take_ready, 1)
                    pool.wait_ge(take_ready, i + 1)
                    net.go_on(pool)
                    pool.indirect_dma_start(out=token[j][:, :], out_offset=None, in_=rows,
                                            in_offset=bass.IndirectOffsetOnAxis(ap=take[j][:, 0:1], axis=0)
                                            ).then_inc(gathered[j], 16)

                def scatter(i, j, first):
                    pool.wait_ge(y_done, i + 1)
                    if not first:
                        pool.wait_ge(added[(j + 1) % 2], (i - 1 - (j + 1) % 2) * 8 + 16)
                    net.go_on(pool)
                    pool.tensor_copy(give[j % 2][:, :], tables.give[:, ds(i, 1)]).then_inc(give_ready, 1)
                    pool.wait_ge(give_ready, i + 1)
                    net.go_on(pool)
                    pool.indirect_dma_start(out=total, out_offset=bass.IndirectOffsetOnAxis(
                        ap=give[j % 2][:, 0:1], axis=0), in_=result[j % 2][:, :], in_offset=None,
                        compute_op=ALU.add).then_inc(added[j % 2], 16)
                for i in range(4):
                    gather(i, i, True)
                pool.wait_ge(total_stored, 32)
                scatter(0, 0, True)
                for i in range(1, 4):
                    gather(i + 3, (i + 3) % 4, False)
                    scatter(i, i, False)
                with pool.Fori(1, NS // 4 - 1) as r:
                    for j in range(4):
                        gather(r * 4 + j + 3, (j + 3) % 4, False)
                        scatter(r * 4 + j, j, False)
                gather(NS - 1, 3, False)
                for j in range(4):
                    scatter(NS - 4 + j, j, False)
                for j in range(2):
                    pool.wait_ge(added[j], NS // 2 * 16)

            @block.tensor
            def _(pe):
                def turn_x(i, j, first):
                    pe.wait_ge(gathered[j], (i - j) * 4 + 16)
                    if not first:
                        pe.wait_ge(x_copied, i)
                    for k in range(KC):
                        last = pe.transpose(ps_x[:, k, :], token[j][:, k * P:(k + 1) * P], net.ident[:, :])
                    last.then_inc(x_turned, 1)

                def up(i, j, first):
                    e = expert_of(pe, i)
                    pe.wait_ge(x_copied, i + 1)
                    if not first:
                        pe.wait_ge(h_copied, i)
                    for n in range(FN):
                        for k in range(KC):
                            last = pe.matmul(ps_h[:, n, :], tokenT[j % 2][:, k, :],
                                             w1[:, k, ds(e, 1), n * 512:(n + 1) * 512],
                                             start=k == 0, stop=k == KC - 1)
                    last.then_inc(h_ready, 1)

                def turn_h(i, first):
                    pe.wait_ge(h_copied, i + 1)
                    if not first:
                        pe.wait_ge(f_done, i)
                    for c in range(FC):
                        last = pe.transpose(ps_t[:, c, :], hidden[:, c * P:(c + 1) * P], net.ident[:, :])
                    last.then_inc(h_turned, 1)

                def down(i, j, first):
                    e = expert_of(pe, i)
                    pe.wait_ge(f_done, i + 1)
                    if not first:
                        pe.wait_ge(y_done, i - 1)
                    for c in range(FC):
                        last = pe.matmul(ps_y[j % 2][:, 0:C], hiddenT[:, c, :], w2[:, ds(e, 1), c, :],
                                         start=c == 0, stop=c == FC - 1)
                    last.then_inc(y_ready, 1)

                def tile(i, j, first=False, second=False, more=2):
                    turn_h(i, first)
                    if more >= 1:
                        up(i + 1, j + 1, False)
                    if more >= 2:
                        turn_x(i + 2, (j + 2) % 4, False)
                    down(i, j, first or second)
                turn_x(0, 0, True)
                turn_x(1, 1, False)
                up(0, 0, True)
                for i in range(4):
                    tile(i, i, first=i == 0, second=i == 1)
                with pe.Fori(1, NS // 4 - 1) as r:
                    for j in range(4):
                        tile(r * 4 + j, j)
                for j in range(4):
                    tile(NS - 4 + j, j, more=3 - j)

            @block.scalar
            def _(act):
                def apply(i, first):
                    e = expert_of(act, i)
                    act.wait_ge(h_turned, i + 1)
                    if not first:
                        act.wait_ge(y_ready, i)
                    net.go_on(act)
                    for c in range(FC):
                        last = act.activation(hiddenT[:, c, :], ps_t[:, c, :], func, bias=b1[:, ds(e, 1), c])
                    last.then_inc(f_done, 1)
                apply(0, True)
                with act.Fori(1, NS) as i:
                    apply(i, False)

            @block.vector
            def _(dve):
                def copy_x(i, j, first):
                    dve.wait_ge(x_turned, i + 1)
                    if not first:
                        dve.wait_ge(h_ready, i - 1)
                    dve.tensor_copy(tokenT[j % 2][:, :, :], ps_x[:, :, :]).then_inc(x_copied, 1)

                def copy_h(i, first):
                    dve.wait_ge(h_ready, i + 1)
                    if not first:
                        dve.wait_ge(h_turned, i)
                    dve.tensor_copy(hidden[:, :], ps_h[:, :, :].rearrange("p n f -> p (n f)")).then_inc(h_copied, 1)

                def weigh(i, j, first):
                    e = expert_of(dve, i)
                    dve.wait_ge(y_ready, i + 1)
                    dve.tensor_tensor(biased[j % 2][:, :], ps_y[j % 2][:, 0:C], b2[:, ds(e, 1), :], ALU.add
                                      ).then_inc(biased_ready, 1)
                    dve.wait_ge(biased_ready, i + 1)
                    if not first:
                        dve.wait_ge(added[j % 2], (i - j % 2) * 8)
                    dve.tensor_scalar(result[j % 2][:, :], biased[j % 2][:, :], tables.weight[:, ds(i, 1)], None,
                                      ALU.mult).then_inc(y_done, 1)

                def tile(i, j, first=False, more=2):
                    if more >= 1:
                        copy_h(i + 1, False)
                    if more >= 2:
                        copy_x(i + 2, j, False)
                    weigh(i, j, first)
                dve.memset(zero[:, :], 0.0).then_inc(zeroed, 1)
                copy_x(0, 0, True)
                copy_x(1, 1, True)
                copy_h(0, True)
                for i in range(2):
                    tile(i, i, first=True)
                with dve.Fori(1, NS // 2 - 1) as r:
                    for j in range(2):
                        tile(r * 2 + j, j)
                tile(NS - 2, 0, more=1)
                tile(NS - 1, 1, more=0)


def load_expert_weights(net, w1, w2):
    loaded = net.sem("L3_moe_w_loaded")
    with net.nc.Block() as block:
        @block.sync
        def _(sp):
            for k in range(KC):
                sp.dma_start(w1[:, k, :, :], net.dram["L3_ffn_w1"].rearrange("e (k p) f -> k p e f", p=P)[k]
                             ).then_inc(loaded, 16)
            for e in range(E):
                sp.dma_start(w2[:, e, :, :], net.dram["L3_ffn_w2"][e].rearrange("(j p) c -> p j c", p=P)
                             ).then_inc(loaded, 16)
            sp.wait_ge(loaded, (KC + E) * 16)


def load_biases(net, layer, b1, b2, sh_b1=None):
    names = ("L2_ffn_fc1_b", "L2_ffn_fc2_b") if layer == 2 else ("L3_ffn_b1", "L3_ffn_b2")
    loaded = net.sem(f"L{layer}_biases_loaded")
    with net.nc.Block() as block:
        @block.sync
        def _(sp):
            with net.nc.allow_non_contiguous_dma(reason="bias columns"):
                for e in range(E):
                    sp.dma_start(b1[:, e, :], net.dram[names[0]][e].rearrange("(j p) -> p j", p=P)
                                 ).then_inc(loaded, 16)
                if sh_b1 is not None:
                    sp.dma_start(sh_b1[:, :], net.dram["L2_ffn_sh1_b"].rearrange("(j p) -> p j", p=P)
                                 ).then_inc(loaded, 16)
            for e in range(E):
                sp.dma_start(b2[:, e, :], net.dram[names[1]][e].partition_broadcast(P)).then_inc(loaded, 16)
            sp.wait_ge(loaded, (2 * E + (sh_b1 is not None)) * 16)


def read_back(net, tag, total):
    loaded = net.sem(f"{tag}_read_back")
    with net.nc.Block() as block:
        @block.sync
        def _(sp):
            sp.dma_start(net.x[:, :, :], total[0:TOK, :].rearrange("(u p) c -> p u c", p=P)).then_inc(loaded, 16)
            sp.wait_ge(loaded, 16)


def ffn_block(net, layer, total):
    tag = f"L{layer}_moe"
    rows = net.nc.dram_tensor(f"{tag}_rows", (TOK, C), F32).ap()
    FF = 512 if layer == 2 else 1024
    FC = FF // P
    with ExitStack() as ctx:
        tables = Tables(net, tag, ctx)
        b1 = net.sb(f"{tag}_b1", [P, E, FC], F32, ctx)
        b2 = net.sb(f"{tag}_b2", [P, E, C], F32, ctx)
        if layer == 2:
            w1 = net.sb(f"{tag}_w1", [P, KC, E, FF], F32, ctx)
            w2 = net.sb(f"{tag}_w2", [P, E, FC, C], F32, ctx)
        with ExitStack() as early:
            net.hold_channels(tag, early)
            layer_norm(net, f"{tag}_ln", rows)
            route(net, layer, net.xT, tables)
            if layer == 2:
                SH = net.dram["L2_ffn_sh1_b"].shape[0]
                sh1 = net.sb(f"{tag}_sh1", [P, KC, SH], F32, early)
                sh2 = net.sb(f"{tag}_sh2", [P, SH // P, C], F32, early)
                sh_b1 = net.sb(f"{tag}_sh_b1", [P, SH // P], F32, early)
                load_biases(net, layer, b1, b2, sh_b1)
                turn_weights(net, w1, w2, sh1, sh2)
                shared_expert(net, net.xT, sh1, sh2, sh_b1)
        if layer == 3:
            w1 = net.sb(f"{tag}_w1", [P, KC, E, FF], F32, ctx)
            w2 = net.sb(f"{tag}_w2", [P, E, FC, C], F32, ctx)
            load_biases(net, layer, b1, b2)
            load_expert_weights(net, w1, w2)
        experts(net, layer, rows, total, w1, w2, b1, b2, tables)


def build(nc, dram, out):
    with ExitStack() as ctx:
        net = Net(nc, ctx, dram)
        conv_layers(net)
        net.clear_semaphores()
        attention_block(net, 2)
        net.clear_semaphores()
        total = nc.dram_tensor("L2_moe_total", (TOK + P, C), F32).ap()
        ffn_block(net, 2, total)
        read_back(net, "L2_moe", total)
        net.clear_semaphores()
        attention_block(net, 3)
        net.clear_semaphores()
        ffn_block(net, 3, out)


def kernel(**inputs):
    import concourse.bacc as _bacc
    from concourse.bass_utils import run_bass_kernel_spmd as _run

    nc = _bacc.Bacc("TRN2", target_bir_lowering=False, num_devices=1)
    arrays = {k: np.ascontiguousarray(v) for k, v in inputs.items()}
    arrays.update(host_constants())
    dram = {k: nc.dram_tensor(k, v.shape, mybir.dt.from_np(v.dtype), kind="ExternalInput").ap()
            for k, v in arrays.items()}
    out = nc.dram_tensor("out", (TOK + P, C), F32, kind="ExternalOutput").ap()
    build(nc, dram, out)
    nc.finalize()
    r = _run(nc, [arrays], core_ids=[0])
    return r.results[0]["out"][:TOK].reshape(B, T, N, C)
```

```python
from contextlib import ExitStack

import numpy as np

import concourse.bass as bass
from concourse import mybir

F32 = mybir.dt.float32
BF16 = mybir.dt.bfloat16
I32 = mybir.dt.int32
U32 = mybir.dt.uint32
ALU = mybir.AluOpType
ACT = mybir.ActivationFunctionType
AX = mybir.AxisListType
ds = bass.ds

P = 128
B, T, N, C = 8, 16, 32, 256
LAT = C // 2
S = T * N
TOK = B * S
KC = C // P
NT = TOK // P
TB = S // P
NH, NKV, HD = 16, 4, 16
GR = NH // NKV
E = 8
CAP = 1280
SLOT_TILES = 2 * TOK // P + E
SLOTS = SLOT_TILES * P
BN_EPS = 1e-5
LN_EPS = 1e-5


def host_constants():
    tok = np.arange(S)
    same_time = tok[:, None] // N == tok[None, :] // N
    same_joint = tok[:, None] % N == tok[None, :] % N
    mix = (same_time / np.float32(N) + same_joint / np.float32(T)) / np.float32(T + N)
    mix = mix.astype(np.float32).reshape(TB, P, S).transpose(1, 0, 2)
    q, k = np.arange(P)[:, None], np.arange(P)[None, :]
    inv = np.float32(1.0) / np.float32(10000.0) ** (np.arange(0, HD, 2, dtype=np.float32) / np.float32(HD))
    freqs = np.arange(S, dtype=np.float32)[:, None] * inv.astype(np.float32)
    emb = np.concatenate([freqs, freqs], axis=-1)
    width_of = (np.arange(P) % (GR * HD) // GR, np.arange(P) % HD)
    step_of = (GR, 1)
    rope = np.stack([f(emb).T[w] for w in width_of for f in (np.cos, np.sin)], 1)
    swap = np.zeros((P, 2, P), np.float32)
    for j, (w, step) in enumerate(zip(width_of, step_of)):
        for r in range(P):
            if w[r] < HD // 2:
                swap[r + step * HD // 2, j, r] = -1.0
            else:
                swap[r - step * HD // 2, j, r] = 1.0
    return {
        "c_ident": np.eye(P, dtype=np.float32),
        "c_mix": np.ascontiguousarray(mix),
        "c_causal": np.where(k > q, np.float32(-1e30), np.float32(0)).astype(np.float32),
        "c_rope": np.ascontiguousarray(rope.astype(np.float32)),
        "c_swap": swap,
        "c_before": (q < k).astype(np.float32),
        "c_expert": np.ascontiguousarray(np.broadcast_to(np.arange(E, dtype=np.float32), (P, E))),
        "c_tilestart": np.ascontiguousarray(np.broadcast_to(
            np.arange(SLOT_TILES, dtype=np.float32) * P, (P, SLOT_TILES))),
        "c_bits": np.ascontiguousarray(np.broadcast_to(
            (1 << np.arange(30, -1, -1)).astype(np.int32)[:, None], (P, 31, E))),
        "c_lane": np.ascontiguousarray(np.broadcast_to(np.arange(P, dtype=np.float32), (P, P))),
    }


class Order:

    def __init__(self, engine, semaphore, base=0):
        self.engine, self.semaphore, self.base, self.n = engine, semaphore, base, 0

    def did(self, instruction):
        instruction.then_inc(self.semaphore, 1)
        self.n += 1
        return self.n

    def wait(self):
        self.engine.wait_ge(self.semaphore, self.base + self.n)


class Net:

    def __init__(self, nc, ctx, dram):
        self.nc, self.ctx, self.dram = nc, ctx, dram
        self.part, self.sems = 0, []
        self.going = self.sem("going0")
        self.ident = self.sb("ident", [P, P], F32)
        self.x = self.sb("x_tokens", [P, NT, C], F32)
        self.xT = None

    def hold_channels(self, tag, ctx):
        self.xT = self.sb(f"{tag}_x_channels", [P, KC, TOK], F32, ctx)

    def go_on(self, engine):
        engine.sem_inc(self.going, 1)

    def sb(self, name, shape, dt, ctx=None):
        return (ctx or self.ctx).enter_context(self.nc.sbuf_tensor(name, shape, dt))

    def ps(self, name, shape, dt, ctx):
        return ctx.enter_context(self.nc.psum_tensor(name, shape, dt))

    def sem(self, name):
        semaphore = self.nc.alloc_semaphore(name=name)
        self.sems.append(semaphore)
        return semaphore

    def clear_semaphores(self):
        self.nc.clear_and_free_semaphores(self.sems)
        self.nc.all_engine_barrier()
        self.part += 1
        self.sems = []
        self.going = self.sem(f"going{self.part}")


def load_tokens(net):
    nc = net.nc
    with ExitStack() as ctx:
        ring = [net.sb(f"load_ring{p}", [P, TB, C], F32, ctx) for p in range(2)]
        turned = net.ps("load_turned", [P, 2, KC, S], F32, ctx)
        const_in = net.sem("load_const_in")
        loaded = [net.sem(f"load_loaded{p}") for p in range(2)]
        turned_ready = net.sem("load_turned_ready")
        copied_a = net.sem("load_copied_a")
        copied_v = net.sem("load_copied_v")
        x_tiles = net.dram["x"].rearrange("b t n c -> (b t n) c").rearrange("(u p) c -> p u c", p=P)
        with nc.Block() as block:
            @block.sync
            def _(sp):
                sp.dma_start(net.ident[:, :], net.dram["c_ident"]).then_inc(const_in, 16)

                def load(b, p):
                    sp.dma_start(ring[p][:, :, :], x_tiles[:, ds(b * TB, TB), :]).then_inc(loaded[p], 16)
                load(0, 0)
                load(1, 1)
                with sp.Fori(1, B // 2) as i:
                    for p in range(2):
                        sp.wait_ge(turned_ready, i * 2 + p - 1)
                        net.go_on(sp)
                        load(i * 2 + p, p)

            @block.tensor
            def _(pe):
                pe.wait_ge(const_in, 16)

                def turn(b, p, first):
                    if not first:
                        pe.wait_ge(copied_a, b - 1)
                        pe.wait_ge(copied_v, b - 1)
                    for c in range(KC):
                        for t in range(TB):
                            last = pe.transpose(turned[:, p, c, t * P:(t + 1) * P],
                                                ring[p][:, t, c * P:(c + 1) * P], net.ident[:, :])
                    last.then_inc(turned_ready, 1)
                for p in range(2):
                    pe.wait_ge(loaded[p], 16)
                    turn(p, p, True)
                with pe.Fori(1, B // 2) as i:
                    for p in range(2):
                        pe.wait_ge(loaded[p], i * 16 + 16)
                        turn(i * 2 + p, p, False)

            @block.scalar
            def _(act):
                with act.Fori(0, B // 2) as i:
                    for p in range(2):
                        act.wait_ge(turned_ready, i * 2 + p + 1)
                        act.activation(net.xT[:, 0, ds((i * 2 + p) * S, S)], turned[:, p, 0, :],
                                       ACT.Copy).then_inc(copied_a, 1)

            @block.vector
            def _(dve):
                with dve.Fori(0, B // 2) as i:
                    for p in range(2):
                        dve.wait_ge(turned_ready, i * 2 + p + 1)
                        dve.tensor_copy(net.xT[:, 1, ds((i * 2 + p) * S, S)],
                                        turned[:, p, 1, :]).then_inc(copied_v, 1)


def inverse_root(net, eng_steps, dve, var, root, out, tmp, sqrt_asked, sqrt_done, asked):
    s = eng_steps
    s.wait()
    dve.tensor_copy(root, var).then_inc(sqrt_asked, 1)
    dve.wait_ge(sqrt_done, asked)
    s.did(dve.reciprocal(out, root))
    s.wait()
    s.did(dve.tensor_tensor(tmp, out, out, ALU.mult))
    s.wait()
    s.did(dve.tensor_tensor(tmp, tmp, var, ALU.mult))
    s.wait()
    s.did(dve.tensor_scalar(tmp, tmp, -0.5, 1.5, ALU.mult, ALU.add))
    s.wait()
    s.did(dve.tensor_tensor(out, out, tmp, ALU.mult))


def conv_block(net, layer, to_tokens):
    nc = net.nc
    n_ = f"L{layer}"
    with ExitStack() as ctx:
        sb = lambda name, shape, dt=F32: net.sb(f"{n_}_{name}", shape, dt, ctx)
        sem = lambda name: net.sem(f"{n_}_{name}")
        w_in = sb("w_in", [P, 3, C])
        ww_in = sb("ww_in", [P, KC, LAT])
        affine = sb("affine", [P, 2, KC])
        wT = sb("wT", [P, KC, 3, LAT])
        wwT = sb("wwT", [P, C])
        mix = sb("mix", [P, TB, S])
        xb = [sb(f"xb{p}", [P, KC, S]) for p in range(2)]
        theta = [sb(f"theta{p}", [P, S]) for p in range(2)]
        phi = [sb(f"phi{p}", [P, S]) for p in range(2)]
        g = [sb(f"g{p}", [P, TB, LAT]) for p in range(2)]
        mixed = [sb(f"mixed{p}", [P, TB, S]) for p in range(2)]
        st = [sb(f"st{p}", [P, S]) for p in range(2)]
        stats = sb("stats", [P, KC, B, 6])
        norm = sb("norm", [P, 12, KC])
        mv = sb("mv", [P, KC, 2])
        turned = net.ps(f"{n_}_ps_turned", [P, S], F32, ctx)
        ps_phi = net.ps(f"{n_}_ps_phi", [P, S], F32, ctx)
        ps_g = net.ps(f"{n_}_ps_g", [P, TB, LAT], F32, ctx)
        ps_s = net.ps(f"{n_}_ps_s", [P, 2, S], F32, ctx)
        ps_st = net.ps(f"{n_}_ps_st", [P, S], F32, ctx)
        ps_out = net.ps(f"{n_}_ps_out", [P, KC, S], F32, ctx)
        ps_theta = turned

        w_loaded = sem("w_loaded")
        mix_loaded = sem("mix_loaded")
        affine_loaded = sem("affine_loaded")
        w_turned = sem("w_turned")
        w_ready = sem("w_ready")
        xb_ready = sem("xb_ready")
        projected = sem("projected")
        proj_copied = sem("proj_copied")
        scored = sem("scored")
        masked = sem("masked")
        st_ready = sem("st_ready")
        st_copied = sem("st_copied")
        out_ready = sem("out_ready")
        out_added = sem("out_added")
        stats_step = sem("stats_step")
        sqrt_asked, sqrt_done = sem("sqrt_asked"), sem("sqrt_done")
        norm_step = sem("norm_step")
        norm_ready = sem("norm_ready")
        bn_done_a, bn_done_v = sem("bn_done_a"), sem("bn_done_v")
        bn_turned = sem("bn_turned")
        bn_copied_a, bn_copied_v = sem("bn_copied_a"), sem("bn_copied_v")

        mean, var, root, inv, scale, shift, tmp = (norm[:, j, :] for j in range(7))

        with nc.Block() as block:
            @block.sync
            def _(sp):
                for j, w in enumerate(("Wt", "Wp", "Wg")):
                    sp.dma_start(w_in[:, j, :], net.dram[f"L{layer}_conv_{w}"]).then_inc(w_loaded, 16)
                sp.dma_start(ww_in[:, :, :], net.dram[f"L{layer}_conv_Ww"].rearrange("(k p) l -> p k l", p=P)
                             ).then_inc(w_loaded, 16)
                sp.dma_start(mix[:, :, :], net.dram["c_mix"]).then_inc(mix_loaded, 16)
                for j, w in enumerate(("gamma", "beta")):
                    for c in range(KC):
                        sp.dma_start(affine[:, j, c:c + 1],
                                     net.dram[f"L{layer}_conv_{w}"][c * P:(c + 1) * P].rearrange("(p a) -> p a", a=1)
                                     ).then_inc(affine_loaded, 16)

            @block.tensor
            def _(pe):
                pe.wait_ge(w_loaded, 64)
                for j in range(3):
                    for k in range(KC):
                        bank, at = ((ps_s[:, 0, :], 2 * j + k) if 2 * j + k < 4 else (ps_s[:, 1, :], 2 * j + k - 4))
                        pe.transpose(bank[:, at * P:(at + 1) * P], w_in[:, j, k * P:(k + 1) * P], net.ident[:, :])
                for c in range(KC):
                    last = pe.transpose(ps_s[:, 1, (2 + c) * P:(3 + c) * P], ww_in[:, c, :], net.ident[:, :])
                last.then_inc(w_turned, 1)
                pe.wait_ge(w_ready, 2)

                def project(b, p, first):
                    pe.wait_ge(xb_ready, b + 1)
                    for j, out in enumerate((ps_theta, ps_phi)):
                        if not first:
                            pe.wait_ge(proj_copied, b * 3 + j - 2)
                        for k in range(KC):
                            last = pe.matmul(out[:, :], wT[:, k, j, :], xb[p][:, k, :], start=k == 0, stop=k == KC - 1)
                        last.then_inc(projected, 1)
                    if not first:
                        pe.wait_ge(proj_copied, b * 3)
                    for t in range(TB):
                        for k in range(KC):
                            last = pe.matmul(ps_g[:, t, :], xb[p][:, k, t * P:(t + 1) * P], wT[:, k, 2, :],
                                             start=k == 0, stop=k == KC - 1)
                    last.then_inc(projected, 1)

                def score(b, p, first):
                    pe.wait_ge(proj_copied, b * 3 + 2)
                    for kb in range(TB):
                        if not (first and kb < 2):
                            pe.wait_ge(masked, b * TB + kb - 1)
                        pe.matmul(ps_s[:, kb % 2, :], phi[p][:, kb * P:(kb + 1) * P], theta[p][:, :],
                                  start=True, stop=True).then_inc(scored, 1)

                def output(b, p, first):
                    pe.wait_ge(proj_copied, b * 3 + 3)
                    pe.wait_ge(masked, b * TB + TB)
                    if not first:
                        pe.wait_ge(st_copied, b)
                    for kb in range(TB):
                        last = pe.matmul(ps_st[:, :], g[p][:, kb, :], mixed[p][:, kb, :],
                                         start=kb == 0, stop=kb == TB - 1)
                    last.then_inc(st_ready, 1)
                    pe.wait_ge(st_copied, b + 1)
                    if not first:
                        pe.wait_ge(out_added, b * KC)
                    for c in range(KC):
                        pe.matmul(ps_out[:, c, :], wwT[:, c * P:(c + 1) * P], st[p][:, :],
                                  start=True, stop=True).then_inc(out_ready, 1)

                project(0, 0, True)
                score(0, 0, True)
                project(1, 1, False)
                score(1, 1, False)
                output(0, 0, True)
                with pe.Fori(1, B // 2) as i:
                    for p in range(2):
                        project(i * 2 + p, p, False)
                        score(i * 2 + p, p, False)
                        output(i * 2 + p - 1, 1 - p, False)
                output(B - 1, 1, False)
                if to_tokens:
                    def turn(b, p, first):
                        pe.wait_ge(bn_done_a, b + 1)
                        pe.wait_ge(bn_done_v, b + 1)
                        if not first:
                            pe.wait_ge(bn_copied_a, b - 1)
                            pe.wait_ge(bn_copied_v, b - 1)
                        dst = (ps_out, ps_s)[p]
                        for t in range(TB):
                            for c in range(KC):
                                last = pe.transpose(dst[:, t // 2, (t % 2) * C + c * P:(t % 2) * C + (c + 1) * P],
                                                    xb[p][:, c, t * P:(t + 1) * P], net.ident[:, :])
                        last.then_inc(bn_turned, 1)
                    turn(0, 0, True)
                    turn(1, 1, True)
                    with pe.Fori(1, B // 2) as i:
                        for p in range(2):
                            turn(i * 2 + p, p, False)

            @block.scalar
            def _(act):
                def fetch(b, p, first):
                    if not first:
                        act.wait_ge(projected, b * 3 - 3)
                    act.activation(xb[p][:, :, :], net.xT[:, :, ds(b * S, S)], ACT.Copy).then_inc(xb_ready, 1)

                def copy_projections(b, p, first):
                    for j, (src, dst) in enumerate(((ps_theta, theta), (ps_phi, phi), (ps_g, g))):
                        act.wait_ge(projected, b * 3 + j + 1)
                        if j == 0 and not first:
                            act.wait_ge(st_ready, b - 1)
                        act.activation(dst[p][:], src[:], ACT.Copy).then_inc(proj_copied, 1)

                def copy_st(b, p):
                    act.wait_ge(st_ready, b + 1)
                    act.activation(st[p][:, :], ps_st[:, :], ACT.Copy).then_inc(st_copied, 1)
                act.wait_ge(w_ready, 2)
                fetch(0, 0, True)
                fetch(1, 1, True)
                copy_projections(0, 0, True)
                copy_projections(1, 1, True)
                fetch(2, 0, False)
                copy_st(0, 0)
                with act.Fori(1, B // 2 - 1) as i:
                    for p in range(2):
                        copy_projections(i * 2 + p, p, False)
                        fetch(i * 2 + p + 1, 1 - p, False)
                        copy_st(i * 2 + p - 1, 1 - p)
                copy_projections(B - 2, 0, False)
                fetch(B - 1, 1, False)
                copy_st(B - 3, 1)
                copy_projections(B - 1, 1, False)
                copy_st(B - 2, 0)
                copy_st(B - 1, 1)
                act.wait_ge(sqrt_asked, 1)
                act.activation(root, root, ACT.Sqrt).then_inc(sqrt_done, 1)
                act.wait_ge(norm_ready, 1)
                if not to_tokens:
                    act.activation(net.xT[:, 0, :], net.xT[:, 0, :], ACT.Identity, bias=shift[:, 0:1],
                                   scale=scale[:, 0:1]).then_inc(bn_done_a, 1)
                else:
                    def norm0(b, p, first):
                        if not first:
                            act.wait_ge(bn_turned, b - 1)
                        act.activation(xb[p][:, 0, :], net.xT[:, 0, ds(b * S, S)], ACT.Identity,
                                       bias=shift[:, 0:1], scale=scale[:, 0:1]).then_inc(bn_done_a, 1)

                    def take(b, p):
                        act.wait_ge(bn_turned, b + 1)
                        act.activation(net.x[:, ds(b * TB, 2), :], (ps_out, ps_s)[p][:, 0, :].rearrange(
                            "p (t c) -> p t c", c=C), ACT.Copy).then_inc(bn_copied_a, 1)
                    norm0(0, 0, True)
                    norm0(1, 1, True)
                    with act.Fori(1, B // 2) as i:
                        for p in range(2):
                            take(i * 2 + p - 2, p)
                            norm0(i * 2 + p, p, False)
                    take(B - 2, 0)
                    take(B - 1, 1)

            @block.vector
            def _(dve):
                dve.wait_ge(w_turned, 1)
                dve.tensor_copy(wT[:, :, :, :].rearrange("p k j l -> p j k l")[:, 0:2, :, :],
                                ps_s[:, 0, :].rearrange("p (j k l) -> p j k l", j=2, k=KC)).then_inc(w_ready, 1)
                dve.tensor_copy(wT[:, :, 2, :], ps_s[:, 1, 0:2 * P].rearrange("p (k l) -> p k l", k=KC))
                dve.tensor_copy(wwT[:, :], ps_s[:, 1, 2 * P:4 * P]).then_inc(w_ready, 1)
                dve.wait_ge(mix_loaded, 16)

                def mask(b, p, first):
                    if not first:
                        dve.wait_ge(st_ready, b - 1)
                    for kb in range(TB):
                        dve.wait_ge(scored, b * TB + kb + 1)
                        dve.tensor_tensor(mixed[p][:, kb, :], ps_s[:, kb % 2, :], mix[:, kb, :],
                                          ALU.mult).then_inc(masked, 1)

                def add(b, p):
                    for c in range(KC):
                        dve.wait_ge(out_ready, b * KC + c + 1)
                        x_c = net.xT[:, c, ds(b * S, S)]
                        dve.tensor_tensor(x_c, ps_out[:, c, :], x_c, ALU.add).then_inc(out_added, 1)
                        dve.wait_ge(out_added, b * KC + c + 1)
                        dve.bn_stats(stats[:, c, ds(b, 1), :], x_c).then_inc(stats_step, 1)
                mask(0, 0, True)
                mask(1, 1, True)
                add(0, 0)
                with dve.Fori(1, B // 2) as i:
                    for p in range(2):
                        mask(i * 2 + p, p, False)
                        add(i * 2 + p - 1, 1 - p)
                add(B - 1, 1)
                s = Order(dve, norm_step)
                dve.wait_ge(affine_loaded, 64)
                dve.wait_ge(stats_step, B * KC)
                for c in range(KC):
                    s.did(dve.bn_aggr(mv[:, c, :], stats[:, c, :, :].rearrange("p b f -> p (b f)")))
                s.wait()
                s.did(dve.tensor_copy(mean, mv[:, :, 0]))
                s.did(dve.tensor_scalar(var, mv[:, :, 1], BN_EPS, None, ALU.add))
                inverse_root(net, s, dve, var, root, inv, tmp, sqrt_asked, sqrt_done, 1)
                s.wait()
                s.did(dve.tensor_tensor(scale, inv, affine[:, 0, :], ALU.mult))
                s.wait()
                s.did(dve.tensor_tensor(tmp, mean, scale, ALU.mult))
                s.wait()
                dve.tensor_tensor(shift, affine[:, 1, :], tmp, ALU.subtract).then_inc(norm_ready, 1)
                dve.wait_ge(norm_ready, 1)
                if not to_tokens:
                    dve.tensor_scalar(net.xT[:, 1, :], net.xT[:, 1, :], scale[:, 1:2], shift[:, 1:2],
                                      ALU.mult, ALU.add).then_inc(bn_done_v, 1)
                else:
                    def norm1(b, p, first):
                        if not first:
                            dve.wait_ge(bn_turned, b - 1)
                        dve.tensor_scalar(xb[p][:, 1, :], net.xT[:, 1, ds(b * S, S)], scale[:, 1:2], shift[:, 1:2],
                                          ALU.mult, ALU.add).then_inc(bn_done_v, 1)

                    def take(b, p):
                        dve.wait_ge(bn_turned, b + 1)
                        dve.tensor_copy(net.x[:, ds(b * TB + 2, 2), :], (ps_out, ps_s)[p][:, 1, :].rearrange(
                            "p (t c) -> p t c", c=C)).then_inc(bn_copied_v, 1)
                    norm1(0, 0, True)
                    norm1(1, 1, True)
                    with dve.Fori(1, B // 2) as i:
                        for p in range(2):
                            take(i * 2 + p - 2, p)
                            norm1(i * 2 + p, p, False)
                    take(B - 2, 0)
                    take(B - 1, 1)


def conv_layers(net):
    with ExitStack() as ctx:
        net.hold_channels("conv", ctx)
        load_tokens(net)
        conv_block(net, 0, False)
        conv_block(net, 1, True)


def layer_norm(net, tag, to_dram=None):
    nc = net.nc
    with ExitStack() as ctx:
        sb = lambda name, shape, dt=F32: net.sb(f"{tag}_{name}", shape, dt, ctx)
        sem = lambda name: net.sem(f"{tag}_{name}")
        stats = sb("stats", [P, NT, 6])
        mv = sb("mv", [P, NT, 2])
        var, root, rstd, tmp = (sb(n, [P, NT]) for n in ("var", "root", "rstd", "tmp"))
        normed = [sb(f"normed{p}", [P, TB, C]) for p in range(2)]
        turned = net.ps(f"{tag}_turned", [P, 2, KC, S], F32, ctx)
        stats_step, aggr_step, step = sem("stats_step"), sem("aggr_step"), sem("step")
        sqrt_asked, sqrt_done = sem("sqrt_asked"), sem("sqrt_done")
        normed_ready = sem("normed_ready")
        turned_ready = sem("turned_ready")
        copied = sem("copied")
        stored = [sem(f"stored{p}") for p in range(2)]
        with nc.Block() as block:
            @block.vector
            def _(dve):
                with dve.Fori(0, B) as b:
                    for t in range(TB):
                        dve.bn_stats(stats[:, ds(b * TB + t, 1), :], net.x[:, ds(b * TB + t, 1), :]
                                     ).then_inc(stats_step, 1)
                dve.wait_ge(stats_step, NT)
                for t in range(NT):
                    dve.bn_aggr(mv[:, t, :], stats[:, t, :]).then_inc(aggr_step, 1)
                dve.wait_ge(aggr_step, NT)
                s = Order(dve, step)
                s.did(dve.tensor_scalar(var[:, :], mv[:, :, 1], LN_EPS, None, ALU.add))
                inverse_root(net, s, dve, var[:, :], root[:, :], rstd[:, :], tmp[:, :], sqrt_asked, sqrt_done, 1)
                s.wait()

                def normalise(b, p, first):
                    if not first:
                        dve.wait_ge(turned_ready, b - 1)
                        if to_dram is not None:
                            dve.wait_ge(stored[p], (b - p) * 8)
                    for t in range(TB):
                        last = dve.tensor_scalar(normed[p][:, t, :], net.x[:, ds(b * TB + t, 1), :],
                                                 mv[:, ds(b * TB + t, 1), 0], rstd[:, ds(b * TB + t, 1)],
                                                 ALU.subtract, ALU.mult)
                    last.then_inc(normed_ready, 1)
                normalise(0, 0, True)
                normalise(1, 1, True)
                with dve.Fori(1, B // 2) as i:
                    for p in range(2):
                        normalise(i * 2 + p, p, False)

            @block.tensor
            def _(pe):
                def turn(b, p, first):
                    pe.wait_ge(normed_ready, b + 1)
                    if not first:
                        pe.wait_ge(copied, b - 1)
                    for c in range(KC):
                        for t in range(TB):
                            last = pe.transpose(turned[:, p, c, t * P:(t + 1) * P],
                                                normed[p][:, t, c * P:(c + 1) * P], net.ident[:, :])
                    last.then_inc(turned_ready, 1)
                turn(0, 0, True)
                turn(1, 1, True)
                with pe.Fori(1, B // 2) as i:
                    for p in range(2):
                        turn(i * 2 + p, p, False)

            @block.scalar
            def _(act):
                act.wait_ge(sqrt_asked, 1)
                act.activation(root[:, :], root[:, :], ACT.Sqrt).then_inc(sqrt_done, 1)
                with act.Fori(0, B // 2) as i:
                    for p in range(2):
                        act.wait_ge(turned_ready, i * 2 + p + 1)
                        act.activation(net.xT[:, :, ds((i * 2 + p) * S, S)], turned[:, p, :, :],
                                       ACT.Copy).then_inc(copied, 1)

            if to_dram is not None:
                rows = to_dram.rearrange("(u p) c -> p u c", p=P)

                @block.sync
                def _(sp):
                    with sp.Fori(0, B // 2) as i:
                        for p in range(2):
                            sp.wait_ge(normed_ready, i * 2 + p + 1)
                            net.go_on(sp)
                            sp.dma_start(rows[:, ds((i * 2 + p) * TB, TB), :], normed[p][:, :, :]
                                         ).then_inc(stored[p], 16)
                    for p in range(2):
                        sp.wait_ge(stored[p], 16 * B // 2)


def project_qkv(net, layer, scratch, values, gates):
    nc = net.nc
    rotary = layer == 3
    tag = f"L{layer}_qkv"
    regions = ((slice(0, P), slice(0, 2)), (slice(0, NKV * HD), slice(2, 3)))
    with ExitStack() as ctx:
        sb = lambda name, shape, dt=F32: net.sb(f"{tag}_{name}", shape, dt, ctx)
        sem = lambda name: net.sem(f"{tag}_{name}")
        w = sb("w", [P, KC, 3 * P + 32])
        w_plain = None if rotary else sb("w_plain", [P, KC, 3 * P])
        full = [sb(f"full{p}", [P, 3, S]) for p in range(2)]
        parts = [sb(f"parts{p}", [P, 3, 3, S], BF16) for p in range(2)]
        rest = sb("rest", [P, 3, S])
        proj = net.ps(f"{tag}_proj", [P, 3, S], F32, ctx)
        small = net.ps(f"{tag}_small", [P, TB, P], F32, ctx)
        w_loaded = sem("w_loaded")
        w_turned, w_ready = sem("w_turned"), sem("w_ready")
        projected = sem("projected")
        copied = sem("copied")
        turned_ready = sem("turned_ready")
        values_ready = sem("values_ready")
        hi_ready = sem("hi_ready")
        mid_ready = sem("mid_ready")
        rest_ready = sem("rest_ready")
        lo_ready = sem("lo_ready")
        written = [sem(f"written{p}") for p in range(2)]
        if rotary:
            w_in = sb("w_in", [P, 3, C])
            wg_in = sb("wg_in", [32, C])
            rope = sb("rope", [P, 4, S])
            swap = sb("swap", [P, 2, P])
            cosd = sb("cosd", [P, 3, S])
            sind = sb("sind", [P, 3, S])
            rot = [sb(f"rot{p}", [P, 3, S]) for p in range(2)]
            gate_row = [sb(f"gate_row{p}", [32, S]) for p in range(2)]
            gate_e = sb("gate_e", [P, TB, 32])
            gate_s = sb("gate_s", [P, TB, 32])
            swapped = net.ps(f"{tag}_swapped", [P, 3, S], F32, ctx)
            gate_ps = net.ps(f"{tag}_gate", [32, S], F32, ctx)
            swapped_ready = sem("swapped_ready")
            cos_ready = sem("cos_ready")
            sin_ready = sem("sin_ready")
            rot_ready = sem("rot_ready")
            gate_exp = sem("gate_exp")
            gate_step = sem("gate_step")
            gates_done = sem("gates_done")
        source = rot if rotary else full
        source_ready = rot_ready if rotary else copied

        with nc.Block() as block:
            @block.sync
            def _(sp):
                if not rotary:
                    sp.dma_start(w_plain[:, :, :], net.dram["L2_attn_W_qkv"].rearrange("(k p) n -> p k n", p=P)
                                 ).then_inc(w_loaded, 16)
                else:
                    sp.dma_start(w_in[:, 0:2, :], net.dram["L3_attn_Wq"].rearrange("(j p) c -> p j c", p=P)
                                 ).then_inc(w_loaded, 16)
                    sp.dma_start(w_in[0:64, 2, :], net.dram["L3_attn_Wk"]).then_inc(w_loaded, 16)
                    sp.dma_start(w_in[64:128, 2, :], net.dram["L3_attn_Wv"]).then_inc(w_loaded, 16)
                    sp.dma_start(wg_in[0:16, :], net.dram["L3_attn_Wg_slc"]).then_inc(w_loaded, 16)
                    sp.dma_start(wg_in[16:32, :], net.dram["L3_attn_Wg_swa"]).then_inc(w_loaded, 16)
                    sp.dma_start(rope[:, :, :], net.dram["c_rope"]).then_inc(w_loaded, 16)
                    sp.dma_start(swap[:, :, :], net.dram["c_swap"]).then_inc(w_loaded, 16)
                with sp.Fori(0, B // 2) as i:
                    for p in range(2):
                        b = i * 2 + p
                        sp.wait_ge(lo_ready, b + 1)
                        sp.wait_ge(mid_ready, b + 1)
                        net.go_on(sp)
                        for c in range(2):
                            for g in range(2):
                                sp.dma_start(scratch["q"][ds(b * NKV + 2 * c + g, 1), :, :].rearrange(
                                    "u (a r) t -> r (u a) t", a=3), parts[p][64 * g:64 * g + 64, c, :, :]
                                    ).then_inc(written[p], 16)
                        sp.dma_start(scratch["k"][:, ds(b * NKV * HD, NKV * HD), :].rearrange("a r t -> r a t"),
                                     parts[p][0:64, 2, :, :]).then_inc(written[p], 16)
                for p in range(2):
                    sp.wait_ge(written[p], 5 * 16 * B // 2)

            @block.tensor
            def _(pe):
                if rotary:
                    pe.wait_ge(w_loaded, 7 * 16)
                    for k in range(KC):
                        for j in range(3):
                            pe.transpose(swapped[:, k, j * P:(j + 1) * P], w_in[:, j, k * P:(k + 1) * P],
                                         net.ident[:, :])
                        last = pe.transpose(swapped[:, k, 3 * P:3 * P + 32], wg_in[:, k * P:(k + 1) * P],
                                            net.ident[0:32, 0:32])
                    last.then_inc(w_turned, 1)
                pe.wait_ge(w_ready, 1)

                def project(b, first):
                    if not first:
                        pe.wait_ge(copied, b)
                    for j in range(3):
                        for k in range(KC):
                            last = pe.matmul(proj[:, j, :], w[:, k, j * P:(j + 1) * P], net.xT[:, k, ds(b * S, S)],
                                             start=k == 0, stop=k == KC - 1)
                    if rotary:
                        for k in range(KC):
                            last = pe.matmul(gate_ps[:, :], w[:, k, 3 * P:3 * P + 32], net.xT[:, k, ds(b * S, S)],
                                             start=k == 0, stop=k == KC - 1)
                    last.then_inc(projected, 1)

                def turn(b, p, first):
                    pe.wait_ge(copied, b + 1)
                    if not first:
                        pe.wait_ge(values_ready, b)
                        if rotary:
                            pe.wait_ge(gate_exp, b)
                    for t in range(TB):
                        last = pe.transpose(small[:, t, :], full[p][:, 2, t * P:(t + 1) * P], net.ident[:, :])
                        if rotary:
                            last = pe.transpose(small[:, t, 0:32], gate_row[p][:, t * P:(t + 1) * P],
                                                net.ident[0:32, 0:32])
                    last.then_inc(turned_ready, 1)
                    if rotary:
                        if not first:
                            pe.wait_ge(sin_ready, b)
                        for j in range(3):
                            last = pe.matmul(swapped[:, j, :], swap[:, j // 2, :], full[p][:, j, :], start=True, stop=True)
                        last.then_inc(swapped_ready, 1)
                project(0, True)
                project(1, False)
                turn(0, 0, True)
                with pe.Fori(1, B // 2) as i:
                    for p in range(2):
                        project(i * 2 + p, False)
                        turn(i * 2 + p - 1, 1 - p, False)
                turn(B - 1, 1, False)

            @block.scalar
            def _(act):
                def copy(b, p, first):
                    act.wait_ge(projected, b + 1)
                    if not first:
                        act.wait_ge(turned_ready, b - 1)
                        if rotary:
                            act.wait_ge(swapped_ready, b - 1)
                            act.wait_ge(cos_ready, b - 1)
                        else:
                            act.wait_ge(rest_ready, b - 1)
                    if rotary:
                        act.activation(gate_row[p][:, :], gate_ps[:, :], ACT.Copy)
                    act.activation(full[p][:, :, :], proj[:, :, :], ACT.Copy).then_inc(copied, 1)

                def split(b, p, first, early):
                    act.wait_ge(source_ready, b + 1)
                    if not early:
                        act.wait_ge(written[p], (b - p) * 40)
                    for rows, chunks in regions:
                        last = act.activation(parts[p][rows, chunks, 0, :], source[p][rows, chunks, :], ACT.Copy)
                    last.then_inc(hi_ready, 1)
                    act.wait_ge(rest_ready, b + 1)
                    for rows, chunks in regions:
                        last = act.activation(parts[p][rows, chunks, 1, :], rest[rows, chunks, :], ACT.Copy)
                    last.then_inc(mid_ready, 1)
                    if rotary:
                        act.wait_ge(values_ready, b + 1)
                        if not first:
                            act.wait_ge(gates_done, b)
                        act.activation(gate_e[:, :, :], small[:, :, 0:32], ACT.Exp, scale=-1.0).then_inc(gate_exp, 1)
                copy(0, 0, True)
                copy(1, 1, True)
                split(0, 0, True, True)
                copy(2, 0, False)
                split(1, 1, False, True)
                copy(3, 1, False)
                with act.Fori(1, B // 2 - 1) as i:
                    for p in range(2):
                        split(i * 2 + p, p, False, False)
                        copy(i * 2 + p + 2, p, False)
                split(B - 2, 0, False, False)
                split(B - 1, 1, False, False)

            @block.vector
            def _(dve):
                if rotary:
                    dve.wait_ge(w_turned, 1)
                    plain, end = swapped, 3 * P + 32
                else:
                    dve.wait_ge(w_loaded, 16)
                    plain, end = w_plain, 3 * P
                for k in range(KC):
                    dve.tensor_copy(w[:, k, 0:2 * P].rearrange("p (g d h) -> p g d h", g=NKV, h=GR),
                                    plain[:, k, 0:2 * P].rearrange("p (g h d) -> p g d h", g=NKV, h=GR))
                dve.tensor_copy(w[:, :, 2 * P:end], plain[:, 0:KC, 2 * P:end]).then_inc(w_ready, 1)

                def per_element(b, p, first):
                    if rotary:
                        dve.wait_ge(swapped_ready, b + 1)
                        if not first:
                            dve.wait_ge(rot_ready, b)
                        sin_q = rope[:, 1:2, :].to_broadcast([P, 2, S])
                        dve.tensor_tensor(sind[:, 0:2, :], swapped[:, 0:2, :], sin_q, ALU.mult)
                        dve.tensor_tensor(sind[0:64, 2, :], swapped[0:64, 2, :], rope[0:64, 3, :],
                                          ALU.mult).then_inc(sin_ready, 1)
                    dve.wait_ge(hi_ready, b + 1)
                    if not first:
                        dve.wait_ge(lo_ready, b)
                        dve.wait_ge(mid_ready, b)
                    for rows, chunks in regions:
                        last = dve.tensor_tensor(rest[rows, chunks, :], source[p][rows, chunks, :],
                                                 parts[p][rows, chunks, 0, :], ALU.subtract)
                    last.then_inc(rest_ready, 1)
                    dve.wait_ge(turned_ready, b + 1)
                    dve.tensor_copy(values[:, ds(b * NKV, NKV), :, :],
                                    small[:, :, 64:128].rearrange("p t (g d) -> p g t d", g=NKV)
                                    ).then_inc(values_ready, 1)
                    dve.wait_ge(mid_ready, b + 1)
                    for rows, chunks in regions:
                        last = dve.tensor_tensor(parts[p][rows, chunks, 2, :], rest[rows, chunks, :],
                                                 parts[p][rows, chunks, 1, :], ALU.subtract)
                    last.then_inc(lo_ready, 1)
                    if rotary:
                        dve.wait_ge(gate_exp, b + 1)
                        s = Order(dve, gate_step, b * 2)
                        s.did(dve.tensor_scalar(gate_s[:, :, :], gate_e[:, :, :], 1.0, None, ALU.add))
                        s.wait()
                        s.did(dve.reciprocal(gate_s[:, :, :], gate_s[:, :, :]))
                        s.wait()
                        dve.tensor_tensor(gates[:, ds(b * NKV, NKV), :, :],
                                          gate_s[:, :, 0:16].rearrange("p t (g h) -> p g t h", g=NKV),
                                          gate_s[:, :, 16:32].rearrange("p t (g h) -> p g t h", g=NKV),
                                          ALU.add).then_inc(gates_done, 1)
                per_element(0, 0, True)
                per_element(1, 1, False)
                with dve.Fori(1, B // 2) as i:
                    for p in range(2):
                        per_element(i * 2 + p, p, False)

            if rotary:
                @block.gpsimd
                def _(pool):
                    def turn_positions(b, p, first, early):
                        pool.wait_ge(copied, b + 1)
                        if not first:
                            pool.wait_ge(rot_ready, b)
                        pool.tensor_tensor(cosd[:, 0:2, :], full[p][:, 0:2, :],
                                           rope[:, 0:1, :].to_broadcast([P, 2, S]), ALU.mult)
                        pool.tensor_tensor(cosd[0:64, 2, :], full[p][0:64, 2, :], rope[0:64, 2, :],
                                           ALU.mult).then_inc(cos_ready, 1)
                        pool.wait_ge(cos_ready, b + 1)
                        pool.wait_ge(sin_ready, b + 1)
                        if not early:
                            pool.wait_ge(rest_ready, b - 1)
                        pool.tensor_tensor(rot[p][:, 0:2, :], cosd[:, 0:2, :], sind[:, 0:2, :], ALU.add)
                        pool.tensor_tensor(rot[p][0:64, 2, :], cosd[0:64, 2, :], sind[0:64, 2, :],
                                           ALU.add).then_inc(rot_ready, 1)
                    pool.wait_ge(w_loaded, 7 * 16)
                    turn_positions(0, 0, True, True)
                    turn_positions(1, 1, False, True)
                    with pool.Fori(1, B // 2) as i:
                        for p in range(2):
                            turn_positions(i * 2 + p, p, False, False)


def attention(net, layer, scratch, values, gates, out):
    nc = net.nc
    tag = f"L{layer}_attn"
    U = B * NKV
    scale = float(HD) ** -0.5
    order = [("A", 0), ("B", 0), ("A", 1), ("B", 1), ("C", 0), ("A", 2), ("B", 2), ("A", 3), ("B", 3), ("C", 2)]
    place = {("A", r): r for r in range(GR)} | {("B", r): GR + r for r in range(GR)} | {("C", 0): 8, ("C", 2): 9}
    UN = len(order)
    TURN_AT, WEIGH_AT = 2, (3, 5, 7, 8)
    with ExitStack() as ctx:
        sb = lambda name, shape, dt=F32: net.sb(f"{tag}_{name}", shape, dt, ctx)
        sem = lambda name: net.sem(f"{tag}_{name}")
        q = [sb(f"q{j}", [P, GR, S], BF16) for j in range(4)]
        k = [sb(f"k{j}", [P, S], BF16) for j in range(4)]
        v = [sb(f"v{j}", [P, TB, 32]) for j in range(4)]
        probs = [sb(f"probs{j}", [P, UN, S]) for j in range(2)]
        ident16 = sb("ident16", [P, P], BF16)
        causal = sb("causal", [P, P])
        causal16 = sb("causal16", [P, P], BF16)
        top = [sb(f"top{j}", [P, GR, TB]) for j in range(2)]
        top_rows = [sb(f"top_rows{j}", [GR * TB, 2, P], BF16) for j in range(2)]
        oT = [sb(f"oT{j}", [P, S]) for j in range(2)]
        inv = sb("inv", [P, TB, GR])
        ps_m = net.ps(f"{tag}_ps_m", [P, 2, S], F32, ctx)
        ps_t = net.ps(f"{tag}_ps_t", [P, 2, S], F32, ctx)
        ps_v = net.ps(f"{tag}_ps_v", [P, 2, S], F32, ctx)
        ps_o = net.ps(f"{tag}_ps_o", [P, TB, P], F32, ctx)
        ps_top = net.ps(f"{tag}_ps_top", [P, S], F32, ctx)
        const_in = sem("const_in")
        const_ready = sem("const_ready")
        v_const = sem("v_const")
        loaded = [sem(f"loaded{j}") for j in range(4)]
        tops_in = [sem(f"tops_in{j}") for j in range(4)]
        m_scored = sem("m_scored")
        m_reduced = sem("m_reduced")
        top_turned = sem("top_turned")
        top_hi = sem("top_hi")
        top_ready = sem("top_ready")
        t_scored = sem("t_scored")
        exped = sem("exped")
        v_ready = sem("v_ready")
        probs_ready = sem("probs_ready")
        pv_done = sem("pv_done")
        oT_ready = sem("oT_ready")
        o_turned = sem("o_turned")
        inv_step = sem("inv_step")
        o_done = sem("o_done")

        with nc.Block() as block:
            @block.sync
            def _(sp):
                sp.dma_start(causal[:, :], net.dram["c_causal"]).then_inc(const_in, 16)

                def load(u, j):
                    for at, n in ((0, 3), (3, 2), (5, 1)):
                        sp.dma_start(q[j][at * HD:(at + n) * HD, :, :],
                                     scratch["q"][ds(u, 1), 0:n * HD * GR, :].rearrange("u (p h) t -> (u p) h t", h=GR)
                                     ).then_inc(loaded[j], 16)
                    for part, at, n in ((0, 0, 3), (1, 3, 2), (2, 5, 1)):
                        sp.dma_start(k[j][at * HD:(at + n) * HD, :],
                                     scratch["k"][part:part + 1, ds(u * HD, HD), :].broadcast_to([n, HD, S])
                                     ).then_inc(loaded[j], 16)

                def put_tops(u, j, first):
                    sp.wait_ge(top_ready, u + 1)
                    net.go_on(sp)
                    if not first:
                        sp.wait_ge(t_scored, (u - 3) * UN)
                    for a in range(2):
                        sp.dma_start(q[j][6 * HD + a:6 * HD + a + 1, :, :], top_rows[j % 2][:, a, :]
                                     ).then_inc(tops_in[j], 16)

                def unit(u, j, more=True):
                    if more:
                        sp.wait_ge(t_scored, u * UN)
                        net.go_on(sp)
                        load(u + 3, (j + 3) % 4)
                    put_tops(u + 1, (j + 1) % 4, False)
                for j in range(4):
                    load(j, j)
                for u in range(2):
                    put_tops(u, u, True)
                for u in range(1, 5):
                    sp.wait_ge(t_scored, u * UN)
                    load(u + 3, (u + 3) % 4)
                    put_tops(u + 1, (u + 1) % 4, u < 3)
                with sp.Fori(1, U // 4 - 1) as i:
                    for j in range(1, 5):
                        unit(i * 4 + j, j % 4)
                unit(U - 3, 1, False)
                unit(U - 2, 2, False)

            @block.gpsimd
            def _(pool):
                pool.wait_ge(v_const, 12)

                def keep_causal(block, columns):
                    return pool.affine_select(out=block, in_=block, compare_op=ALU.is_ge, fill=0.0, base=0,
                                              pattern=columns, channel_multiplier=-1)

                def unit(u, j, first):
                    if not first:
                        pool.wait_ge(pv_done, u - 3)
                    pool.tensor_copy(v[j][:, :, 0:HD], values[:, ds(u, 1), :, :]).then_inc(v_ready, 1)
                    pool.wait_ge(exped, u * UN + UN)
                    net.go_on(pool)
                    pr = probs[j % 2]
                    keep_causal(pr[:, 0:GR, 0:P], [[0, GR], [1, P]])
                    keep_causal(pr[:, GR:2 * GR, 0:P], [[0, GR], [1, P]])
                    keep_causal(pr[:, GR:2 * GR, 3 * P:4 * P], [[0, GR], [1, P]])
                    keep_causal(pr[:, 8:10, :].rearrange("p c (r q) -> p (c r) q", r=2)[:, :, 0:P],
                                [[0, GR], [1, P]]).then_inc(probs_ready, 1)
                for u in range(4):
                    unit(u, u, True)
                with pool.Fori(1, U // 4) as i:
                    for j in range(4):
                        unit(i * 4 + j, j, False)

            @block.tensor
            def _(pe):
                pe.wait_ge(const_ready, 2)
                pe.wait_ge(v_const, 12)

                def max_unit(u, j, n, first):
                    kind, r = order[n]
                    if n == 0:
                        pe.wait_ge(loaded[j], (u - j) * 24 + 96)
                    if not (first and n < 2):
                        pe.wait_ge(m_reduced, u * UN + n - 1)
                    bank = ps_m[:, n % 2, :]
                    pieces = {"A": [(r, 3, 0)], "B": [(r, 2, 0), (r, 0, 3 * P)], "C": [(r, 1, 0), (r + 1, 1, 2 * P)]}
                    for head, qb, at in pieces[kind]:
                        width = (qb + 1) * P
                        pe.matmul(bank[:, at:at + width], q[j][0:96, head, qb * P:(qb + 1) * P], k[j][0:96, 0:width],
                                  start=True, stop=False)
                        last = pe.matmul(bank[:, at + width - P:at + width], ident16[:, :], causal16[:, :],
                                         start=False, stop=True)
                    last.then_inc(m_scored, 1)

                def exp_unit(u, j, n, first):
                    kind, r = order[n]
                    if n == 0:
                        pe.wait_ge(tops_in[j], (u - j) * 8 + 32)
                    if not (first and n < 2):
                        pe.wait_ge(exped, u * UN + n - 1)
                    bank = ps_t[:, n % 2, :]
                    pieces = {"A": [(r, 0, 0)], "B": [(r, 1, 0), (r, 3, 3 * P)], "C": [(r, 2, 0), (r + 1, 2, 2 * P)]}
                    for head, kb, at in pieces[kind]:
                        width = (TB - kb) * P
                        last = pe.matmul(bank[:, at:at + width], k[j][0:98, kb * P:(kb + 1) * P],
                                         q[j][0:98, head, kb * P:S], start=True, stop=True)
                    last.then_inc(t_scored, 1)

                def turn_tops(u, j):
                    pe.wait_ge(m_reduced, u * UN + UN)
                    pe.transpose(ps_top[0:GR * TB, 0:P], top[j % 2][:, :, :].rearrange("p h t -> p (h t)"),
                                 net.ident[:, :]).then_inc(top_turned, 1)

                def weigh_values(u, j, kb, first):
                    if kb == 0:
                        pe.wait_ge(probs_ready, u + 1)
                        pe.wait_ge(v_ready, u + 1)
                        if not first:
                            pe.wait_ge(oT_ready, u - 1)
                    pr = probs[j % 2]
                    for r in range(GR):
                        src = {0: pr[:, r, :], 1: pr[:, GR + r, 0:3 * P],
                               2: pr[:, 8 + r // 2, (r % 2) * 2 * P:(r % 2 + 1) * 2 * P],
                               3: pr[:, GR + r, 3 * P:4 * P]}[kb]
                        last = pe.matmul(ps_v[32 * r:32 * r + 32, j % 2, kb * P:S], v[j][:, kb, :], src,
                                         start=kb == 0, stop=kb == TB - 1, tile_position=(0, 32 * r))
                    if kb == TB - 1:
                        last.then_inc(pv_done, 1)

                def turn_out(u, j, first):
                    pe.wait_ge(oT_ready, u + 1)
                    if not first:
                        pe.wait_ge(o_done, u)
                    for t in range(TB):
                        last = pe.transpose(ps_o[:, t, :], oT[j % 2][:, t * P:(t + 1) * P], net.ident[:, :])
                    last.then_inc(o_turned, 1)

                def unit(u, j, maxima=True, tops=True, weigh=True, turn=True, first=False, first_turn=False, first_weigh=False):
                    for n in range(UN):
                        if maxima:
                            max_unit(u + 2, (j + 2) % 4, n, False)
                        exp_unit(u, j, n, first)
                        if n == 0 and tops:
                            turn_tops(u + 1, (j + 1) % 4)
                        if n == TURN_AT and turn:
                            turn_out(u - 2, (j + 2) % 4, first_turn)
                        if n in WEIGH_AT and weigh:
                            weigh_values(u - 1, (j + 3) % 4, WEIGH_AT.index(n), first_weigh)
                for u in range(2):
                    for n in range(UN):
                        max_unit(u, u, n, u == 0)
                    if u == 0:
                        turn_tops(0, 0)
                unit(0, 0, weigh=False, turn=False, first=True)
                unit(1, 1, turn=False, first_weigh=True)
                unit(2, 2, first_turn=True, first_weigh=True)
                unit(3, 3)
                unit(4, 0)
                with pe.Fori(1, U // 4 - 1) as i:
                    for j in range(1, 5):
                        unit(i * 4 + j, j % 4)
                unit(U - 3, 1)
                unit(U - 2, 2, maxima=False)
                unit(U - 1, 3, maxima=False, tops=False)
                turn_out(U - 2, 2, False)
                for kb in range(TB):
                    weigh_values(U - 1, 3, kb, False)
                turn_out(U - 1, 3, False)

            @block.scalar
            def _(act):
                def exponentials(u, j, first, mid=None):
                    if not first:
                        act.wait_ge(pv_done, u - 1)
                    for n, unit in enumerate(order):
                        act.wait_ge(t_scored, u * UN + n + 1)
                        act.activation(probs[j % 2][:, place[unit], :], ps_t[:, n % 2, :], ACT.Exp,
                                       scale=scale).then_inc(exped, 1)

                def copy_out(u, j, first):
                    act.wait_ge(pv_done, u + 1)
                    if not first:
                        act.wait_ge(o_turned, u - 1)
                    act.activation(oT[j % 2][:, :], ps_v[:, j % 2, :], ACT.Copy).then_inc(oT_ready, 1)
                exponentials(0, 0, True)
                exponentials(1, 1, True)
                copy_out(0, 0, True)
                exponentials(2, 2, False)
                copy_out(1, 1, True)
                exponentials(3, 3, False)
                copy_out(2, 2, False)
                with act.Fori(1, U // 4) as i:
                    for j in range(4):
                        exponentials(i * 4 + j, j, False)
                        copy_out(i * 4 + j - 1, (j + 3) % 4, False)
                copy_out(U - 1, 3, False)

            @block.vector
            def _(dve):
                for j in range(4):
                    dve.memset(k[j][96:98, :], -1.0).then_inc(v_const, 1)
                    dve.memset(v[j][:, :, :], 0.0).then_inc(v_const, 1)
                dve.wait_ge(v_const, 8)
                for j in range(4):
                    dve.memset(v[j][:, :, HD:HD + 1], 1.0).then_inc(v_const, 1)
                dve.tensor_copy(ident16[:, :], net.ident[:, :]).then_inc(const_ready, 1)
                dve.wait_ge(const_in, 16)
                dve.tensor_copy(causal16[:, :], causal[:, :]).then_inc(const_ready, 1)

                def reduce(u, j, n, first):
                    kind, r = order[n]
                    if n == 0 and not first:
                        dve.wait_ge(top_turned, u - 1)
                    dve.wait_ge(m_scored, u * UN + n + 1)
                    bank, t = ps_m[:, n % 2, :], top[j % 2]
                    if kind == "A":
                        last = dve.tensor_reduce(t[:, r, 3:4], bank, AX.X, ALU.max)
                    elif kind == "B":
                        dve.tensor_reduce(t[:, r, 2:3], bank[:, 0:3 * P], AX.X, ALU.max)
                        last = dve.tensor_reduce(t[:, r, 0:1], bank[:, 3 * P:4 * P], AX.X, ALU.max)
                    else:
                        last = dve.tensor_reduce(t[:, r:r + 2, 1], bank.rearrange("p (h k) -> p h k", h=2),
                                                 AX.X, ALU.max)
                    last.then_inc(m_reduced, 1)

                def split_tops(u, j, first):
                    dve.wait_ge(top_turned, u + 1)
                    if not first:
                        dve.wait_ge(tops_in[(j + 2) % 4], (u - 2 - (j + 2) % 4) * 8 + 32)
                    rows, src = top_rows[j % 2], ps_top[0:GR * TB, 0:P]
                    dve.tensor_copy(rows[:, 0, :], src).then_inc(top_hi, 1)
                    dve.wait_ge(top_hi, u + 1)
                    dve.tensor_tensor(rows[:, 1, :], src, rows[:, 0, :], ALU.subtract).then_inc(top_ready, 1)

                def normalise(u, first):
                    dve.wait_ge(o_turned, u + 1)
                    heads = ps_o[:, :, :].rearrange("p t (h c) -> p t h c", h=GR)
                    n = 2 if layer == 3 else 1
                    if not first:
                        dve.wait_ge(o_done, u)
                    dve.reciprocal(inv[:, :, :], heads[:, :, :, HD]).then_inc(inv_step, 1)
                    dve.wait_ge(inv_step, u * n + 1)
                    if layer == 3:
                        dve.tensor_tensor(inv[:, :, :], inv[:, :, :], gates[:, ds(u, 1), :, :].rearrange(
                            "p u t h -> p (u t) h"), ALU.mult).then_inc(inv_step, 1)
                        dve.wait_ge(inv_step, u * n + 2)
                    dve.tensor_tensor(out[:, ds(u, 1), :, :].rearrange("p u t (h d) -> p (u t) h d", h=GR),
                                      heads[:, :, :, 0:HD],
                                      inv[:, :, :].unsqueeze(3).to_broadcast([P, TB, GR, HD]),
                                      ALU.mult).then_inc(o_done, 1)

                def unit(u, j, maxima=True, tops=True, turn=True, first_tops=False, first_norm=False):
                    for n in range(UN):
                        if maxima:
                            reduce(u + 2, (j + 2) % 4, n, False)
                        if n == 1 and tops:
                            split_tops(u + 1, (j + 1) % 4, first_tops)
                        if n == TURN_AT + 1 and turn:
                            normalise(u - 2, first_norm)
                for u in range(2):
                    for n in range(UN):
                        reduce(u, u, n, True)
                    if u == 0:
                        split_tops(0, 0, True)
                unit(0, 0, turn=False, first_tops=True)
                unit(1, 1, turn=False)
                unit(2, 2, first_norm=True)
                unit(3, 3)
                unit(4, 0)
                with dve.Fori(1, U // 4 - 1) as i:
                    for j in range(1, 5):
                        unit(i * 4 + j, j % 4)
                unit(U - 3, 1)
                unit(U - 2, 2, maxima=False)
                unit(U - 1, 3, maxima=False, tops=False)
                normalise(U - 2, False)
                normalise(U - 1, False)


def project_out(net, layer, heads):
    nc = net.nc
    tag = f"L{layer}_wo"
    with ExitStack() as ctx:
        sb = lambda name, shape, dt=F32: net.sb(f"{tag}_{name}", shape, dt, ctx)
        sem = lambda name: net.sem(f"{tag}_{name}")
        w_in = sb("w_in", [P, KC, C])
        w = sb("w", [P, KC, C]) if layer == 3 else w_in
        rows = [sb(f"rows{p}", [P, TB, C]) for p in range(2)]
        rowsT = [sb(f"rowsT{p}", [P, KC, S]) for p in range(2)]
        turned = net.ps(f"{tag}_turned", [P, KC, S], F32, ctx)
        w_ps = net.ps(f"{tag}_w_ps", [P, KC, C], F32, ctx)
        proj = [net.ps(f"{tag}_proj{p}", [P, TB, C], F32, ctx) for p in range(2)]
        w_loaded, w_turned, w_ready = sem("w_loaded"), sem("w_turned"), sem("w_ready")
        rows_ready = sem("rows_ready")
        turned_ready = sem("turned_ready")
        copied = sem("copied")
        projected = sem("projected")
        added = sem("added")
        with nc.Block() as block:
            @block.sync
            def _(sp):
                src = net.dram["L2_attn_W_o" if layer == 2 else "L3_attn_Wo"]
                sp.dma_start(w_in[:, :, :], src.rearrange("(k p) c -> p k c", p=P)).then_inc(w_loaded, 16)

            @block.tensor
            def _(pe):
                pe.wait_ge(w_loaded, 16)
                if layer == 3:
                    for k in range(KC):
                        for j in range(KC):
                            last = pe.transpose(w_ps[:, k, j * P:(j + 1) * P], w_in[:, j, k * P:(k + 1) * P],
                                                net.ident[:, :])
                    last.then_inc(w_turned, 1)
                    pe.wait_ge(w_ready, 1)

                def turn(b, p, first):
                    pe.wait_ge(rows_ready, b + 1)
                    if not first:
                        pe.wait_ge(copied, b)
                    for c in range(KC):
                        for t in range(TB):
                            last = pe.transpose(turned[:, c, t * P:(t + 1) * P], rows[p][:, t, c * P:(c + 1) * P],
                                                net.ident[:, :])
                    last.then_inc(turned_ready, 1)

                def project(b, p, first):
                    pe.wait_ge(copied, b + 1)
                    if not first:
                        pe.wait_ge(added, b - 1)
                    for t in range(TB):
                        for k in range(KC):
                            last = pe.matmul(proj[p][:, t, :], rowsT[p][:, k, t * P:(t + 1) * P], w[:, k, :],
                                             start=k == 0, stop=k == KC - 1)
                    last.then_inc(projected, 1)
                turn(0, 0, True)
                turn(1, 1, False)
                project(0, 0, True)
                turn(2, 0, False)
                project(1, 1, True)
                with pe.Fori(1, B // 2 - 1) as i:
                    for p in range(2):
                        turn(i * 2 + p + 1, 1 - p, False)
                        project(i * 2 + p, p, False)
                turn(B - 1, 1, False)
                project(B - 2, 0, False)
                project(B - 1, 1, False)

            @block.scalar
            def _(act):
                def gather(b, p, first):
                    if not first:
                        act.wait_ge(turned_ready, b - 1)
                    act.activation(rows[p][:, :, :].rearrange("p t (g c) -> p g t c", g=NKV),
                                   heads[:, ds(b * NKV, NKV), :, :], ACT.Copy).then_inc(rows_ready, 1)

                def copy(b, p, first):
                    act.wait_ge(turned_ready, b + 1)
                    if not first:
                        act.wait_ge(projected, b - 1)
                    act.activation(rowsT[p][:, :, :], turned[:, :, :], ACT.Copy).then_inc(copied, 1)
                gather(0, 0, True)
                gather(1, 1, True)
                copy(0, 0, True)
                copy(1, 1, True)
                with act.Fori(1, B // 2) as i:
                    for p in range(2):
                        gather(i * 2 + p, p, False)
                        copy(i * 2 + p, p, False)

            @block.vector
            def _(dve):
                if layer == 3:
                    dve.wait_ge(w_turned, 1)
                    dve.tensor_copy(w[:, :, :], w_ps[:, :, :]).then_inc(w_ready, 1)
                with dve.Fori(0, B // 2) as i:
                    for p in range(2):
                        b = i * 2 + p
                        dve.wait_ge(projected, b + 1)
                        x_b = net.x[:, ds(b * TB, TB), :]
                        dve.tensor_tensor(x_b, proj[p][:, :, :], x_b, ALU.add).then_inc(added, 1)


def attention_block(net, layer):
    with ExitStack() as ctx:
        values = net.sb(f"L{layer}_values", [P, B * NKV, TB, HD], F32, ctx)
        heads = net.sb(f"L{layer}_heads", [P, B * NKV, TB, GR * HD], F32, ctx)
        gates = net.sb(f"L{layer}_gates", [P, B * NKV, TB, GR], F32, ctx) if layer == 3 else None
        scratch = {"q": net.nc.dram_tensor(f"L{layer}_q_parts", (B * NKV, 3 * GR * HD, S), BF16).ap(),
                   "k": net.nc.dram_tensor(f"L{layer}_k_parts", (3, B * NKV * HD, S), BF16).ap()}
        with ExitStack() as early:
            net.hold_channels(f"L{layer}_attn", early)
            layer_norm(net, f"L{layer}_ln")
            project_qkv(net, layer, scratch, values, gates)
        attention(net, layer, scratch, values, gates, heads)
        project_out(net, layer, heads)


BITS = 31


class Tables:

    def __init__(self, net, tag, ctx):
        self.take = net.sb(f"{tag}_take", [P, SLOT_TILES], I32, ctx)
        self.give = net.sb(f"{tag}_give", [P, SLOT_TILES], I32, ctx)
        self.weight = net.sb(f"{tag}_weight", [P, SLOT_TILES], F32, ctx)
        self.expert = net.sb(f"{tag}_expert", [P, SLOT_TILES], I32, ctx)


def route(net, layer, tables, early_load=None, shared=None):
    nc = net.nc
    tag = f"L{layer}_route"
    with ExitStack() as ctx:
        sb = lambda name, shape, dt=F32: net.sb(f"{tag}_{name}", shape, dt, ctx)
        sem = lambda name: net.sem(f"{tag}_{name}")
        by_tile = [P, NT, E]
        by_expert = [P, E, NT]
        lefts, rights = sb("lefts", [P, 4, P]), sb("rights", [P, 4, 2, P])
        left = [[lefts[:, 2 * p + c, :] for c in range(2)] for p in range(2)]
        right = [[rights[:, 2 * p + c, :, :] for c in range(2)] for p in range(2)]
        w_in = lefts[0:E, 0:2, :].rearrange("e k c -> e (k c)")
        tile_cmp = rights[:, :, :, :].rearrange("p a b c -> p (a b c)")[:, 0:SLOT_TILES * E].rearrange(
            "p (t e) -> p t e", e=E)
        table_rows = right[0][0]
        w = sb("w", [P, KC, E])
        bias_col = sb("bias_col", [E, 1])
        bias_row = sb("bias_row", [P, E])
        if shared is None:
            z_row = [sb(f"z_row{p}", [E, S]) for p in range(2)]
        else:
            z_row = [shared.active[1][0:E, p, :] for p in range(2)]
        z, sig, key, first, second, chosen, tmp, weights = (
            sb(n, by_tile) for n in ("z", "sig", "key", "first", "second", "chosen", "tmp", "weights"))
        best, where_, total, slot, wslot, token1 = (
            sb("best", [P, NT]), sb("where", [P, NT]), sb("total", [P, NT]),
            sb("slot", [P, 2, NT]), sb("wslot", [P, 2, NT]), sb("token1", [P, NT]))
        slot_i, high_i, low_i = (sb(n, [P, 2, NT], I32) for n in ("slot_i", "high_i", "low_i"))
        high, low = sb("high", [P, 2, NT]), sb("low", [P, 2, NT])
        chosen16 = sb("chosen16", by_tile, BF16)
        before, before16 = sb("before", [P, P]), sb("before16", [P, P], BF16)
        ones16, ones = sb("ones16", [P, P], BF16), sb("ones", [P, NT])
        lane, expert_no, tile_start = sb("lane", [P, P]), sb("expert_no", [P, E]), sb("tile_start", [P, SLOT_TILES])
        less8 = sb("less8", [P, E])
        per_tile, upto, ranks = sb("per_tile", by_expert), sb("upto", by_expert), sb("ranks", by_expert)
        small = sb("small", [P, 8, E])
        padded_i = sb("padded_i", [P, E], I32)
        tile_exp = sb("tile_exp", [P, SLOT_TILES])
        table = sb("table", [P, 2, SLOT_TILES])
        empty = sb("empty", [P, SLOT_TILES])
        lane_col = sb("lane_col", [P, 1])
        if layer == 2:
            bits = sb("bits", [P, BITS, E], I32)
            floor_, candidate, gain = (sb(n, [P, E], I32) for n in ("floor", "candidate", "gain"))
            rated, over, level = (t[:, :, :].rearrange("p t e -> p (t e)").rearrange("p (e t) -> p e t", e=E)
                                  for t in (z, sig, key))
            level16 = sb("level16", by_expert, BF16)
            count16 = sb("count16", [P, E], BF16)
        ps_wide = net.ps(f"{tag}_ps_wide", [P, 2, S], F32, ctx)
        ps_out = net.ps(f"{tag}_ps_out", [P, 2, 2, S], F32, ctx)
        ps_count = net.ps(f"{tag}_ps_count", [P, S], F32, ctx)
        ps_tab = net.ps(f"{tag}_ps_tab", [P, S], F32, ctx)
        ps_z, ps_t = ps_wide, ps_out[:, :, 0, :]
        NP = NT * E
        if shared is not None:
            shared.banks(ps_wide, ps_out, ctx)
        loaded = sem("loaded")
        early_loaded = sem("early_loaded")
        w_turned, w_ready = sem("w_turned"), sem("w_ready")
        z_ready = sem("z_ready")
        z_copied = sem("z_copied")
        z_turned = sem("z_turned")
        z_in = sem("z_in")
        const_ready = sem("const_ready")
        exp_done = sem("exp_done")
        step = sem("step")
        loop_step = sem("loop_step")
        counts_asked, counted = sem("counts_asked"), sem("counted")
        level_asked, level_counted = sem("level_asked"), sem("level_counted")
        sides_ready = sem("sides_ready")
        sides_used = sem("sides_used")
        table_ready, table_copied, table_turned = sem("table_ready"), sem("table_copied"), sem("table_turned")
        dram = net.dram
        w_name = "L2_ffn_proj_w" if layer == 2 else "L3_ffn_gate_w"
        b_name = "L2_ffn_proj_b" if layer == 2 else "L3_ffn_gate_b"
        e_name = "L2_ffn_expert_bias" if layer == 2 else "L3_ffn_expert_biases"
        n_loaded = 7 + (1 if layer == 2 else 0)

        with nc.Block() as block:
            @block.sync
            def _(sp):
                if layer == 2:
                    sp.dma_start(w_in[:, :], dram[w_name]).then_inc(loaded, 16)
                    sp.dma_start(bits[:, :, :], dram["c_bits"]).then_inc(loaded, 16)
                else:
                    sp.dma_start(w[:, :, :], dram[w_name].rearrange("(k p) e -> p k e", p=P)).then_inc(loaded, 16)
                sp.dma_start(bias_col[:, :], dram[b_name].rearrange("(e a) -> e a", a=1)).then_inc(loaded, 16)
                sp.dma_start(bias_row[:, :], dram[e_name].partition_broadcast(P)).then_inc(loaded, 16)
                sp.dma_start(before[:, :], dram["c_before"]).then_inc(loaded, 16)
                sp.dma_start(expert_no[:, :], dram["c_expert"]).then_inc(loaded, 16)
                sp.dma_start(tile_start[:, :], dram["c_tilestart"]).then_inc(loaded, 16)
                sp.dma_start(lane[:, :], dram["c_lane"]).then_inc(loaded, 16)
                if early_load is not None:
                    to, source = early_load
                    for k in range(KC):
                        sp.dma_start(to[:, k], source[k]).then_inc(early_loaded, 16)
                if shared is not None:
                    shared.load(sp)
                if early_load is not None:
                    sp.wait_ge(early_loaded, KC * 16)

            @block.tensor
            def _(pe):
                pe.wait_ge(loaded, 16 * n_loaded)
                if layer == 2:
                    for k in range(KC):
                        last = pe.transpose(ps_count[:, k * E:(k + 1) * E], w_in[:, k * P:(k + 1) * P],
                                            net.ident[0:E, 0:E])
                    last.then_inc(w_turned, 1)
                    pe.wait_ge(w_ready, 1)

                def logits(b, p, first):
                    if not first:
                        pe.wait_ge(z_copied, b - 1)
                        net.go_on(pe)
                    for k in range(KC):
                        last = pe.matmul(ps_z[0:E, p, :], w[:, k, :], net.xT[:, k, ds(b * S, S)],
                                         start=k == 0, stop=k == KC - 1)
                    last.then_inc(z_ready, 1)

                def turn(b, p, first):
                    pe.wait_ge(z_copied, b + 1)
                    if not first:
                        pe.wait_ge(z_in, b - 1)
                    net.go_on(pe)
                    for t in range(TB):
                        last = pe.transpose(ps_t[:, p, t * E:(t + 1) * E], z_row[p][:, t * P:(t + 1) * P],
                                            net.ident[0:E, 0:E])
                    last.then_inc(z_turned, 1)
                logits(0, 0, True)
                logits(1, 1, True)
                turn(0, 0, True)
                logits(2, 0, False)
                turn(1, 1, True)
                with pe.Fori(1, B // 2 - 1) as i:
                    for p in range(2):
                        logits(i * 2 + p + 1, 1 - p, False)
                        turn(i * 2 + p, p, False)
                logits(B - 1, 1, False)
                turn(B - 2, 0, False)
                turn(B - 1, 1, False)

                def count_pairs():
                    pe.wait_ge(counts_asked, 1)
                    pairs = chosen16[:, :, :].rearrange("p t e -> p (t e)")
                    pe.matmul(ps_count[:, 0:NP], before16[:, :], pairs, start=True, stop=True)
                    pe.matmul(ps_count[:, NP:2 * NP], ones16[:, :], pairs, start=True, stop=True
                              ).then_inc(counted, 1)

                def count_over(i):
                    pe.wait_ge(level_asked, i + 1)
                    net.go_on(pe)
                    pe.matmul(ps_count[:, 0:E], ones16[:, :], count16[:, :], start=True, stop=True
                              ).then_inc(level_counted, 1)

                def count_level():
                    pe.wait_ge(level_asked, BITS + 2)
                    pairs = level16[:, :, :].rearrange("p e t -> p (e t)")
                    pe.matmul(ps_tab[:, 0:NP], before16[:, :], pairs, start=True, stop=True)
                    pe.matmul(ps_tab[:, NP:2 * NP], ones16[:, :], pairs, start=True, stop=True
                              ).then_inc(level_counted, 1)

                def place(t, p, first, last_one):
                    for c in range(2):
                        pe.wait_ge(sides_ready, t * 2 + c + 1)
                        pe.matmul(ps_tab[:, 0:2 * P], left[p][c], right[p][c],
                                  start=first and c == 0, stop=last_one and c == 1).then_inc(sides_used, 1)
                if shared is None:
                    count_pairs()
                    place(0, 0, True, False)
                    with pe.Fori(0, NT // 2 - 1) as i:
                        place(i * 2 + 1, 1, False, False)
                        place(i * 2 + 2, 0, False, False)
                    place(NT - 1, 1, False, True)
                else:
                    pe.wait_ge(z_in, B)
                    shared.turn_weights(pe)
                    count_pairs()
                    shared.up(pe, 0, 0, True)
                    shared.round(pe, 0, 0, True, lambda slot: count_over(slot))
                    shared.round(pe, 1, 1, True, lambda slot: count_over(8 + slot))
                    shared.round(pe, 2, 0, False, lambda slot: count_over(16 + slot))
                    shared.round(pe, 3, 1, False, lambda slot: count_over(24 + slot))
                    count_level()
                    for b in range(4, B - 1):
                        def place_one(slot):
                            t = (b - 4) * 8 + slot
                            place(t, t % 2, t == 0, False)
                        shared.round(pe, b, b % 2, False, place_one)

                    def place_two(slot):
                        for t in (24 + 2 * slot, 25 + 2 * slot):
                            place(t, t % 2, False, t == NT - 1)
                    shared.down(pe, B - 1, 1, False, place_two)
                pe.wait_ge(table_copied, 1)
                for j in range(2):
                    last = pe.transpose(ps_count[:, j * P:(j + 1) * P], table_rows[:, j, :], net.ident[:, :])
                last.then_inc(table_turned, 1)

            @block.scalar
            def _(act):
                act.wait_ge(loaded, 16 * n_loaded)

                def copy(b, p, first):
                    act.wait_ge(z_ready, b + 1)
                    if not first:
                        act.wait_ge(z_turned, b - 1)
                    act.activation(z_row[p][:, :], ps_z[0:E, p, :], ACT.Identity, bias=bias_col[:, 0:1]
                                   ).then_inc(z_copied, 1)
                copy(0, 0, True)
                copy(1, 1, True)
                with act.Fori(1, B // 2) as i:
                    for p in range(2):
                        copy(i * 2 + p, p, False)
                act.wait_ge(z_in, B)
                act.activation(sig[:, :, :], z[:, :, :], ACT.Exp, scale=-1.0).then_inc(exp_done, 1)
                if shared is not None:
                    shared.activate(act)

            if shared is not None:
                @block.gpsimd
                def _(pool):
                    shared.add(pool)

            @block.vector
            def _(dve):
                s = Order(dve, step)
                did, wait = s.did, s.wait
                if layer == 2:
                    dve.wait_ge(w_turned, 1)
                    dve.tensor_copy(w[:, :, :], ps_count[:, 0:KC * E].rearrange("p (k e) -> p k e", k=KC)
                                    ).then_inc(w_ready, 1)
                dve.wait_ge(loaded, 16 * n_loaded)
                did(dve.memset(ones[:, :], 1.0))
                did(dve.memset(ones16[:, :], 1.0))
                did(dve.tensor_copy(before16[:, :], before[:, :]))
                did(dve.tensor_scalar(less8[:, :], expert_no[:, :], float(-E), None, ALU.add))
                with dve.Fori(0, B // 2) as i:
                    for p in range(2):
                        b = i * 2 + p
                        dve.wait_ge(z_turned, b + 1)
                        dve.tensor_copy(z[:, ds(b * TB, TB), :], ps_t[:, p, 0:TB * E].rearrange(
                            "p (t e) -> p t e", e=E)).then_inc(z_in, 1)

                def over_experts(column):
                    return column.unsqueeze(2).to_broadcast(by_tile)

                def over_tiles(row):
                    return row.unsqueeze(1).to_broadcast(by_tile)

                def by_e(row):
                    return row.unsqueeze(2).to_broadcast(by_expert)

                did(dve.tensor_reduce(total[:, 0:1], before[:, :], AX.X, ALU.add))
                wait()
                did(dve.tensor_scalar(lane_col[:, :], total[:, 0:1], -1.0, float(P - 1), ALU.mult, ALU.add))
                dve.wait_ge(z_in, B)
                dve.wait_ge(exp_done, 1)
                did(dve.tensor_scalar(sig[:, :, :], sig[:, :, :], 1.0, None, ALU.add))
                wait()
                did(dve.reciprocal(sig[:, :, :], sig[:, :, :]))
                wait()
                if layer == 2:
                    did(dve.tensor_tensor(sig[:, :, :], sig[:, :, :], over_tiles(bias_row[:, :]), ALU.add))
                    wait()
                    did(dve.tensor_scalar(sig[:, :, :], sig[:, :, :], 1e-12, None, ALU.max))
                    wait()
                    did(dve.tensor_reduce(total[:, :], sig[:, :, :], AX.X, ALU.add))
                    wait()
                    did(dve.reciprocal(total[:, :], total[:, :]))
                    wait()
                    did(dve.tensor_tensor(sig[:, :, :], sig[:, :, :], over_experts(total[:, :]), ALU.mult))
                    wait()
                    did(dve.tensor_copy(key[:, :, :], sig[:, :, :]))
                else:
                    did(dve.tensor_tensor(key[:, :, :], z[:, :, :], over_tiles(bias_row[:, :]), ALU.add))
                for n, one_hot in enumerate((first, second)):
                    wait()
                    did(dve.tensor_reduce(best[:, :], key[:, :, :], AX.X, ALU.max))
                    wait()
                    did(dve.tensor_tensor(tmp[:, :, :], key[:, :, :], over_experts(best[:, :]), ALU.is_equal))
                    wait()
                    did(dve.tensor_tensor(tmp[:, :, :], tmp[:, :, :], over_tiles(less8[:, :]), ALU.mult))
                    wait()
                    did(dve.tensor_reduce(where_[:, :], tmp[:, :, :], AX.X, ALU.min))
                    wait()
                    did(dve.tensor_tensor(one_hot[:, :, :], over_tiles(less8[:, :]), over_experts(where_[:, :]),
                                          ALU.is_equal))
                    if n == 0:
                        wait()
                        did(dve.scalar_tensor_tensor(key[:, :, :], one_hot[:, :, :], -3e38, key[:, :, :],
                                                     ALU.mult, ALU.add))
                wait()
                did(dve.tensor_tensor(chosen[:, :, :], first[:, :, :], second[:, :, :], ALU.add))
                wait()
                dve.tensor_copy(chosen16[:, :, :], chosen[:, :, :]).then_inc(counts_asked, 1)
                did(dve.tensor_tensor(weights[:, :, :], sig[:, :, :], chosen[:, :, :], ALU.mult))
                wait()
                did(dve.tensor_reduce(total[:, :], weights[:, :, :], AX.X, ALU.add))
                wait()
                if layer == 2:
                    did(dve.tensor_scalar(total[:, :], total[:, :], 1e-12, None, ALU.max))
                    wait()
                did(dve.reciprocal(total[:, :], total[:, :]))
                wait()
                did(dve.tensor_tensor(weights[:, :, :], weights[:, :, :], over_experts(total[:, :]), ALU.mult))

                dve.wait_ge(counted, 1)
                did(dve.tensor_copy(per_tile[:, :, :], ps_count[:, NP:2 * NP].rearrange("p (t e) -> p e t", e=E)))
                wait()

                def running(out, per):
                    for e in range(E):
                        last = dve.tensor_tensor_scan(out[:, e, :], ones[:, :], per[:, e, :], 0.0, ALU.mult, ALU.add)
                        did(last)
                running(upto, per_tile)
                wait()
                did(dve.tensor_tensor(ranks[:, :, :], upto[:, :, :], per_tile[:, :, :], ALU.subtract))
                did(dve.tensor_scalar(small[:, 0, :], upto[:, :, NT - 1], float(P - 1), None, ALU.add))
                wait()
                did(dve.tensor_copy(padded_i[:, :], small[:, 0, :]))
                wait()
                did(dve.tensor_scalar(padded_i[:, :], padded_i[:, :], -P, None, ALU.bitwise_and))
                wait()
                did(dve.tensor_copy(small[:, 1, :], padded_i[:, :]))
                wait()
                did(dve.tensor_tensor_scan(small[:, 2, :], ones[:, 0:E], small[:, 1, :], 0.0, ALU.mult, ALU.add))
                wait()
                did(dve.tensor_tensor(small[:, 3, :], small[:, 2, :], small[:, 1, :], ALU.subtract))
                did(dve.tensor_tensor(tile_cmp[:, :, :], tile_start[:, :].unsqueeze(2).to_broadcast([P, SLOT_TILES, E]),
                                      small[:, 2, :].unsqueeze(1).to_broadcast([P, SLOT_TILES, E]), ALU.is_ge))
                wait()
                did(dve.tensor_tensor(ranks[:, :, :], ranks[:, :, :], by_e(small[:, 3, :]), ALU.add))
                did(dve.tensor_reduce(tile_exp[:, :], tile_cmp[:, :, :], AX.X, ALU.add))
                wait()
                did(dve.tensor_scalar(tile_exp[:, :], tile_exp[:, :], float(E - 1), None, ALU.min))
                did(dve.tensor_tensor(key[:, :, :], ps_count[:, 0:NP].rearrange("p (t e) -> p t e", e=E),
                                      ranks[:, :, :].rearrange("p e t -> p t e"), ALU.add))
                wait()
                did(dve.tensor_copy(tables.expert[:, :], tile_exp[:, :]))
                for c, one_hot in enumerate((first, second)):
                    wait()
                    did(dve.tensor_tensor(tmp[:, :, :], key[:, :, :], one_hot[:, :, :], ALU.mult))
                    wait()
                    did(dve.tensor_reduce(slot[:, c, :], tmp[:, :, :], AX.X, ALU.add))
                wait()
                did(dve.tensor_copy(slot_i[:, :, :], slot[:, :, :]))
                wait()
                did(dve.tensor_scalar(high_i[:, :, :], slot_i[:, :, :], 7, None, ALU.logical_shift_right))
                did(dve.tensor_scalar(low_i[:, :, :], slot_i[:, :, :], P - 1, None, ALU.bitwise_and))
                wait()
                did(dve.tensor_copy(high[:, :, :], high_i[:, :, :]))
                did(dve.tensor_copy(low[:, :, :], low_i[:, :, :]))

                if layer == 2:
                    did(dve.scalar_tensor_tensor(rated[:, :, :], chosen[:, :, :].rearrange("p t e -> p e t"), -1.0,
                                                 weights[:, :, :].rearrange("p t e -> p e t"), ALU.add, ALU.add))
                    did(dve.memset(floor_[:, :], 0))
                    wait()
                    STEPS = 5
                    with dve.Fori(0, BITS) as i:
                        o = Order(dve, loop_step, i * STEPS)
                        o.did(dve.tensor_tensor(candidate[:, :], floor_[:, :], bits[:, ds(i, 1), :], ALU.bitwise_or))
                        o.wait()
                        o.did(dve.tensor_tensor(over[:, :, :], rated[:, :, :], by_e(candidate[:, :].bitcast(F32)),
                                                ALU.is_ge))
                        o.wait()
                        with nc.allow_low_precision(reason="counts up to 32 are exact"):
                            dve.tensor_reduce(count16[:, :], over[:, :, :], AX.X, ALU.add).then_inc(level_asked, 1)
                        dve.wait_ge(level_counted, i + 1)
                        o.did(dve.tensor_scalar(small[:, 4, :], ps_count[:, 0:E], float(CAP), None, ALU.is_ge))
                        o.wait()
                        o.did(dve.tensor_tensor(gain[:, :], small[:, 4, :], bits[:, ds(i, 1), :], ALU.mult))
                        o.wait()
                        o.did(dve.tensor_tensor(floor_[:, :], floor_[:, :], gain[:, :], ALU.bitwise_or))
                        o.wait()
                        assert o.n == STEPS
                    floor_f = by_e(floor_[:, :].bitcast(F32))
                    did(dve.tensor_tensor(over[:, :, :], rated[:, :, :], floor_f, ALU.is_gt))
                    did(dve.tensor_tensor(level[:, :, :], rated[:, :, :], floor_f, ALU.is_equal))
                    wait()
                    with nc.allow_low_precision(reason="counts up to 32 are exact"):
                        dve.tensor_reduce(count16[:, :], over[:, :, :], AX.X, ALU.add).then_inc(level_asked, 1)
                    dve.tensor_copy(level16[:, :, :], level[:, :, :]).then_inc(level_asked, 1)
                    dve.wait_ge(level_counted, BITS + 1)
                    did(dve.tensor_scalar(small[:, 5, :], ps_count[:, 0:E], -1.0, float(CAP), ALU.mult, ALU.add))
                    dve.wait_ge(level_counted, BITS + 2)
                    did(dve.tensor_copy(per_tile[:, :, :], ps_tab[:, NP:2 * NP].rearrange("p (e t) -> p e t", e=E)))
                    wait()
                    running(upto, per_tile)
                    wait()
                    did(dve.tensor_tensor(upto[:, :, :], upto[:, :, :], per_tile[:, :, :], ALU.subtract))
                    wait()
                    did(dve.tensor_tensor(upto[:, :, :], upto[:, :, :], ps_tab[:, 0:NP].rearrange(
                        "p (e t) -> p e t", e=E), ALU.add))
                    wait()
                    did(dve.tensor_tensor(upto[:, :, :], upto[:, :, :], by_e(small[:, 5, :]), ALU.is_lt))
                    wait()
                    did(dve.tensor_tensor(level[:, :, :], level[:, :, :], upto[:, :, :], ALU.mult))
                    wait()
                    did(dve.tensor_tensor(over[:, :, :], over[:, :, :], level[:, :, :], ALU.add))
                    wait()
                    did(dve.tensor_tensor(weights[:, :, :], weights[:, :, :], over[:, :, :].rearrange(
                        "p e t -> p t e"), ALU.mult))
                for c, one_hot in enumerate((first, second)):
                    wait()
                    did(dve.tensor_tensor(tmp[:, :, :], weights[:, :, :], one_hot[:, :, :], ALU.mult))
                    wait()
                    did(dve.tensor_reduce(wslot[:, c, :], tmp[:, :, :], AX.X, ALU.add))
                wait()

                def sides(t, p, first_):
                    for c in range(2):
                        if not first_:
                            dve.wait_ge(sides_used, t * 2 + c - 3)
                        dve.tensor_scalar(left[p][c], lane[:, :], high[:, c, ds(t, 1)], None, ALU.is_equal)
                        dve.tensor_scalar(right[p][c][:, 0, :], lane[:, :], low[:, c, ds(t, 1)],
                                          token1[:, ds(t, 1)], ALU.is_equal, ALU.mult)
                        dve.tensor_scalar(right[p][c][:, 1, :], lane[:, :], low[:, c, ds(t, 1)],
                                          wslot[:, c, ds(t, 1)], ALU.is_equal, ALU.mult).then_inc(sides_ready, 1)
                did(dve.tensor_scalar(token1[:, :], upto[:, 0, :], 0.0, None, ALU.mult))
                wait()
                did(dve.tensor_tensor_scan(token1[:, :], ones[:, :], ones[:, :], -1.0, ALU.mult, ALU.add))
                wait()
                did(dve.tensor_scalar(token1[:, :], token1[:, :], float(P), lane_col[:, 0:1], ALU.mult, ALU.add))
                wait()
                did(dve.tensor_scalar(token1[:, :], token1[:, :], 1.0, None, ALU.add))
                wait()
                sides(0, 0, True)
                sides(1, 1, True)
                with dve.Fori(1, NT // 2) as i:
                    for p in range(2):
                        sides(i * 2 + p, p, False)
                dve.wait_ge(sides_used, 2 * NT)
                dve.tensor_copy(table_rows[:, :, :], ps_tab[:, 0:2 * P].rearrange("p (j l) -> p j l", j=2)
                                ).then_inc(table_copied, 1)
                dve.wait_ge(table_turned, 1)
                did(dve.tensor_copy(table[:, :, :], ps_count[:, 0:2 * P].rearrange("p (j t) -> p j t", j=2)[
                    :, :, 0:SLOT_TILES]))
                wait()
                did(dve.tensor_copy(tables.weight[:, :], table[:, 1, :]))
                did(dve.tensor_scalar(empty[:, :], table[:, 0, :], 0.0, None, ALU.is_equal))
                wait()
                did(dve.tensor_scalar(table[:, 1, :], table[:, 0, :], -1.0, 0.0, ALU.add, ALU.max))
                did(dve.tensor_scalar(tile_exp[:, :], empty[:, :], lane_col[:, 0:1], None, ALU.mult))
                wait()
                did(dve.tensor_copy(tables.take[:, :], table[:, 1, :]))
                did(dve.scalar_tensor_tensor(empty[:, :], empty[:, :], float(TOK), table[:, 1, :],
                                             ALU.mult, ALU.add))
                wait()
                did(dve.tensor_tensor(empty[:, :], empty[:, :], tile_exp[:, :], ALU.add))
                wait()
                did(dve.tensor_copy(tables.give[:, :], empty[:, :]))
                wait()


class SharedExpert:

    SH = 8

    def __init__(self, net, w1, w2, ctx):
        self.net = net
        sb = lambda name, shape: net.sb(f"L2_shared_{name}", shape, F32, ctx)
        sem = lambda name: net.sem(f"L2_shared_{name}")
        self.w1, self.w2 = w1, w2
        self.sh1 = sb("w1", [P, KC, self.SH * P])
        self.sh2 = sb("w2", [P, self.SH, C])
        self.b1 = sb("b1", [P, self.SH])
        self.b2 = sb("b2", [P, C])
        self.active = [sb(f"active{p}", [P, self.SH, S]) for p in range(2)]
        ring = [self.active[0][:, 2 * j:2 * j + 2, :] for j in range(4)]
        self.up_in = [ring[p].rearrange("p a (b c) -> p (a b) c", c=C) for p in range(2)]
        self.down_in = [ring[2 + p] for p in range(2)]
        self.b_in = sem("b_in")
        self.w_in = [sem(f"w_in{p}") for p in range(2)]
        self.turned = sem("turned")
        self.w_copied = sem("w_copied")
        self.hidden_ready = sem("hidden_ready")
        self.gelu_done = sem("gelu_done")
        self.out_ready = sem("out_ready")
        self.part = sb("part", [P, 2, S])
        self.out_copied = sem("out_copied")
        self.b_added = sem("b_added")
        self.added = sem("added")

    def banks(self, wide, out, ctx):
        self.hidden, self.out = wide, out

    def load(self, sp):
        dram, net = self.net.dram, self.net
        fc1 = dram["L2_ffn_fc1_w"].rearrange("e (j p) c -> e p j c", p=P)
        fc2 = dram["L2_ffn_fc2_w"].rearrange("e (k p) h -> e p k h", p=P)
        sh1 = dram["L2_ffn_sh1_w"].rearrange("(u j p) c -> u p j c", p=P, u=2)
        sh2 = dram["L2_ffn_sh2_w"].rearrange("(k p) (u h) -> u p k h", p=P, u=2)

        def load(p, up, down):
            sp.dma_start(self.up_in[p][:, :, :], up).then_inc(self.w_in[p], 16)
            sp.dma_start(self.down_in[p][:, :, :], down).then_inc(self.w_in[p], 16)
        for e in range(2):
            load(e, fc1[e], fc2[e])
        sp.dma_start(self.b2[:, :], dram["L2_ffn_sh2_b"].partition_broadcast(P)).then_inc(self.b_in, 16)
        with net.nc.allow_non_contiguous_dma(reason="bias columns"):
            sp.dma_start(self.b1[:, :], dram["L2_ffn_sh1_b"].rearrange("(j p) -> p j", p=P)
                         ).then_inc(self.b_in, 16)
        with sp.Fori(1, E // 2) as i:
            for p in range(2):
                e = i * 2 + p
                sp.wait_ge(self.turned, e * 2 - 2)
                net.go_on(sp)
                load(p, fc1[ds(e, 1)].rearrange("e p j c -> p (e j) c"),
                     fc2[ds(e, 1)].rearrange("e p k h -> p (e k) h"))
        for h in range(2):
            sp.wait_ge(self.turned, (E + h) * 2 - 2)
            load(h, sh1[h], sh2[h])

    def turn_weights(self, pe):
        ident = self.net.ident

        def turn(u, p, first, earliest):
            pe.wait_ge(self.w_in[p], (u - p) * 16 + 32)
            if not first:
                pe.wait_ge(self.w_copied, u * 2 - 3)
            for k in range(KC):
                for j in range(4):
                    last = pe.transpose(self.out[:, p, k, j * P:(j + 1) * P],
                                        self.up_in[p][:, j, k * P:(k + 1) * P], ident[:, :])
            last.then_inc(self.turned, 1)
            if not earliest:
                pe.wait_ge(self.w_copied, u * 2)
            for j in range(4):
                for k in range(KC):
                    at = (j % 2) * C + k * P
                    last = pe.transpose(self.hidden[:, j // 2, at:at + P],
                                        self.down_in[p][:, k, j * P:(j + 1) * P], ident[:, :])
            last.then_inc(self.turned, 1)
        turn(0, 0, True, True)
        turn(1, 1, True, False)
        with pe.Fori(1, E // 2 + 1) as i:
            for p in range(2):
                turn(i * 2 + p, p, False, False)
        pe.wait_ge(self.w_copied, (E + 2) * 2)

    def up(self, pe, b, p, first, between=None):
        for j in range(self.SH):
            if not (first and j < 2):
                pe.wait_ge(self.gelu_done, b * self.SH + j - 1)
            for k in range(KC):
                last = pe.matmul(self.hidden[:, j % 2, :], self.sh1[:, k, j * P:(j + 1) * P],
                                 self.net.xT[:, k, ds(b * S, S)], start=k == 0, stop=k == KC - 1)
            last.then_inc(self.hidden_ready, 1)
            if between is not None and j % 2 == 1:
                between(j // 2)

    def down(self, pe, b, p, first, between):
        pe.wait_ge(self.gelu_done, b * self.SH + self.SH)
        if not first:
            pe.wait_ge(self.out_copied, b - 1)
        for t in range(TB):
            for j in range(self.SH):
                last = pe.matmul(self.out[:, p, t // 2, (t % 2) * C:(t % 2 + 1) * C],
                                 self.active[p][:, j, t * P:(t + 1) * P], self.sh2[:, j, :],
                                 start=j == 0, stop=j == self.SH - 1)
            if t == TB - 1:
                last.then_inc(self.out_ready, 1)
            between(t)

    def round(self, pe, b, p, first, between):
        self.up(pe, b + 1, 1 - p, False, between)
        self.down(pe, b, p, first, lambda t: between(4 + t))

    def activate(self, act):
        def copy_weights(u, w1, w2, p):
            act.wait_ge(self.turned, u * 2 + 1)
            act.activation(w1, self.out[:, p, :, :], ACT.Copy).then_inc(self.w_copied, 1)
            act.wait_ge(self.turned, u * 2 + 2)
            act.activation(w2, self.hidden[:, :, :].rearrange("p b (j c) -> p (b j) c", c=C), ACT.Copy
                           ).then_inc(self.w_copied, 1)

        def gelus(b, p, first):
            if not first:
                act.wait_ge(self.out_ready, b - 1)
            for j in range(self.SH):
                act.wait_ge(self.hidden_ready, b * self.SH + j + 1)
                act.activation(self.active[p][:, j, :], self.hidden[:, j % 2, :], ACT.Gelu,
                               bias=self.b1[:, j:j + 1]).then_inc(self.gelu_done, 1)

        def copy_out(b, p, first):
            act.wait_ge(self.out_ready, b + 1)
            if not first:
                act.wait_ge(self.added, b)
            act.activation(self.part[:, :, :], self.out[:, p, :, :], ACT.Copy).then_inc(self.out_copied, 1)
        with act.Fori(0, E // 2) as i:
            for p in range(2):
                e = i * 2 + p
                copy_weights(e, self.w1[:, :, ds(e, 1), :].rearrange("p k e h -> p k (e h)"),
                             self.w2[:, ds(e, 1), :, :].rearrange("p e j c -> p (e j) c"), p)
        for h in range(2):
            copy_weights(E + h, self.sh1[:, :, h * 4 * P:(h + 1) * 4 * P], self.sh2[:, h * 4:(h + 1) * 4, :], h)
        act.wait_ge(self.b_in, 32)
        gelus(0, 0, True)
        gelus(1, 1, True)
        copy_out(0, 0, True)
        gelus(2, 0, False)
        with act.Fori(1, B // 2 - 1) as i:
            for p in range(2):
                copy_out(i * 2 + p - 1, 1 - p, False)
                gelus(i * 2 + p + 1, 1 - p, False)
        copy_out(B - 3, 1, False)
        gelus(B - 1, 1, False)
        copy_out(B - 2, 0, False)
        copy_out(B - 1, 1, False)

    def add(self, pool):
        pool.wait_ge(self.b_in, 32)
        with pool.Fori(0, B) as b:
            x_b = self.net.x[:, ds(b * TB, TB), :]
            pool.tensor_tensor(x_b, x_b, self.b2[:, :].unsqueeze(1).to_broadcast([P, TB, C]), ALU.add
                               ).then_inc(self.b_added, 1)
        pool.wait_ge(self.b_added, B)
        with pool.Fori(0, B // 2) as i:
            for p in range(2):
                b = i * 2 + p
                x_b = self.net.x[:, ds(b * TB, TB), :].rearrange("p (b t) c -> p b (t c)", b=2)
                pool.wait_ge(self.out_copied, b + 1)
                self.net.go_on(pool)
                pool.tensor_tensor(x_b, self.part[:, :, :], x_b, ALU.add).then_inc(self.added, 1)


def experts(net, layer, rows, total, w1, w2, tables):
    nc = net.nc
    tag = f"L{layer}_experts"
    FF = w1.shape[3]
    FC = FF // P
    FN = FF // 512
    func = ACT.Gelu if layer == 2 else ACT.Relu
    with ExitStack() as ctx:
        sb = lambda name, shape, dt=F32: net.sb(f"{tag}_{name}", shape, dt, ctx)
        sem = lambda name: net.sem(f"{tag}_{name}")
        token = [sb(f"token{j}", [P, C]) for j in range(4)]
        take = [sb(f"take{j}", [P, 1], I32) for j in range(4)]
        give = [sb(f"give{j}", [P, 1], I32) for j in range(2)]
        tokenT = [sb(f"tokenT{j}", [P, KC, P]) for j in range(2)]
        hidden = sb("hidden", [P, FF])
        hiddenT = sb("hiddenT", [P, FC, P])
        biased = [sb(f"biased{j}", [P, C]) for j in range(2)]
        result = [sb(f"result{j}", [P, C]) for j in range(2)]
        ps_x = net.ps(f"{tag}_ps_x", [P, KC, P], F32, ctx)
        ps_h = net.ps(f"{tag}_ps_h", [P, FN, 512], F32, ctx)
        ps_t = net.ps(f"{tag}_ps_t", [P, FC, P], F32, ctx)
        ps_y = [net.ps(f"{tag}_ps_y{j}", [P, 512], F32, ctx) for j in range(2)]
        take_ready = sem("take_ready")
        give_ready = sem("give_ready")
        zero = sb("zero", [P, C])
        zeroed = sem("zeroed")
        total_stored = sem("total_stored")
        w2_loaded = sem("w2_loaded")
        b1, b2 = sb("b1", [P, E, FC]), sb("b2", [P, E, C])
        b_in = sem("b_in")
        b_names = ("L2_ffn_fc1_b", "L2_ffn_fc2_b") if layer == 2 else ("L3_ffn_b1", "L3_ffn_b2")
        gathered = [sem(f"gathered{j}") for j in range(4)]
        added = [sem(f"added{j}") for j in range(2)]
        x_turned = sem("x_turned")
        x_copied = sem("x_copied")
        h_ready = sem("h_ready")
        h_copied = sem("h_copied")
        h_turned = sem("h_turned")
        f_done = sem("f_done")
        y_ready = sem("y_ready")
        biased_ready = sem("biased_ready")
        y_done = sem("y_done")
        NS = SLOT_TILES

        def expert_of(engine, i):
            return engine.value_load(tables.expert[0:1, ds(i, 1)], min_val=0, max_val=E - 1)

        with nc.Block() as block:
            @block.sync
            def _(sp):
                for e in range(E):
                    with nc.allow_non_contiguous_dma(reason="bias columns"):
                        sp.dma_start(b1[:, e, :], net.dram[b_names[0]][e].rearrange("(j p) -> p j", p=P)
                                     ).then_inc(b_in, 16)
                    sp.dma_start(b2[:, e, :], net.dram[b_names[1]][e].partition_broadcast(P)).then_inc(b_in, 16)
                if layer == 3:
                    for e in range(E):
                        sp.dma_start(w2[:, e, :, :], net.dram["L3_ffn_w2"][e].rearrange("(j p) c -> p j c", p=P)
                                     ).then_inc(w2_loaded, 16)
                sp.dma_start(total[0:TOK, :].rearrange("(u p) c -> p u c", p=P), net.x[:, :, :]
                             ).then_inc(total_stored, 16)
                sp.wait_ge(zeroed, 1)
                sp.dma_start(total[TOK:TOK + P, :], zero[:, :]).then_inc(total_stored, 16)
                sp.wait_ge(total_stored, 32)

            @block.gpsimd
            def _(pool):
                def gather(i, j, first):
                    if not first:
                        pool.wait_ge(x_turned, i - 3)
                        net.go_on(pool)
                    pool.tensor_copy(take[j][:, :], tables.take[:, ds(i, 1)]).then_inc(take_ready, 1)
                    pool.wait_ge(take_ready, i + 1)
                    net.go_on(pool)
                    pool.indirect_dma_start(out=token[j][:, :], out_offset=None, in_=rows,
                                            in_offset=bass.IndirectOffsetOnAxis(ap=take[j][:, 0:1], axis=0)
                                            ).then_inc(gathered[j], 16)

                def scatter(i, j, first):
                    pool.wait_ge(y_done, i + 1)
                    if not first:
                        pool.wait_ge(added[(j + 1) % 2], (i - 1 - (j + 1) % 2) * 8 + 16)
                    net.go_on(pool)
                    pool.tensor_copy(give[j % 2][:, :], tables.give[:, ds(i, 1)]).then_inc(give_ready, 1)
                    pool.wait_ge(give_ready, i + 1)
                    net.go_on(pool)
                    pool.indirect_dma_start(out=total, out_offset=bass.IndirectOffsetOnAxis(
                        ap=give[j % 2][:, 0:1], axis=0), in_=result[j % 2][:, :], in_offset=None,
                        compute_op=ALU.add).then_inc(added[j % 2], 16)
                for i in range(4):
                    gather(i, i, True)
                pool.wait_ge(total_stored, 32)
                scatter(0, 0, True)
                for i in range(1, 4):
                    gather(i + 3, (i + 3) % 4, False)
                    scatter(i, i, False)
                with pool.Fori(1, NS // 4 - 1) as r:
                    for j in range(4):
                        gather(r * 4 + j + 3, (j + 3) % 4, False)
                        scatter(r * 4 + j, j, False)
                gather(NS - 1, 3, False)
                for j in range(4):
                    scatter(NS - 4 + j, j, False)
                for j in range(2):
                    pool.wait_ge(added[j], NS // 2 * 16)

            @block.tensor
            def _(pe):
                def turn_x(i, j, first):
                    pe.wait_ge(gathered[j], (i - j) * 4 + 16)
                    if not first:
                        pe.wait_ge(x_copied, i)
                    for k in range(KC):
                        last = pe.transpose(ps_x[:, k, :], token[j][:, k * P:(k + 1) * P], net.ident[:, :])
                    last.then_inc(x_turned, 1)

                def up(i, j, first):
                    e = expert_of(pe, i)
                    pe.wait_ge(x_copied, i + 1)
                    if not first:
                        pe.wait_ge(h_copied, i)
                    for n in range(FN):
                        for k in range(KC):
                            last = pe.matmul(ps_h[:, n, :], tokenT[j % 2][:, k, :],
                                             w1[:, k, ds(e, 1), n * 512:(n + 1) * 512],
                                             start=k == 0, stop=k == KC - 1)
                    last.then_inc(h_ready, 1)

                def turn_h(i, first):
                    pe.wait_ge(h_copied, i + 1)
                    if not first:
                        pe.wait_ge(f_done, i)
                    for c in range(FC):
                        last = pe.transpose(ps_t[:, c, :], hidden[:, c * P:(c + 1) * P], net.ident[:, :])
                    last.then_inc(h_turned, 1)

                def down(i, j, first):
                    e = expert_of(pe, i)
                    pe.wait_ge(f_done, i + 1)
                    if not first:
                        pe.wait_ge(y_done, i - 1)
                    for c in range(FC):
                        last = pe.matmul(ps_y[j % 2][:, 0:C], hiddenT[:, c, :], w2[:, ds(e, 1), c, :],
                                         start=c == 0, stop=c == FC - 1)
                    last.then_inc(y_ready, 1)

                def tile(i, j, first=False, second=False, more=2):
                    turn_h(i, first)
                    if more >= 1:
                        up(i + 1, j + 1, False)
                    if more >= 2:
                        turn_x(i + 2, (j + 2) % 4, False)
                    down(i, j, first or second)
                turn_x(0, 0, True)
                turn_x(1, 1, False)
                up(0, 0, True)
                if layer == 3:
                    pe.wait_ge(w2_loaded, E * 16)
                for i in range(4):
                    tile(i, i, first=i == 0, second=i == 1)
                with pe.Fori(1, NS // 4 - 1) as r:
                    for j in range(4):
                        tile(r * 4 + j, j)
                for j in range(4):
                    tile(NS - 4 + j, j, more=3 - j)

            @block.scalar
            def _(act):
                def apply(i, first):
                    e = expert_of(act, i)
                    act.wait_ge(h_turned, i + 1)
                    if not first:
                        act.wait_ge(y_ready, i)
                    net.go_on(act)
                    for c in range(FC):
                        last = act.activation(hiddenT[:, c, :], ps_t[:, c, :], func, bias=b1[:, ds(e, 1), c])
                    last.then_inc(f_done, 1)
                act.wait_ge(b_in, 2 * E * 16)
                apply(0, True)
                with act.Fori(1, NS) as i:
                    apply(i, False)

            @block.vector
            def _(dve):
                def copy_x(i, j, first):
                    dve.wait_ge(x_turned, i + 1)
                    if not first:
                        dve.wait_ge(h_ready, i - 1)
                    dve.tensor_copy(tokenT[j % 2][:, :, :], ps_x[:, :, :]).then_inc(x_copied, 1)

                def copy_h(i, first):
                    dve.wait_ge(h_ready, i + 1)
                    if not first:
                        dve.wait_ge(h_turned, i)
                    dve.tensor_copy(hidden[:, :], ps_h[:, :, :].rearrange("p n f -> p (n f)")).then_inc(h_copied, 1)

                def weigh(i, j, first):
                    e = expert_of(dve, i)
                    dve.wait_ge(y_ready, i + 1)
                    dve.tensor_tensor(biased[j % 2][:, :], ps_y[j % 2][:, 0:C], b2[:, ds(e, 1), :], ALU.add
                                      ).then_inc(biased_ready, 1)
                    dve.wait_ge(biased_ready, i + 1)
                    if not first:
                        dve.wait_ge(added[j % 2], (i - j % 2) * 8)
                    dve.tensor_scalar(result[j % 2][:, :], biased[j % 2][:, :], tables.weight[:, ds(i, 1)], None,
                                      ALU.mult).then_inc(y_done, 1)

                def tile(i, j, first=False, more=2):
                    if more >= 1:
                        copy_h(i + 1, False)
                    if more >= 2:
                        copy_x(i + 2, j, False)
                    weigh(i, j, first)
                dve.memset(zero[:, :], 0.0).then_inc(zeroed, 1)
                copy_x(0, 0, True)
                copy_x(1, 1, True)
                copy_h(0, True)
                dve.wait_ge(b_in, 2 * E * 16)
                for i in range(2):
                    tile(i, i, first=True)
                with dve.Fori(1, NS // 2 - 1) as r:
                    for j in range(2):
                        tile(r * 2 + j, j)
                tile(NS - 2, 0, more=1)
                tile(NS - 1, 1, more=0)


def read_back(net, tag, total):
    loaded = net.sem(f"{tag}_read_back")
    with net.nc.Block() as block:
        @block.sync
        def _(sp):
            sp.dma_start(net.x[:, :, :], total[0:TOK, :].rearrange("(u p) c -> p u c", p=P)).then_inc(loaded, 16)
            sp.wait_ge(loaded, 16)


def ffn_block(net, layer, total):
    tag = f"L{layer}_moe"
    rows = net.nc.dram_tensor(f"{tag}_rows", (TOK, C), F32).ap()
    FF = 512 if layer == 2 else 1024
    FC = FF // P
    with ExitStack() as ctx:
        tables = Tables(net, tag, ctx)
        if layer == 2:
            w1 = net.sb(f"{tag}_w1", [P, KC, E, FF], F32, ctx)
            w2 = net.sb(f"{tag}_w2", [P, E, FC, C], F32, ctx)
        if layer == 3:
            w1 = net.sb(f"{tag}_w1", [P, KC, E, FF], F32, ctx)
        with ExitStack() as early:
            net.hold_channels(tag, early)
            layer_norm(net, f"{tag}_ln", rows)
            if layer == 2:
                route(net, layer, tables, shared=SharedExpert(net, w1, w2, early))
            else:
                w1_in = net.dram["L3_ffn_w1"].rearrange("e (k p) f -> k p e f", p=P)
                route(net, layer, tables, early_load=(w1, w1_in))
        if layer == 3:
            w2 = net.sb(f"{tag}_w2", [P, E, FC, C], F32, ctx)
        experts(net, layer, rows, total, w1, w2, tables)


def build(nc, dram, out):
    with ExitStack() as ctx:
        net = Net(nc, ctx, dram)
        conv_layers(net)
        net.clear_semaphores()
        attention_block(net, 2)
        net.clear_semaphores()
        total = nc.dram_tensor("L2_moe_total", (TOK + P, C), F32).ap()
        ffn_block(net, 2, total)
        read_back(net, "L2_moe", total)
        net.clear_semaphores()
        attention_block(net, 3)
        net.clear_semaphores()
        ffn_block(net, 3, out)


def kernel(**inputs):
    import concourse.bacc as _bacc
    from concourse.bass_utils import run_bass_kernel_spmd as _run

    nc = _bacc.Bacc("TRN2", target_bir_lowering=False, num_devices=1)
    arrays = {k: np.ascontiguousarray(v) for k, v in inputs.items()}
    arrays.update(host_constants())
    dram = {k: nc.dram_tensor(k, v.shape, mybir.dt.from_np(v.dtype), kind="ExternalInput").ap()
            for k, v in arrays.items()}
    out = nc.dram_tensor("out", (TOK + P, C), F32, kind="ExternalOutput").ap()
    build(nc, dram, out)
    nc.finalize()
    r = _run(nc, [arrays], core_ids=[0])
    return r.results[0]["out"][:TOK].reshape(B, T, N, C)
```

```python
from contextlib import ExitStack

import numpy as np

import concourse.bass as bass
from concourse import mybir

F32 = mybir.dt.float32
F32R = mybir.dt.float32r
BF16 = mybir.dt.bfloat16
I32 = mybir.dt.int32
U32 = mybir.dt.uint32
ALU = mybir.AluOpType
ACT = mybir.ActivationFunctionType
AX = mybir.AxisListType
ds = bass.ds

P = 128
B, T, N, C = 8, 16, 32, 256
LAT = C // 2
S = T * N
TOK = B * S
KC = C // P
NT = TOK // P
TB = S // P
NH, NKV, HD = 16, 4, 16
GR = NH // NKV
E = 8
CAP = 1280
SLOT_TILES = 2 * TOK // P + E
SLOTS = SLOT_TILES * P
BN_EPS = 1e-5
LN_EPS = 1e-5


def host_constants():
    tok = np.arange(S)
    same_time = tok[:, None] // N == tok[None, :] // N
    same_joint = tok[:, None] % N == tok[None, :] % N
    mix = (same_time / np.float32(N) + same_joint / np.float32(T)) / np.float32(T + N)
    mix = mix.astype(np.float32).reshape(TB, P, S).transpose(1, 0, 2)
    q, k = np.arange(P)[:, None], np.arange(P)[None, :]
    inv = np.float32(1.0) / np.float32(10000.0) ** (np.arange(0, HD, 2, dtype=np.float32) / np.float32(HD))
    freqs = np.arange(S, dtype=np.float32)[:, None] * inv.astype(np.float32)
    emb = np.concatenate([freqs, freqs], axis=-1)
    width_of = (np.arange(P) % (GR * HD) // GR, np.arange(P) % HD)
    step_of = (GR, 1)
    rope = np.stack([f(emb).T[w] for w in width_of for f in (np.cos, np.sin)], 1)
    swap = np.zeros((P, 2, P), np.float32)
    for j, (w, step) in enumerate(zip(width_of, step_of)):
        for r in range(P):
            if w[r] < HD // 2:
                swap[r + step * HD // 2, j, r] = -1.0
            else:
                swap[r - step * HD // 2, j, r] = 1.0
    return {
        "c_ident": np.eye(P, dtype=np.float32),
        "c_mix": np.ascontiguousarray(mix),
        "c_causal": np.where(k > q, np.float32(-1e30), np.float32(0)).astype(np.float32),
        "c_rope": np.ascontiguousarray(rope.astype(np.float32)),
        "c_swap": swap,
        "c_before": (q < k).astype(np.float32),
        "c_expert": np.ascontiguousarray(np.broadcast_to(np.arange(E, dtype=np.float32), (P, E))),
        "c_tilestart": np.ascontiguousarray(np.broadcast_to(
            np.arange(SLOT_TILES, dtype=np.float32) * P, (P, SLOT_TILES))),
        "c_bits": np.ascontiguousarray(np.broadcast_to(
            (1 << np.arange(30, -1, -1)).astype(np.int32)[:, None], (P, 31, E))),
        "c_lane": np.ascontiguousarray(np.broadcast_to(np.arange(P, dtype=np.float32), (P, P))),
    }


class Order:

    def __init__(self, engine, semaphore, base=0):
        self.engine, self.semaphore, self.base, self.n = engine, semaphore, base, 0

    def did(self, instruction):
        instruction.then_inc(self.semaphore, 1)
        self.n += 1
        return self.n

    def wait(self):
        self.engine.wait_ge(self.semaphore, self.base + self.n)


class Net:

    def __init__(self, nc, ctx, dram):
        self.nc, self.ctx, self.dram = nc, ctx, dram
        self.part, self.sems = 0, []
        self.going = self.sem("going0")
        self.ident = self.sb("ident", [P, P], F32)
        self.x = self.sb("x_tokens", [P, NT, C], F32)
        self.stats = self.sb("x_stats", [P, NT, 6], F32)
        self.xT = None

    def hold_channels(self, tag, ctx):
        self.xT = self.sb(f"{tag}_x_channels", [P, KC, TOK], F32, ctx)

    def go_on(self, engine):
        engine.sem_inc(self.going, 1)

    def sb(self, name, shape, dt, ctx=None):
        return (ctx or self.ctx).enter_context(self.nc.sbuf_tensor(name, shape, dt))

    def ps(self, name, shape, dt, ctx):
        return ctx.enter_context(self.nc.psum_tensor(name, shape, dt))

    def sem(self, name):
        semaphore = self.nc.alloc_semaphore(name=name)
        self.sems.append(semaphore)
        return semaphore

    def clear_semaphores(self):
        self.nc.clear_and_free_semaphores(self.sems)
        self.nc.all_engine_barrier()
        self.part += 1
        self.sems = []
        self.going = self.sem(f"going{self.part}")


def load_tokens(net):
    nc = net.nc
    with ExitStack() as ctx:
        ring = [net.sb(f"load_ring{p}", [P, TB, C], F32, ctx) for p in range(2)]
        turned = net.ps("load_turned", [P, 2, KC, S], F32, ctx)
        const_in = net.sem("load_const_in")
        loaded = [net.sem(f"load_loaded{p}") for p in range(2)]
        turned_ready = net.sem("load_turned_ready")
        copied_a = net.sem("load_copied_a")
        copied_v = net.sem("load_copied_v")
        x_tiles = net.dram["x"].rearrange("b t n c -> (b t n) c").rearrange("(u p) c -> p u c", p=P)
        with nc.Block() as block:
            @block.sync
            def _(sp):
                sp.dma_start(net.ident[:, :], net.dram["c_ident"]).then_inc(const_in, 16)

                def load(b, p):
                    sp.dma_start(ring[p][:, :, :], x_tiles[:, ds(b * TB, TB), :]).then_inc(loaded[p], 16)
                load(0, 0)
                load(1, 1)
                with sp.Fori(1, B // 2) as i:
                    for p in range(2):
                        sp.wait_ge(turned_ready, i * 2 + p - 1)
                        net.go_on(sp)
                        load(i * 2 + p, p)

            @block.tensor
            def _(pe):
                pe.wait_ge(const_in, 16)

                def turn(b, p, first):
                    if not first:
                        pe.wait_ge(copied_a, b - 1)
                        pe.wait_ge(copied_v, b - 1)
                    for c in range(KC):
                        for t in range(TB):
                            last = pe.transpose(turned[:, p, c, t * P:(t + 1) * P],
                                                ring[p][:, t, c * P:(c + 1) * P], net.ident[:, :])
                    last.then_inc(turned_ready, 1)
                for p in range(2):
                    pe.wait_ge(loaded[p], 16)
                    turn(p, p, True)
                with pe.Fori(1, B // 2) as i:
                    for p in range(2):
                        pe.wait_ge(loaded[p], i * 16 + 16)
                        turn(i * 2 + p, p, False)

            @block.scalar
            def _(act):
                with act.Fori(0, B // 2) as i:
                    for p in range(2):
                        act.wait_ge(turned_ready, i * 2 + p + 1)
                        act.activation(net.xT[:, 0, ds((i * 2 + p) * S, S)], turned[:, p, 0, :],
                                       ACT.Copy).then_inc(copied_a, 1)

            @block.vector
            def _(dve):
                with dve.Fori(0, B // 2) as i:
                    for p in range(2):
                        dve.wait_ge(turned_ready, i * 2 + p + 1)
                        dve.tensor_copy(net.xT[:, 1, ds((i * 2 + p) * S, S)],
                                        turned[:, p, 1, :]).then_inc(copied_v, 1)


def inverse_root(net, eng_steps, dve, var, root, out, tmp, sqrt_asked, sqrt_done, asked):
    s = eng_steps
    s.wait()
    dve.tensor_copy(root, var).then_inc(sqrt_asked, 1)
    dve.wait_ge(sqrt_done, asked)
    s.did(dve.reciprocal(out, root))
    s.wait()
    s.did(dve.tensor_tensor(tmp, out, out, ALU.mult))
    s.wait()
    s.did(dve.tensor_tensor(tmp, tmp, var, ALU.mult))
    s.wait()
    s.did(dve.tensor_scalar(tmp, tmp, -0.5, 1.5, ALU.mult, ALU.add))
    s.wait()
    s.did(dve.tensor_tensor(out, out, tmp, ALU.mult))


def conv_block(net, layer, to_tokens):
    nc = net.nc
    n_ = f"L{layer}"
    with ExitStack() as ctx:
        sb = lambda name, shape, dt=F32: net.sb(f"{n_}_{name}", shape, dt, ctx)
        sem = lambda name: net.sem(f"{n_}_{name}")
        w_in = sb("w_in", [P, 3, C])
        ww_in = sb("ww_in", [P, KC, LAT])
        affine = sb("affine", [P, 2, KC])
        wT = [sb(f"wT_{part}", [P, KC, 3, LAT], F32R) for part in ("high", "low")]
        wwT = [sb(f"wwT_{part}", [P, C], F32R) for part in ("high", "low")]
        mix = sb("mix", [P, TB, S])
        def parts_of(name, shape):
            return [tuple(sb(f"{name}_{part}{p}", shape, F32R) for part in ("high", "low")) for p in range(2)]
        xb_parts = parts_of("xb", [P, KC, S])
        normed = [sb(f"normed{p}", [P, KC, S]) for p in range(2)] if to_tokens else None
        theta, phi, g = parts_of("theta", [P, S]), parts_of("phi", [P, S]), parts_of("g", [P, TB, LAT])
        mixed_full = [sb(f"mixed_full{p}", [P, TB, S]) for p in range(2)]
        mixed = parts_of("mixed", [P, TB, S])
        st = parts_of("st", [P, S])
        stats = sb("stats", [P, KC, B, 6])
        norm = sb("norm", [P, 12, KC])
        mv = sb("mv", [P, KC, 2])
        turned = net.ps(f"{n_}_ps_turned", [P, S], F32, ctx)
        ps_phi = net.ps(f"{n_}_ps_phi", [P, S], F32, ctx)
        ps_g = net.ps(f"{n_}_ps_g", [P, TB, LAT], F32, ctx)
        ps_s = net.ps(f"{n_}_ps_s", [P, 2, S], F32, ctx)
        ps_st = net.ps(f"{n_}_ps_st", [P, S], F32, ctx)
        ps_out = net.ps(f"{n_}_ps_out", [P, KC, S], F32, ctx)
        ps_theta = turned

        w_loaded = sem("w_loaded")
        mix_loaded = sem("mix_loaded")
        affine_loaded = sem("affine_loaded")
        w_turned = sem("w_turned")
        w_ready = sem("w_ready")
        w_high = sem("w_high")
        xb_ready = sem("xb_ready")
        xb_low = sem("xb_low")
        projected = sem("projected")
        proj_copied = sem("proj_copied")
        proj_low = sem("proj_low")
        scored = sem("scored")
        masked = sem("masked")
        mixed_high = sem("mixed_high")
        mixed_low_p = sem("mixed_low_p")
        mixed_low_v = sem("mixed_low_v")
        st_ready = sem("st_ready")
        st_copied = sem("st_copied")
        st_low = sem("st_low")
        out_ready = sem("out_ready")
        out_added = sem("out_added")
        stats_step = sem("stats_step")
        sqrt_asked, sqrt_done = sem("sqrt_asked"), sem("sqrt_done")
        norm_step = sem("norm_step")
        norm_ready = sem("norm_ready")
        bn_done_a, bn_done_v = sem("bn_done_a"), sem("bn_done_v")
        bn_turned = sem("bn_turned")
        bn_copied_a, bn_copied_v = sem("bn_copied_a"), sem("bn_copied_v")

        LOW_P = 2

        mean, var, root, inv, scale, shift, tmp = (norm[:, j, :] for j in range(7))

        with nc.Block() as block:
            @block.sync
            def _(sp):
                for j, w in enumerate(("Wt", "Wp", "Wg")):
                    sp.dma_start(w_in[:, j, :], net.dram[f"L{layer}_conv_{w}"]).then_inc(w_loaded, 16)
                sp.dma_start(ww_in[:, :, :], net.dram[f"L{layer}_conv_Ww"].rearrange("(k p) l -> p k l", p=P)
                             ).then_inc(w_loaded, 16)
                sp.dma_start(mix[:, :, :], net.dram["c_mix"]).then_inc(mix_loaded, 16)
                for j, w in enumerate(("gamma", "beta")):
                    for c in range(KC):
                        sp.dma_start(affine[:, j, c:c + 1],
                                     net.dram[f"L{layer}_conv_{w}"][c * P:(c + 1) * P].rearrange("(p a) -> p a", a=1)
                                     ).then_inc(affine_loaded, 16)

            @block.tensor
            def _(pe):
                pe.wait_ge(w_loaded, 64)
                for j in range(3):
                    for k in range(KC):
                        bank, at = ((ps_s[:, 0, :], 2 * j + k) if 2 * j + k < 4 else (ps_s[:, 1, :], 2 * j + k - 4))
                        pe.transpose(bank[:, at * P:(at + 1) * P], w_in[:, j, k * P:(k + 1) * P], net.ident[:, :])
                for c in range(KC):
                    last = pe.transpose(ps_s[:, 1, (2 + c) * P:(3 + c) * P], ww_in[:, c, :], net.ident[:, :])
                last.then_inc(w_turned, 1)
                pe.wait_ge(w_ready, 2)

                def product(out, left, right, first=True, last=True):
                    (left_high, left_low), (right_high, right_low) = left, right
                    pe.matmul(out, left_low, right_high, start=first, stop=False)
                    pe.matmul(out, left_high, right_high, start=False, stop=False)
                    return pe.matmul(out, left_high, right_low, start=False, stop=last)

                def cut(parts, *at):
                    return tuple(part[at] for part in parts)
                every = slice(None)

                def project(b, p, first):
                    pe.wait_ge(xb_ready, b + 1)
                    pe.wait_ge(xb_low, b + 1)
                    for j, out in enumerate((ps_theta, ps_phi)):
                        if not first:
                            pe.wait_ge(proj_low, b * 3 + j - 2)
                        for k in range(KC):
                            last = product(out[:, :], cut(wT, every, k, j, every), cut(xb_parts[p], every, k, every),
                                           k == 0, k == KC - 1)
                        last.then_inc(projected, 1)
                    if not first:
                        pe.wait_ge(proj_low, b * 3)
                    for t in range(TB):
                        for k in range(KC):
                            last = product(ps_g[:, t, :], cut(xb_parts[p], every, k, slice(t * P, (t + 1) * P)),
                                           cut(wT, every, k, 2, every), k == 0, k == KC - 1)
                    last.then_inc(projected, 1)

                def score(b, p, first):
                    pe.wait_ge(proj_low, b * 3 + 2)
                    for kb in range(TB):
                        if not (first and kb < 2):
                            pe.wait_ge(masked, b * TB + kb - 1)
                        product(ps_s[:, kb % 2, :], cut(phi[p], every, slice(kb * P, (kb + 1) * P)),
                                cut(theta[p], every, every)).then_inc(scored, 1)

                def weigh(b, p, first):
                    pe.wait_ge(proj_low, b * 3 + 3)
                    pe.wait_ge(mixed_low_p, b + 1)
                    pe.wait_ge(mixed_low_v, b + 1)
                    if not first:
                        pe.wait_ge(st_low, b)
                    for kb in range(TB):
                        last = product(ps_st[:, :], cut(g[p], every, kb, every), cut(mixed[p], every, kb, every),
                                       kb == 0, kb == TB - 1)
                    last.then_inc(st_ready, 1)

                def output(b, p, first):
                    pe.wait_ge(st_low, b + 1)
                    if not first:
                        pe.wait_ge(out_added, b * KC)
                    for c in range(KC):
                        product(ps_out[:, c, :], cut(wwT, every, slice(c * P, (c + 1) * P)),
                                cut(st[p], every, every)).then_inc(out_ready, 1)

                project(0, 0, True)
                score(0, 0, True)
                project(1, 1, False)
                weigh(0, 0, True)
                score(1, 1, False)
                output(0, 0, True)
                with pe.Fori(1, B // 2) as i:
                    for p in range(2):
                        project(i * 2 + p, p, False)
                        weigh(i * 2 + p - 1, 1 - p, False)
                        score(i * 2 + p, p, False)
                        output(i * 2 + p - 1, 1 - p, False)
                weigh(B - 1, 1, False)
                output(B - 1, 1, False)
                if to_tokens:
                    def turn(b, p, first):
                        pe.wait_ge(bn_done_a, b + 1)
                        pe.wait_ge(bn_done_v, b + 1)
                        if not first:
                            pe.wait_ge(bn_copied_a, b - 1)
                            pe.wait_ge(bn_copied_v, b - 1)
                        dst = (ps_out, ps_s)[p]
                        for t in range(TB):
                            for c in range(KC):
                                last = pe.transpose(dst[:, t // 2, (t % 2) * C + c * P:(t % 2) * C + (c + 1) * P],
                                                    normed[p][:, c, t * P:(t + 1) * P], net.ident[:, :])
                        last.then_inc(bn_turned, 1)
                    turn(0, 0, True)
                    turn(1, 1, True)
                    with pe.Fori(1, B // 2) as i:
                        for p in range(2):
                            turn(i * 2 + p, p, False)

            @block.scalar
            def _(act):
                def fetch(b, p, first):
                    if not first:
                        act.wait_ge(projected, b * 3 - 3)
                    act.activation(xb_parts[p][0][:, :, :], net.xT[:, :, ds(b * S, S)], ACT.Copy).then_inc(xb_ready, 1)

                def copy_projections(b, p, first):
                    for j, (src, dst) in enumerate(((ps_theta, theta), (ps_phi, phi), (ps_g, g))):
                        act.wait_ge(projected, b * 3 + j + 1)
                        if j == 0 and not first:
                            act.wait_ge(st_ready, b - 1)
                        act.activation(dst[p][0][:], src[:], ACT.Copy).then_inc(proj_copied, 1)

                def copy_st(b, p):
                    act.wait_ge(st_ready, b + 1)
                    act.activation(st[p][0][:, :], ps_st[:, :], ACT.Copy).then_inc(st_copied, 1)

                def copy_mixed(b, p, first):
                    if not first:
                        act.wait_ge(st_ready, b - 1)
                    for kb in range(TB):
                        act.wait_ge(masked, b * TB + kb + 1)
                        act.activation(mixed[p][0][:, kb, :], mixed_full[p][:, kb, :], ACT.Copy).then_inc(mixed_high, 1)

                def element(b, p, first=False, last=False):
                    copy_projections(b, p, first)
                    copy_st(b - 1, 1 - p)
                    if not last:
                        fetch(b + 1, 1 - p, False)
                    copy_mixed(b, p, first)
                act.wait_ge(w_ready, 2)
                fetch(0, 0, True)
                fetch(1, 1, True)
                copy_projections(0, 0, True)
                copy_mixed(0, 0, True)
                element(1, 1, first=True)
                with act.Fori(1, B // 2 - 1) as i:
                    for p in range(2):
                        element(i * 2 + p, p)
                element(B - 2, 0)
                element(B - 1, 1, last=True)
                copy_st(B - 1, 1)
                act.wait_ge(sqrt_asked, 1)
                act.activation(root, root, ACT.Sqrt).then_inc(sqrt_done, 1)
                act.wait_ge(norm_ready, 1)
                if not to_tokens:
                    act.activation(net.xT[:, 0, :], net.xT[:, 0, :], ACT.Identity, bias=shift[:, 0:1],
                                   scale=scale[:, 0:1]).then_inc(bn_done_a, 1)
                else:
                    def norm0(b, p, first):
                        if not first:
                            act.wait_ge(bn_turned, b - 1)
                        act.activation(normed[p][:, 0, :], net.xT[:, 0, ds(b * S, S)], ACT.Identity,
                                       bias=shift[:, 0:1], scale=scale[:, 0:1]).then_inc(bn_done_a, 1)

                    def take(b, p):
                        act.wait_ge(bn_turned, b + 1)
                        act.activation(net.x[:, ds(b * TB, 2), :], (ps_out, ps_s)[p][:, 0, :].rearrange(
                            "p (t c) -> p t c", c=C), ACT.Copy).then_inc(bn_copied_a, 1)
                    norm0(0, 0, True)
                    norm0(1, 1, True)
                    with act.Fori(1, B // 2) as i:
                        for p in range(2):
                            take(i * 2 + p - 2, p)
                            norm0(i * 2 + p, p, False)
                    take(B - 2, 0)
                    take(B - 1, 1)

            @block.gpsimd
            def _(pool):
                def low_x(b, p):
                    pool.wait_ge(xb_ready, b + 1)
                    net.go_on(pool)
                    pool.tensor_tensor(xb_parts[p][1][:, :, :], net.xT[:, :, ds(b * S, S)],
                                       xb_parts[p][0][:, :, :].bitcast(F32), ALU.subtract
                                       ).then_inc(xb_low, 1)

                def low_mixed(b, p):
                    for kb in range(LOW_P):
                        pool.wait_ge(mixed_high, b * TB + kb + 1)
                        net.go_on(pool)
                        last = pool.tensor_tensor(mixed[p][1][:, kb, :], mixed_full[p][:, kb, :],
                                                  mixed[p][0][:, kb, :].bitcast(F32), ALU.subtract)
                    last.then_inc(mixed_low_p, 1)
                low_x(0, 0)
                low_x(1, 1)
                low_mixed(0, 0)
                low_x(2, 0)
                low_mixed(1, 1)
                with pool.Fori(1, B // 2 - 1) as i:
                    for p in range(2):
                        low_x(i * 2 + p + 1, 1 - p)
                        low_mixed(i * 2 + p, p)
                low_x(B - 1, 1)
                low_mixed(B - 2, 0)
                low_mixed(B - 1, 1)

            @block.vector
            def _(dve):
                dve.wait_ge(w_turned, 1)
                pairs = [([w[:, :, :, :].rearrange("p k j l -> p j k l")[:, 0:2, :, :] for w in wT],
                          ps_s[:, 0, :].rearrange("p (j k l) -> p j k l", j=2, k=KC)),
                         ([w[:, :, 2, :] for w in wT], ps_s[:, 1, 0:2 * P].rearrange("p (k l) -> p k l", k=KC)),
                         ([w[:, :] for w in wwT], ps_s[:, 1, 2 * P:4 * P])]
                for (high, _), full in pairs:
                    dve.tensor_copy(high, full).then_inc(w_high, 1)
                for n, ((high, low), full) in enumerate(pairs):
                    dve.wait_ge(w_high, n + 1)
                    last = dve.tensor_tensor(low, full, high.bitcast(F32), ALU.subtract)
                last.then_inc(w_ready, 2)
                dve.wait_ge(mix_loaded, 16)

                def mask(b, p, first):
                    if not first:
                        dve.wait_ge(mixed_low_p, b - 1)
                        dve.wait_ge(mixed_low_v, b - 1)
                    for kb in range(TB):
                        dve.wait_ge(scored, b * TB + kb + 1)
                        dve.tensor_tensor(mixed_full[p][:, kb, :], ps_s[:, kb % 2, :], mix[:, kb, :],
                                          ALU.mult).then_inc(masked, 1)

                def add(b, p):
                    for c in range(KC):
                        dve.wait_ge(out_ready, b * KC + c + 1)
                        x_c = net.xT[:, c, ds(b * S, S)]
                        dve.tensor_tensor(x_c, ps_out[:, c, :], x_c, ALU.add).then_inc(out_added, 1)
                        dve.wait_ge(out_added, b * KC + c + 1)
                        dve.bn_stats(stats[:, c, ds(b, 1), :], x_c).then_inc(stats_step, 1)
                def low_projections(b, p):
                    for j, (src, dst) in enumerate(((ps_theta, theta), (ps_phi, phi), (ps_g, g))):
                        dve.wait_ge(proj_copied, b * 3 + j + 1)
                        dve.tensor_tensor(dst[p][1][:], src[:], dst[p][0][:].bitcast(F32), ALU.subtract
                                          ).then_inc(proj_low, 1)

                def low_st(b, p):
                    dve.wait_ge(st_copied, b + 1)
                    dve.tensor_tensor(st[p][1][:, :], ps_st[:, :], st[p][0][:, :].bitcast(F32), ALU.subtract
                                      ).then_inc(st_low, 1)

                def low_mixed(b, p):
                    for kb in range(LOW_P, TB):
                        dve.wait_ge(mixed_high, b * TB + kb + 1)
                        last = dve.tensor_tensor(mixed[p][1][:, kb, :], mixed_full[p][:, kb, :],
                                                 mixed[p][0][:, kb, :].bitcast(F32), ALU.subtract)
                    last.then_inc(mixed_low_v, 1)

                def element(b, p, first=False):
                    low_projections(b, p)
                    low_st(b - 1, 1 - p)
                    mask(b, p, first)
                    low_mixed(b, p)
                    add(b - 1, 1 - p)
                low_projections(0, 0)
                mask(0, 0, True)
                low_mixed(0, 0)
                element(1, 1, first=True)
                with dve.Fori(1, B // 2) as i:
                    for p in range(2):
                        element(i * 2 + p, p)
                low_st(B - 1, 1)
                add(B - 1, 1)
                s = Order(dve, norm_step)
                dve.wait_ge(affine_loaded, 64)
                dve.wait_ge(stats_step, B * KC)
                for c in range(KC):
                    s.did(dve.bn_aggr(mv[:, c, :], stats[:, c, :, :].rearrange("p b f -> p (b f)")))
                s.wait()
                s.did(dve.tensor_copy(mean, mv[:, :, 0]))
                s.did(dve.tensor_scalar(var, mv[:, :, 1], BN_EPS, None, ALU.add))
                inverse_root(net, s, dve, var, root, inv, tmp, sqrt_asked, sqrt_done, 1)
                s.wait()
                s.did(dve.tensor_tensor(scale, inv, affine[:, 0, :], ALU.mult))
                s.wait()
                s.did(dve.tensor_tensor(tmp, mean, scale, ALU.mult))
                s.wait()
                dve.tensor_tensor(shift, affine[:, 1, :], tmp, ALU.subtract).then_inc(norm_ready, 1)
                dve.wait_ge(norm_ready, 1)
                if not to_tokens:
                    dve.tensor_scalar(net.xT[:, 1, :], net.xT[:, 1, :], scale[:, 1:2], shift[:, 1:2],
                                      ALU.mult, ALU.add).then_inc(bn_done_v, 1)
                else:
                    def norm1(b, p, first):
                        if not first:
                            dve.wait_ge(bn_turned, b - 1)
                        dve.tensor_scalar(normed[p][:, 1, :], net.xT[:, 1, ds(b * S, S)], scale[:, 1:2], shift[:, 1:2],
                                          ALU.mult, ALU.add).then_inc(bn_done_v, 1)

                    def take(b, p):
                        dve.wait_ge(bn_turned, b + 1)
                        dve.tensor_copy(net.x[:, ds(b * TB + 2, 2), :], (ps_out, ps_s)[p][:, 1, :].rearrange(
                            "p (t c) -> p t c", c=C)).then_inc(bn_copied_v, 1)
                    norm1(0, 0, True)
                    norm1(1, 1, True)
                    with dve.Fori(1, B // 2) as i:
                        for p in range(2):
                            take(i * 2 + p - 2, p)
                            norm1(i * 2 + p, p, False)
                    take(B - 2, 0)
                    take(B - 1, 1)


def conv_layers(net):
    with ExitStack() as ctx:
        net.hold_channels("conv", ctx)
        load_tokens(net)
        conv_block(net, 0, False)
        conv_block(net, 1, True)


def token_stats(net, dve, b, done):
    for t in range(TB):
        dve.bn_stats(net.stats[:, ds(b * TB + t, 1), :], net.x[:, ds(b * TB + t, 1), :]).then_inc(done, 1)


def layer_norm(net, tag, to_dram=None, stats_known=True):
    nc = net.nc
    with ExitStack() as ctx:
        sb = lambda name, shape, dt=F32: net.sb(f"{tag}_{name}", shape, dt, ctx)
        sem = lambda name: net.sem(f"{tag}_{name}")
        mv = sb("mv", [P, NT, 2])
        var, root, rstd, tmp = (sb(n, [P, NT]) for n in ("var", "root", "rstd", "tmp"))
        normed = [sb(f"normed{p}", [P, TB, C]) for p in range(2)]
        turned = net.ps(f"{tag}_turned", [P, 2, KC, S], F32, ctx)
        stats_step, aggr_step, step = sem("stats_step"), sem("aggr_step"), sem("step")
        sqrt_asked, sqrt_done = sem("sqrt_asked"), sem("sqrt_done")
        normed_ready = sem("normed_ready")
        turned_ready = sem("turned_ready")
        copied = sem("copied")
        stored = [sem(f"stored{p}") for p in range(2)]
        with nc.Block() as block:
            @block.vector
            def _(dve):
                if not stats_known:
                    with dve.Fori(0, B) as b:
                        token_stats(net, dve, b, stats_step)
                    dve.wait_ge(stats_step, NT)
                for t in range(NT):
                    dve.bn_aggr(mv[:, t, :], net.stats[:, t, :]).then_inc(aggr_step, 1)
                dve.wait_ge(aggr_step, NT)
                s = Order(dve, step)
                s.did(dve.tensor_scalar(var[:, :], mv[:, :, 1], LN_EPS, None, ALU.add))
                inverse_root(net, s, dve, var[:, :], root[:, :], rstd[:, :], tmp[:, :], sqrt_asked, sqrt_done, 1)
                s.wait()

                def normalise(b, p, first):
                    if not first:
                        dve.wait_ge(turned_ready, b - 1)
                        if to_dram is not None:
                            dve.wait_ge(stored[p], (b - p) * 8)
                    for t in range(TB):
                        last = dve.tensor_scalar(normed[p][:, t, :], net.x[:, ds(b * TB + t, 1), :],
                                                 mv[:, ds(b * TB + t, 1), 0], rstd[:, ds(b * TB + t, 1)],
                                                 ALU.subtract, ALU.mult)
                    last.then_inc(normed_ready, 1)
                normalise(0, 0, True)
                normalise(1, 1, True)
                with dve.Fori(1, B // 2) as i:
                    for p in range(2):
                        normalise(i * 2 + p, p, False)

            @block.tensor
            def _(pe):
                def turn(b, p, first):
                    pe.wait_ge(normed_ready, b + 1)
                    if not first:
                        pe.wait_ge(copied, b - 1)
                    for c in range(KC):
                        for t in range(TB):
                            last = pe.transpose(turned[:, p, c, t * P:(t + 1) * P],
                                                normed[p][:, t, c * P:(c + 1) * P], net.ident[:, :])
                    last.then_inc(turned_ready, 1)
                turn(0, 0, True)
                turn(1, 1, True)
                with pe.Fori(1, B // 2) as i:
                    for p in range(2):
                        turn(i * 2 + p, p, False)

            @block.scalar
            def _(act):
                act.wait_ge(sqrt_asked, 1)
                act.activation(root[:, :], root[:, :], ACT.Sqrt).then_inc(sqrt_done, 1)
                with act.Fori(0, B // 2) as i:
                    for p in range(2):
                        act.wait_ge(turned_ready, i * 2 + p + 1)
                        act.activation(net.xT[:, :, ds((i * 2 + p) * S, S)], turned[:, p, :, :],
                                       ACT.Copy).then_inc(copied, 1)

            if to_dram is not None:
                rows = to_dram.rearrange("(u p) c -> p u c", p=P)

                @block.sync
                def _(sp):
                    with sp.Fori(0, B // 2) as i:
                        for p in range(2):
                            sp.wait_ge(normed_ready, i * 2 + p + 1)
                            net.go_on(sp)
                            sp.dma_start(rows[:, ds((i * 2 + p) * TB, TB), :], normed[p][:, :, :]
                                         ).then_inc(stored[p], 16)
                    for p in range(2):
                        sp.wait_ge(stored[p], 16 * B // 2)


def project_qkv(net, layer, scratch, values, gates):
    nc = net.nc
    rotary = layer == 3
    tag = f"L{layer}_qkv"
    regions = ((slice(0, P), slice(0, 2)), (slice(0, NKV * HD), slice(2, 3)))
    with ExitStack() as ctx:
        sb = lambda name, shape, dt=F32: net.sb(f"{tag}_{name}", shape, dt, ctx)
        sem = lambda name: net.sem(f"{tag}_{name}")
        w = sb("w", [P, KC, 3 * P + 32])
        w_plain = None if rotary else sb("w_plain", [P, KC, 3 * P])
        full = [sb(f"full{p}", [P, 3, S]) for p in range(2)]
        parts = [sb(f"parts{p}", [P, 3, 3, S], BF16) for p in range(2)]
        rest = sb("rest", [P, 3, S])
        proj = net.ps(f"{tag}_proj", [P, 3, S], F32, ctx)
        small = net.ps(f"{tag}_small", [P, TB, P], F32, ctx)
        w_loaded = sem("w_loaded")
        w_turned, w_ready = sem("w_turned"), sem("w_ready")
        projected = sem("projected")
        copied = sem("copied")
        turned_ready = sem("turned_ready")
        values_ready = sem("values_ready")
        hi_ready = sem("hi_ready")
        mid_ready = sem("mid_ready")
        rest_ready = sem("rest_ready")
        lo_ready = sem("lo_ready")
        written = [sem(f"written{p}") for p in range(2)]
        if rotary:
            w_in = sb("w_in", [P, 3, C])
            wg_in = sb("wg_in", [32, C])
            rope = sb("rope", [P, 4, S])
            swap = sb("swap", [P, 2, P])
            cosd = sb("cosd", [P, 3, S])
            sind = sb("sind", [P, 3, S])
            rot = [sb(f"rot{p}", [P, 3, S]) for p in range(2)]
            gate_row = [sb(f"gate_row{p}", [32, S]) for p in range(2)]
            gate_e = sb("gate_e", [P, TB, 32])
            gate_s = sb("gate_s", [P, TB, 32])
            swapped = net.ps(f"{tag}_swapped", [P, 3, S], F32, ctx)
            gate_ps = net.ps(f"{tag}_gate", [32, S], F32, ctx)
            swapped_ready = sem("swapped_ready")
            cos_ready = sem("cos_ready")
            sin_ready = sem("sin_ready")
            rot_ready = sem("rot_ready")
            gate_exp = sem("gate_exp")
            gate_step = sem("gate_step")
            gates_done = sem("gates_done")
        source = rot if rotary else full
        source_ready = rot_ready if rotary else copied

        with nc.Block() as block:
            @block.sync
            def _(sp):
                if not rotary:
                    sp.dma_start(w_plain[:, :, :], net.dram["L2_attn_W_qkv"].rearrange("(k p) n -> p k n", p=P)
                                 ).then_inc(w_loaded, 16)
                else:
                    sp.dma_start(w_in[:, 0:2, :], net.dram["L3_attn_Wq"].rearrange("(j p) c -> p j c", p=P)
                                 ).then_inc(w_loaded, 16)
                    sp.dma_start(w_in[0:64, 2, :], net.dram["L3_attn_Wk"]).then_inc(w_loaded, 16)
                    sp.dma_start(w_in[64:128, 2, :], net.dram["L3_attn_Wv"]).then_inc(w_loaded, 16)
                    sp.dma_start(wg_in[0:16, :], net.dram["L3_attn_Wg_slc"]).then_inc(w_loaded, 16)
                    sp.dma_start(wg_in[16:32, :], net.dram["L3_attn_Wg_swa"]).then_inc(w_loaded, 16)
                    sp.dma_start(rope[:, :, :], net.dram["c_rope"]).then_inc(w_loaded, 16)
                    sp.dma_start(swap[:, :, :], net.dram["c_swap"]).then_inc(w_loaded, 16)
                with sp.Fori(0, B // 2) as i:
                    for p in range(2):
                        b = i * 2 + p
                        sp.wait_ge(lo_ready, b + 1)
                        sp.wait_ge(mid_ready, b + 1)
                        net.go_on(sp)
                        for c in range(2):
                            for g in range(2):
                                sp.dma_start(scratch["q"][ds(b * NKV + 2 * c + g, 1), :, :].rearrange(
                                    "u (a r) t -> r (u a) t", a=3), parts[p][64 * g:64 * g + 64, c, :, :]
                                    ).then_inc(written[p], 16)
                        sp.dma_start(scratch["k"][:, ds(b * NKV * HD, NKV * HD), :].rearrange("a r t -> r a t"),
                                     parts[p][0:64, 2, :, :]).then_inc(written[p], 16)
                for p in range(2):
                    sp.wait_ge(written[p], 5 * 16 * B // 2)

            @block.tensor
            def _(pe):
                if rotary:
                    pe.wait_ge(w_loaded, 7 * 16)
                    for k in range(KC):
                        for j in range(3):
                            pe.transpose(swapped[:, k, j * P:(j + 1) * P], w_in[:, j, k * P:(k + 1) * P],
                                         net.ident[:, :])
                        last = pe.transpose(swapped[:, k, 3 * P:3 * P + 32], wg_in[:, k * P:(k + 1) * P],
                                            net.ident[0:32, 0:32])
                    last.then_inc(w_turned, 1)
                pe.wait_ge(w_ready, 1)

                def project(b, first):
                    if not first:
                        pe.wait_ge(copied, b)
                    for j in range(3):
                        for k in range(KC):
                            last = pe.matmul(proj[:, j, :], w[:, k, j * P:(j + 1) * P], net.xT[:, k, ds(b * S, S)],
                                             start=k == 0, stop=k == KC - 1)
                    if rotary:
                        for k in range(KC):
                            last = pe.matmul(gate_ps[:, :], w[:, k, 3 * P:3 * P + 32], net.xT[:, k, ds(b * S, S)],
                                             start=k == 0, stop=k == KC - 1)
                    last.then_inc(projected, 1)

                def turn(b, p, first):
                    pe.wait_ge(copied, b + 1)
                    if not first:
                        pe.wait_ge(values_ready, b)
                        if rotary:
                            pe.wait_ge(gate_exp, b)
                    for t in range(TB):
                        last = pe.transpose(small[:, t, :], full[p][:, 2, t * P:(t + 1) * P], net.ident[:, :])
                        if rotary:
                            last = pe.transpose(small[:, t, 0:32], gate_row[p][:, t * P:(t + 1) * P],
                                                net.ident[0:32, 0:32])
                    last.then_inc(turned_ready, 1)
                    if rotary:
                        if not first:
                            pe.wait_ge(sin_ready, b)
                        for j in range(3):
                            last = pe.matmul(swapped[:, j, :], swap[:, j // 2, :], full[p][:, j, :], start=True, stop=True)
                        last.then_inc(swapped_ready, 1)
                project(0, True)
                turn(0, 0, True)
                project(1, False)
                turn(1, 1, False)
                with pe.Fori(1, B // 2) as i:
                    for p in range(2):
                        project(i * 2 + p, False)
                        turn(i * 2 + p, p, False)

            @block.scalar
            def _(act):
                def copy(b, p, first):
                    act.wait_ge(projected, b + 1)
                    if not first:
                        act.wait_ge(turned_ready, b - 1)
                        if rotary:
                            act.wait_ge(swapped_ready, b - 1)
                            act.wait_ge(cos_ready, b - 1)
                        else:
                            act.wait_ge(rest_ready, b - 1)
                    if rotary:
                        act.activation(gate_row[p][:, :], gate_ps[:, :], ACT.Copy)
                    act.activation(full[p][:, :, :], proj[:, :, :], ACT.Copy).then_inc(copied, 1)

                def exp_gates(b, first):
                    act.wait_ge(values_ready, b + 1)
                    if not first:
                        act.wait_ge(gates_done, b)
                    act.activation(gate_e[:, :, :], small[:, :, 0:32], ACT.Exp, scale=-1.0).then_inc(gate_exp, 1)

                def split(b, p, first=False, early=False, last=False):
                    if rotary:
                        exp_gates(b, first)
                    act.wait_ge(source_ready, b + 1)
                    if not early:
                        act.wait_ge(written[p], (b - p) * 40)
                    for rows, chunks in regions:
                        high = act.activation(parts[p][rows, chunks, 0, :], source[p][rows, chunks, :], ACT.Copy)
                    high.then_inc(hi_ready, 1)
                    if not last:
                        copy(b + 1, 1 - p, first)
                    act.wait_ge(rest_ready, b + 1)
                    for rows, chunks in regions:
                        middle = act.activation(parts[p][rows, chunks, 1, :], rest[rows, chunks, :], ACT.Copy)
                    middle.then_inc(mid_ready, 1)
                copy(0, 0, True)
                split(0, 0, first=True, early=True)
                split(1, 1, early=True)
                with act.Fori(1, B // 2 - 1) as i:
                    for p in range(2):
                        split(i * 2 + p, p)
                split(B - 2, 0)
                split(B - 1, 1, last=True)

            @block.vector
            def _(dve):
                if rotary:
                    dve.wait_ge(w_turned, 1)
                    plain, end = swapped, 3 * P + 32
                else:
                    dve.wait_ge(w_loaded, 16)
                    plain, end = w_plain, 3 * P
                for k in range(KC):
                    dve.tensor_copy(w[:, k, 0:2 * P].rearrange("p (g d h) -> p g d h", g=NKV, h=GR),
                                    plain[:, k, 0:2 * P].rearrange("p (g h d) -> p g d h", g=NKV, h=GR))
                dve.tensor_copy(w[:, :, 2 * P:end], plain[:, 0:KC, 2 * P:end]).then_inc(w_ready, 1)

                def per_element(b, p, first):
                    dve.wait_ge(turned_ready, b + 1)
                    dve.tensor_copy(values[:, ds(b * NKV, NKV), :, :],
                                    small[:, :, 64:128].rearrange("p t (g d) -> p g t d", g=NKV)
                                    ).then_inc(values_ready, 1)
                    if rotary:
                        dve.wait_ge(swapped_ready, b + 1)
                        if not first:
                            dve.wait_ge(rot_ready, b)
                        sin_q = rope[:, 1:2, :].to_broadcast([P, 2, S])
                        dve.tensor_tensor(sind[:, 0:2, :], swapped[:, 0:2, :], sin_q, ALU.mult)
                        dve.tensor_tensor(sind[0:64, 2, :], swapped[0:64, 2, :], rope[0:64, 3, :],
                                          ALU.mult).then_inc(sin_ready, 1)
                        dve.wait_ge(gate_exp, b + 1)
                        s = Order(dve, gate_step, b * 2)
                        s.did(dve.tensor_scalar(gate_s[:, :, :], gate_e[:, :, :], 1.0, None, ALU.add))
                        s.wait()
                        s.did(dve.reciprocal(gate_s[:, :, :], gate_s[:, :, :]))
                        s.wait()
                        dve.tensor_tensor(gates[:, ds(b * NKV, NKV), :, :],
                                          gate_s[:, :, 0:16].rearrange("p t (g h) -> p g t h", g=NKV),
                                          gate_s[:, :, 16:32].rearrange("p t (g h) -> p g t h", g=NKV),
                                          ALU.add).then_inc(gates_done, 1)
                    dve.wait_ge(hi_ready, b + 1)
                    if not first:
                        dve.wait_ge(lo_ready, b)
                        dve.wait_ge(mid_ready, b)
                    for rows, chunks in regions:
                        last = dve.tensor_tensor(rest[rows, chunks, :], source[p][rows, chunks, :],
                                                 parts[p][rows, chunks, 0, :], ALU.subtract)
                    last.then_inc(rest_ready, 1)
                    dve.wait_ge(mid_ready, b + 1)
                    for rows, chunks in regions:
                        last = dve.tensor_tensor(parts[p][rows, chunks, 2, :], rest[rows, chunks, :],
                                                 parts[p][rows, chunks, 1, :], ALU.subtract)
                    last.then_inc(lo_ready, 1)
                per_element(0, 0, True)
                per_element(1, 1, False)
                with dve.Fori(1, B // 2) as i:
                    for p in range(2):
                        per_element(i * 2 + p, p, False)

            if rotary:
                @block.gpsimd
                def _(pool):
                    def turn_positions(b, p, first, early):
                        pool.wait_ge(copied, b + 1)
                        if not first:
                            pool.wait_ge(rot_ready, b)
                        pool.tensor_tensor(cosd[:, 0:2, :], full[p][:, 0:2, :],
                                           rope[:, 0:1, :].to_broadcast([P, 2, S]), ALU.mult)
                        pool.tensor_tensor(cosd[0:64, 2, :], full[p][0:64, 2, :], rope[0:64, 2, :],
                                           ALU.mult).then_inc(cos_ready, 1)
                        pool.wait_ge(cos_ready, b + 1)
                        pool.wait_ge(sin_ready, b + 1)
                        if not early:
                            pool.wait_ge(rest_ready, b - 1)
                        pool.tensor_tensor(rot[p][:, 0:2, :], cosd[:, 0:2, :], sind[:, 0:2, :], ALU.add)
                        pool.tensor_tensor(rot[p][0:64, 2, :], cosd[0:64, 2, :], sind[0:64, 2, :],
                                           ALU.add).then_inc(rot_ready, 1)
                    pool.wait_ge(w_loaded, 7 * 16)
                    turn_positions(0, 0, True, True)
                    turn_positions(1, 1, False, True)
                    with pool.Fori(1, B // 2) as i:
                        for p in range(2):
                            turn_positions(i * 2 + p, p, False, False)


def attention(net, layer, scratch, values, gates, out):
    nc = net.nc
    tag = f"L{layer}_attn"
    U = B * NKV
    scale = float(HD) ** -0.5
    order = [("A", 0), ("B", 0), ("A", 1), ("B", 1), ("C", 0), ("A", 2), ("B", 2), ("A", 3), ("B", 3), ("C", 2)]
    place = {("A", r): r for r in range(GR)} | {("B", r): GR + r for r in range(GR)} | {("C", 0): 8, ("C", 2): 9}
    UN = len(order)
    TURN_AT, WEIGH_AT = 3, (4, 6, 8, 9)
    with ExitStack() as ctx:
        sb = lambda name, shape, dt=F32: net.sb(f"{tag}_{name}", shape, dt, ctx)
        sem = lambda name: net.sem(f"{tag}_{name}")
        q = [sb(f"q{j}", [P, GR, S], BF16) for j in range(4)]
        k = [sb(f"k{j}", [P, S], BF16) for j in range(4)]
        v = [sb(f"v{j}", [P, TB, 32]) for j in range(4)]
        probs = [sb(f"probs{j}", [P, UN, S]) for j in range(2)]
        ident16 = sb("ident16", [P, P], BF16)
        causal = sb("causal", [P, P])
        causal16 = sb("causal16", [P, P], BF16)
        top = [sb(f"top{j}", [P, GR, TB]) for j in range(2)]
        top_rows = [sb(f"top_rows{j}", [GR * TB, 2, P], BF16) for j in range(2)]
        oT = [sb(f"oT{j}", [P, S]) for j in range(2)]
        inv = sb("inv", [P, TB, GR])
        ps_m = net.ps(f"{tag}_ps_m", [P, 2, S], F32, ctx)
        ps_t = net.ps(f"{tag}_ps_t", [P, 2, S], F32, ctx)
        ps_v = net.ps(f"{tag}_ps_v", [P, 2, S], F32, ctx)
        ps_o = net.ps(f"{tag}_ps_o", [P, TB, P], F32, ctx)
        ps_top = net.ps(f"{tag}_ps_top", [P, S], F32, ctx)
        const_in = sem("const_in")
        const_ready = sem("const_ready")
        v_const = sem("v_const")
        loaded = [sem(f"loaded{j}") for j in range(4)]
        tops_in = [sem(f"tops_in{j}") for j in range(4)]
        m_scored = sem("m_scored")
        m_reduced = sem("m_reduced")
        top_turned = sem("top_turned")
        top_hi = sem("top_hi")
        top_ready = sem("top_ready")
        t_scored = sem("t_scored")
        exped = sem("exped")
        v_ready = sem("v_ready")
        probs_ready = sem("probs_ready")
        pv_done = sem("pv_done")
        oT_ready = sem("oT_ready")
        o_turned = sem("o_turned")
        inv_step = sem("inv_step")
        o_done = sem("o_done")

        with nc.Block() as block:
            @block.sync
            def _(sp):
                sp.dma_start(causal[:, :], net.dram["c_causal"]).then_inc(const_in, 16)

                def load(u, j):
                    for at, n in ((0, 3), (3, 2), (5, 1)):
                        sp.dma_start(q[j][at * HD:(at + n) * HD, :, :],
                                     scratch["q"][ds(u, 1), 0:n * HD * GR, :].rearrange("u (p h) t -> (u p) h t", h=GR)
                                     ).then_inc(loaded[j], 16)
                    for part, at, n in ((0, 0, 3), (1, 3, 2), (2, 5, 1)):
                        sp.dma_start(k[j][at * HD:(at + n) * HD, :],
                                     scratch["k"][part:part + 1, ds(u * HD, HD), :].broadcast_to([n, HD, S])
                                     ).then_inc(loaded[j], 16)

                def put_tops(u, j, first):
                    sp.wait_ge(top_ready, u + 1)
                    net.go_on(sp)
                    if not first:
                        sp.wait_ge(t_scored, (u - 3) * UN)
                    for a in range(2):
                        sp.dma_start(q[j][6 * HD + a:6 * HD + a + 1, :, :], top_rows[j % 2][:, a, :]
                                     ).then_inc(tops_in[j], 16)

                def unit(u, j, more=True):
                    if more:
                        sp.wait_ge(t_scored, u * UN)
                        net.go_on(sp)
                        load(u + 3, (j + 3) % 4)
                    put_tops(u + 1, (j + 1) % 4, False)
                for j in range(4):
                    load(j, j)
                for u in range(2):
                    put_tops(u, u, True)
                for u in range(1, 5):
                    sp.wait_ge(t_scored, u * UN)
                    load(u + 3, (u + 3) % 4)
                    put_tops(u + 1, (u + 1) % 4, u < 3)
                with sp.Fori(1, U // 4 - 1) as i:
                    for j in range(1, 5):
                        unit(i * 4 + j, j % 4)
                unit(U - 3, 1, False)
                unit(U - 2, 2, False)

            @block.gpsimd
            def _(pool):
                pool.wait_ge(v_const, 12)

                def keep_causal(block, columns):
                    return pool.affine_select(out=block, in_=block, compare_op=ALU.is_ge, fill=0.0, base=0,
                                              pattern=columns, channel_multiplier=-1)

                def unit(u, j, first):
                    if not first:
                        pool.wait_ge(pv_done, u - 3)
                    pool.tensor_copy(v[j][:, :, 0:HD], values[:, ds(u, 1), :, :]).then_inc(v_ready, 1)
                    pool.wait_ge(exped, u * UN + UN)
                    net.go_on(pool)
                    pr = probs[j % 2]
                    keep_causal(pr[:, 0:GR, 0:P], [[0, GR], [1, P]])
                    keep_causal(pr[:, GR:2 * GR, 0:P], [[0, GR], [1, P]])
                    keep_causal(pr[:, GR:2 * GR, 3 * P:4 * P], [[0, GR], [1, P]])
                    keep_causal(pr[:, 8:10, :].rearrange("p c (r q) -> p (c r) q", r=2)[:, :, 0:P],
                                [[0, GR], [1, P]]).then_inc(probs_ready, 1)
                for u in range(4):
                    unit(u, u, True)
                with pool.Fori(1, U // 4) as i:
                    for j in range(4):
                        unit(i * 4 + j, j, False)

            @block.tensor
            def _(pe):
                pe.wait_ge(const_ready, 2)
                pe.wait_ge(v_const, 12)

                def max_unit(u, j, n, first):
                    kind, r = order[n]
                    if n == 0:
                        pe.wait_ge(loaded[j], (u - j) * 24 + 96)
                    if not (first and n < 2):
                        pe.wait_ge(m_reduced, u * UN + n - 1)
                    bank = ps_m[:, n % 2, :]
                    pieces = {"A": [(r, 3, 0)], "B": [(r, 2, 0), (r, 0, 3 * P)], "C": [(r, 1, 0), (r + 1, 1, 2 * P)]}
                    for head, qb, at in pieces[kind]:
                        width = (qb + 1) * P
                        pe.matmul(bank[:, at:at + width], q[j][0:96, head, qb * P:(qb + 1) * P], k[j][0:96, 0:width],
                                  start=True, stop=False)
                        last = pe.matmul(bank[:, at + width - P:at + width], ident16[:, :], causal16[:, :],
                                         start=False, stop=True)
                    last.then_inc(m_scored, 1)

                def exp_unit(u, j, n, first):
                    kind, r = order[n]
                    if n == 0:
                        pe.wait_ge(tops_in[j], (u - j) * 8 + 32)
                    if not (first and n < 2):
                        pe.wait_ge(exped, u * UN + n - 1)
                    bank = ps_t[:, n % 2, :]
                    pieces = {"A": [(r, 0, 0)], "B": [(r, 1, 0), (r, 3, 3 * P)], "C": [(r, 2, 0), (r + 1, 2, 2 * P)]}
                    for head, kb, at in pieces[kind]:
                        width = (TB - kb) * P
                        last = pe.matmul(bank[:, at:at + width], k[j][0:98, kb * P:(kb + 1) * P],
                                         q[j][0:98, head, kb * P:S], start=True, stop=True)
                    last.then_inc(t_scored, 1)

                def turn_tops(u, j):
                    pe.wait_ge(m_reduced, u * UN + UN)
                    pe.transpose(ps_top[0:GR * TB, 0:P], top[j % 2][:, :, :].rearrange("p h t -> p (h t)"),
                                 net.ident[:, :]).then_inc(top_turned, 1)

                def weigh_values(u, j, kb, first):
                    if kb == 0:
                        pe.wait_ge(probs_ready, u + 1)
                        pe.wait_ge(v_ready, u + 1)
                        if not first:
                            pe.wait_ge(oT_ready, u - 1)
                    pr = probs[j % 2]
                    for r in range(GR):
                        src = {0: pr[:, r, :], 1: pr[:, GR + r, 0:3 * P],
                               2: pr[:, 8 + r // 2, (r % 2) * 2 * P:(r % 2 + 1) * 2 * P],
                               3: pr[:, GR + r, 3 * P:4 * P]}[kb]
                        last = pe.matmul(ps_v[32 * r:32 * r + 32, j % 2, kb * P:S], v[j][:, kb, :], src,
                                         start=kb == 0, stop=kb == TB - 1, tile_position=(0, 32 * r))
                    if kb == TB - 1:
                        last.then_inc(pv_done, 1)

                def turn_out(u, j, first):
                    pe.wait_ge(oT_ready, u + 1)
                    if not first:
                        pe.wait_ge(o_done, u)
                    for t in range(TB):
                        last = pe.transpose(ps_o[:, t, :], oT[j % 2][:, t * P:(t + 1) * P], net.ident[:, :])
                    last.then_inc(o_turned, 1)

                def unit(u, j, maxima=True, tops=True, weigh=True, turn=True, first=False, first_turn=False, first_weigh=False):
                    for n in range(UN):
                        if maxima:
                            max_unit(u + 2, (j + 2) % 4, n, False)
                        exp_unit(u, j, n, first)
                        if n == 0 and tops:
                            turn_tops(u + 1, (j + 1) % 4)
                        if n == TURN_AT and turn:
                            turn_out(u - 2, (j + 2) % 4, first_turn)
                        if n in WEIGH_AT and weigh:
                            weigh_values(u - 1, (j + 3) % 4, WEIGH_AT.index(n), first_weigh)
                for u in range(2):
                    for n in range(UN):
                        max_unit(u, u, n, u == 0)
                    if u == 0:
                        turn_tops(0, 0)
                unit(0, 0, weigh=False, turn=False, first=True)
                unit(1, 1, turn=False, first_weigh=True)
                unit(2, 2, first_turn=True, first_weigh=True)
                unit(3, 3)
                unit(4, 0)
                with pe.Fori(1, U // 4 - 1) as i:
                    for j in range(1, 5):
                        unit(i * 4 + j, j % 4)
                unit(U - 3, 1)
                unit(U - 2, 2, maxima=False)
                unit(U - 1, 3, maxima=False, tops=False)
                turn_out(U - 2, 2, False)
                for kb in range(TB):
                    weigh_values(U - 1, 3, kb, False)
                turn_out(U - 1, 3, False)

            @block.scalar
            def _(act):
                def exponentials(u, j, first, mid=None):
                    if not first:
                        act.wait_ge(pv_done, u - 1)
                    for n, unit in enumerate(order):
                        act.wait_ge(t_scored, u * UN + n + 1)
                        act.activation(probs[j % 2][:, place[unit], :], ps_t[:, n % 2, :], ACT.Exp,
                                       scale=scale).then_inc(exped, 1)

                def copy_out(u, j, first):
                    act.wait_ge(pv_done, u + 1)
                    if not first:
                        act.wait_ge(o_turned, u - 1)
                    act.activation(oT[j % 2][:, :], ps_v[:, j % 2, :], ACT.Copy).then_inc(oT_ready, 1)
                exponentials(0, 0, True)
                exponentials(1, 1, True)
                copy_out(0, 0, True)
                exponentials(2, 2, False)
                copy_out(1, 1, True)
                exponentials(3, 3, False)
                copy_out(2, 2, False)
                with act.Fori(1, U // 4) as i:
                    for j in range(4):
                        exponentials(i * 4 + j, j, False)
                        copy_out(i * 4 + j - 1, (j + 3) % 4, False)
                copy_out(U - 1, 3, False)

            @block.vector
            def _(dve):
                for j in range(4):
                    dve.memset(k[j][96:98, :], -1.0).then_inc(v_const, 1)
                    dve.memset(v[j][:, :, :], 0.0).then_inc(v_const, 1)
                dve.wait_ge(v_const, 8)
                for j in range(4):
                    dve.memset(v[j][:, :, HD:HD + 1], 1.0).then_inc(v_const, 1)
                dve.tensor_copy(ident16[:, :], net.ident[:, :]).then_inc(const_ready, 1)
                dve.wait_ge(const_in, 16)
                dve.tensor_copy(causal16[:, :], causal[:, :]).then_inc(const_ready, 1)

                def reduce(u, j, n, first):
                    kind, r = order[n]
                    if n == 0 and not first:
                        dve.wait_ge(top_turned, u - 1)
                    dve.wait_ge(m_scored, u * UN + n + 1)
                    bank, t = ps_m[:, n % 2, :], top[j % 2]
                    if kind == "A":
                        last = dve.tensor_reduce(t[:, r, 3:4], bank, AX.X, ALU.max)
                    elif kind == "B":
                        dve.tensor_reduce(t[:, r, 2:3], bank[:, 0:3 * P], AX.X, ALU.max)
                        last = dve.tensor_reduce(t[:, r, 0:1], bank[:, 3 * P:4 * P], AX.X, ALU.max)
                    else:
                        last = dve.tensor_reduce(t[:, r:r + 2, 1], bank.rearrange("p (h k) -> p h k", h=2),
                                                 AX.X, ALU.max)
                    last.then_inc(m_reduced, 1)

                def split_tops(u, j, first):
                    dve.wait_ge(top_turned, u + 1)
                    if not first:
                        dve.wait_ge(tops_in[(j + 2) % 4], (u - 2 - (j + 2) % 4) * 8 + 32)
                    rows, src = top_rows[j % 2], ps_top[0:GR * TB, 0:P]
                    dve.tensor_copy(rows[:, 0, :], src).then_inc(top_hi, 1)
                    dve.wait_ge(top_hi, u + 1)
                    dve.tensor_tensor(rows[:, 1, :], src, rows[:, 0, :], ALU.subtract).then_inc(top_ready, 1)

                def normalise(u, first):
                    dve.wait_ge(o_turned, u + 1)
                    heads = ps_o[:, :, :].rearrange("p t (h c) -> p t h c", h=GR)
                    n = 2 if layer == 3 else 1
                    if not first:
                        dve.wait_ge(o_done, u)
                    dve.reciprocal(inv[:, :, :], heads[:, :, :, HD]).then_inc(inv_step, 1)
                    dve.wait_ge(inv_step, u * n + 1)
                    if layer == 3:
                        dve.tensor_tensor(inv[:, :, :], inv[:, :, :], gates[:, ds(u, 1), :, :].rearrange(
                            "p u t h -> p (u t) h"), ALU.mult).then_inc(inv_step, 1)
                        dve.wait_ge(inv_step, u * n + 2)
                    dve.tensor_tensor(out[:, ds(u, 1), :, :].rearrange("p u t (h d) -> p (u t) h d", h=GR),
                                      heads[:, :, :, 0:HD],
                                      inv[:, :, :].unsqueeze(3).to_broadcast([P, TB, GR, HD]),
                                      ALU.mult).then_inc(o_done, 1)

                def unit(u, j, maxima=True, tops=True, turn=True, first_tops=False, first_norm=False):
                    for n in range(UN):
                        if maxima:
                            reduce(u + 2, (j + 2) % 4, n, False)
                        if n == 1 and tops:
                            split_tops(u + 1, (j + 1) % 4, first_tops)
                        if n == TURN_AT + 1 and turn:
                            normalise(u - 2, first_norm)
                for u in range(2):
                    for n in range(UN):
                        reduce(u, u, n, True)
                    if u == 0:
                        split_tops(0, 0, True)
                unit(0, 0, turn=False, first_tops=True)
                unit(1, 1, turn=False)
                unit(2, 2, first_norm=True)
                unit(3, 3)
                unit(4, 0)
                with dve.Fori(1, U // 4 - 1) as i:
                    for j in range(1, 5):
                        unit(i * 4 + j, j % 4)
                unit(U - 3, 1)
                unit(U - 2, 2, maxima=False)
                unit(U - 1, 3, maxima=False, tops=False)
                normalise(U - 2, False)
                normalise(U - 1, False)


def project_out(net, layer, heads):
    nc = net.nc
    tag = f"L{layer}_wo"
    with ExitStack() as ctx:
        sb = lambda name, shape, dt=F32: net.sb(f"{tag}_{name}", shape, dt, ctx)
        sem = lambda name: net.sem(f"{tag}_{name}")
        w_in = sb("w_in", [P, KC, C])
        w = sb("w", [P, KC, C]) if layer == 3 else w_in
        rows = [sb(f"rows{p}", [P, TB, C]) for p in range(2)]
        rowsT = [sb(f"rowsT{p}", [P, KC, S]) for p in range(2)]
        turned = net.ps(f"{tag}_turned", [P, KC, S], F32, ctx)
        w_ps = net.ps(f"{tag}_w_ps", [P, KC, C], F32, ctx)
        proj = [net.ps(f"{tag}_proj{p}", [P, TB, C], F32, ctx) for p in range(2)]
        w_loaded, w_turned, w_ready = sem("w_loaded"), sem("w_turned"), sem("w_ready")
        rows_ready = sem("rows_ready")
        turned_ready = sem("turned_ready")
        copied = sem("copied")
        projected = sem("projected")
        added = sem("added")
        stats_step = sem("stats_step")
        with nc.Block() as block:
            @block.sync
            def _(sp):
                src = net.dram["L2_attn_W_o" if layer == 2 else "L3_attn_Wo"]
                sp.dma_start(w_in[:, :, :], src.rearrange("(k p) c -> p k c", p=P)).then_inc(w_loaded, 16)

            @block.tensor
            def _(pe):
                pe.wait_ge(w_loaded, 16)
                if layer == 3:
                    for k in range(KC):
                        for j in range(KC):
                            last = pe.transpose(w_ps[:, k, j * P:(j + 1) * P], w_in[:, j, k * P:(k + 1) * P],
                                                net.ident[:, :])
                    last.then_inc(w_turned, 1)
                    pe.wait_ge(w_ready, 1)

                def turn(b, p, first):
                    pe.wait_ge(rows_ready, b + 1)
                    if not first:
                        pe.wait_ge(copied, b)
                    for c in range(KC):
                        for t in range(TB):
                            last = pe.transpose(turned[:, c, t * P:(t + 1) * P], rows[p][:, t, c * P:(c + 1) * P],
                                                net.ident[:, :])
                    last.then_inc(turned_ready, 1)

                def project(b, p, first):
                    pe.wait_ge(copied, b + 1)
                    if not first:
                        pe.wait_ge(added, b - 1)
                    for t in range(TB):
                        for k in range(KC):
                            last = pe.matmul(proj[p][:, t, :], rowsT[p][:, k, t * P:(t + 1) * P], w[:, k, :],
                                             start=k == 0, stop=k == KC - 1)
                    last.then_inc(projected, 1)
                turn(0, 0, True)
                turn(1, 1, False)
                project(0, 0, True)
                turn(2, 0, False)
                project(1, 1, True)
                with pe.Fori(1, B // 2 - 1) as i:
                    for p in range(2):
                        turn(i * 2 + p + 1, 1 - p, False)
                        project(i * 2 + p, p, False)
                turn(B - 1, 1, False)
                project(B - 2, 0, False)
                project(B - 1, 1, False)

            @block.scalar
            def _(act):
                def gather(b, p, first):
                    if not first:
                        act.wait_ge(turned_ready, b - 1)
                    act.activation(rows[p][:, :, :].rearrange("p t (g c) -> p g t c", g=NKV),
                                   heads[:, ds(b * NKV, NKV), :, :], ACT.Copy).then_inc(rows_ready, 1)

                def copy(b, p, first):
                    act.wait_ge(turned_ready, b + 1)
                    if not first:
                        act.wait_ge(projected, b - 1)
                    act.activation(rowsT[p][:, :, :], turned[:, :, :], ACT.Copy).then_inc(copied, 1)
                gather(0, 0, True)
                gather(1, 1, True)
                copy(0, 0, True)
                copy(1, 1, True)
                with act.Fori(1, B // 2) as i:
                    for p in range(2):
                        gather(i * 2 + p, p, False)
                        copy(i * 2 + p, p, False)

            @block.vector
            def _(dve):
                if layer == 3:
                    dve.wait_ge(w_turned, 1)
                    dve.tensor_copy(w[:, :, :], w_ps[:, :, :]).then_inc(w_ready, 1)
                with dve.Fori(0, B // 2) as i:
                    for p in range(2):
                        b = i * 2 + p
                        dve.wait_ge(projected, b + 1)
                        x_b = net.x[:, ds(b * TB, TB), :]
                        dve.tensor_tensor(x_b, proj[p][:, :, :], x_b, ALU.add).then_inc(added, 1)
                        dve.wait_ge(added, b + 1)
                        token_stats(net, dve, b, stats_step)


def attention_block(net, layer):
    with ExitStack() as ctx:
        values = net.sb(f"L{layer}_values", [P, B * NKV, TB, HD], F32, ctx)
        heads = net.sb(f"L{layer}_heads", [P, B * NKV, TB, GR * HD], F32, ctx)
        gates = net.sb(f"L{layer}_gates", [P, B * NKV, TB, GR], F32, ctx) if layer == 3 else None
        scratch = {"q": net.nc.dram_tensor(f"L{layer}_q_parts", (B * NKV, 3 * GR * HD, S), BF16).ap(),
                   "k": net.nc.dram_tensor(f"L{layer}_k_parts", (3, B * NKV * HD, S), BF16).ap()}
        with ExitStack() as early:
            net.hold_channels(f"L{layer}_attn", early)
            layer_norm(net, f"L{layer}_ln", stats_known=layer == 3)
            project_qkv(net, layer, scratch, values, gates)
        attention(net, layer, scratch, values, gates, heads)
        project_out(net, layer, heads)


BITS = 31


class Tables:

    def __init__(self, net, tag, ctx):
        self.take = net.sb(f"{tag}_take", [P, SLOT_TILES], I32, ctx)
        self.give = net.sb(f"{tag}_give", [P, SLOT_TILES], I32, ctx)
        self.weight = net.sb(f"{tag}_weight", [P, SLOT_TILES], F32, ctx)
        self.expert = net.sb(f"{tag}_expert", [P, SLOT_TILES], I32, ctx)


def route(net, layer, tables, early_loads=(), shared=None):
    nc = net.nc
    tag = f"L{layer}_route"
    with ExitStack() as ctx:
        sb = lambda name, shape, dt=F32: net.sb(f"{tag}_{name}", shape, dt, ctx)
        sem = lambda name: net.sem(f"{tag}_{name}")
        by_tile = [P, NT, E]
        by_expert = [P, E, NT]
        lanes = [sb(f"lanes{p}", [P, 2, P]) for p in range(2)]
        hits = [sb(f"hits{p}", [P, 2, SLOT_TILES]) for p in range(2)]
        valueds = sb("valueds", [P, 2, 2, 2, SLOT_TILES])
        valued = [valueds[:, p] for p in range(2)]
        w_in = lanes[0][0:E, :, :].rearrange("e k c -> e (k c)")
        tile_cmp = valueds[:, :, :, :, :].rearrange("p a b c t -> p (a b c t)").rearrange(
            "p (t e) -> p t e", e=E)
        w = sb("w", [P, KC, 32])
        z_rows = ([net.xT[:, 0, 4 * h * S:(4 * h + 1) * S] for h in range(2)] if shared is None else
                  [shared.active[1][:, h, :] for h in range(2)])
        late_at = 0

        def late(name, shape):
            nonlocal late_at
            if layer == 2:
                return sb(name, shape)[:, :, :]
            n = shape[1] * shape[2]
            late_at += n
            return net.xT[:, 1, late_at - n:late_at].rearrange("p (a b) -> p a b", b=shape[2])

        bias_z = sb("bias_z", [P, E])
        bias_row = sb("bias_row", [P, E])
        z, sig, key, first, second, chosen, tmp, weights = (
            late(n, by_tile) for n in ("z", "sig", "key", "first", "second", "chosen", "tmp", "weights"))
        best, where_, total, slot, values, token1 = (
            sb("best", [P, NT]), sb("where", [P, NT]), sb("total", [P, NT]),
            sb("slot", [P, 2, NT]), sb("values", [P, NT, 2, 2]), sb("token1", [P, NT]))
        slot_i, high_i, low_i = (sb(n, [P, 2, NT], I32) for n in ("slot_i", "high_i", "low_i"))
        high, low = sb("high", [P, 2, NT]), sb("low", [P, 2, NT])
        chosen16 = sb("chosen16", by_tile, BF16)
        before, before16 = sb("before", [P, P]), sb("before16", [P, P], BF16)
        ones16, ones = sb("ones16", [P, P], BF16), sb("ones", [P, NT])
        lane, expert_no, tile_start = sb("lane", [P, P]), sb("expert_no", [P, E]), sb("tile_start", [P, SLOT_TILES])
        less8 = sb("less8", [P, E])
        per_tile, upto, ranks = late("per_tile", by_expert), late("upto", by_expert), late("ranks", by_expert)
        small = sb("small", [P, 8, E])
        padded_i = sb("padded_i", [P, E], I32)
        tile_exp = sb("tile_exp", [P, SLOT_TILES])
        table = sb("table", [P, 2, SLOT_TILES])
        empty = sb("empty", [P, SLOT_TILES])
        lane_col = sb("lane_col", [P, 1])
        if layer == 2:
            bits = sb("bits", [P, BITS, E], I32)
            floor_, candidate, gain = (sb(n, [P, E], I32) for n in ("floor", "candidate", "gain"))
            rated, over, level = (t[:, :, :].rearrange("p t e -> p (t e)").rearrange("p (e t) -> p e t", e=E)
                                  for t in (z, sig, key))
            level16 = before[:, :].bitcast(BF16).rearrange("p (e t) -> p e t", e=E)
            count16 = sb("count16", [P, E], BF16)
        ps_wide = net.ps(f"{tag}_ps_wide", [P, 2, S], F32, ctx)
        ps_out = net.ps(f"{tag}_ps_out", [P, 2, 2, S], F32, ctx)
        ps_count = net.ps(f"{tag}_ps_count", [P, S], F32, ctx)
        ps_tab = net.ps(f"{tag}_ps_tab", [P, S], F32, ctx)
        NP = NT * E
        if shared is not None:
            shared.banks(ps_wide, ps_out, ctx)
        loaded = sem("loaded")
        early_loaded = sem("early_loaded")
        w_turned, w_ready = sem("w_turned"), sem("w_ready")
        w_zeroed = sem("w_zeroed")
        z_ready = sem("z_ready")
        z_copied = sem("z_copied")
        z_turned = sem("z_turned")
        z_in = sem("z_in")
        const_ready = sem("const_ready")
        exp_done = sem("exp_done")
        step = sem("step")
        loop_step = sem("loop_step")
        counts_asked, counted = sem("counts_asked"), sem("counted")
        level_asked, level_counted = sem("level_asked"), sem("level_counted")
        hits_ready = sem("hits_ready")
        sides_ready = sem("sides_ready")
        sides_used = sem("sides_used")
        dram = net.dram
        w_name = "L2_ffn_proj_w" if layer == 2 else "L3_ffn_gate_w"
        b_name = "L2_ffn_proj_b" if layer == 2 else "L3_ffn_gate_b"
        e_name = "L2_ffn_expert_bias" if layer == 2 else "L3_ffn_expert_biases"
        n_loaded = 7 + (1 if layer == 2 else 0)

        with nc.Block() as block:
            @block.sync
            def _(sp):
                if layer == 2:
                    sp.dma_start(w_in[:, :], dram[w_name]).then_inc(loaded, 16)
                    sp.dma_start(bits[:, :, :], dram["c_bits"]).then_inc(loaded, 16)
                else:
                    sp.wait_ge(w_zeroed, 1)
                    sp.dma_start(w[:, :, 0:E], dram[w_name].rearrange("(k p) e -> p k e", p=P)).then_inc(loaded, 16)
                sp.dma_start(bias_z[:, :], dram[b_name].partition_broadcast(P)).then_inc(loaded, 16)
                sp.dma_start(bias_row[:, :], dram[e_name].partition_broadcast(P)).then_inc(loaded, 16)
                sp.dma_start(before[:, :], dram["c_before"]).then_inc(loaded, 16)
                sp.dma_start(expert_no[:, :], dram["c_expert"]).then_inc(loaded, 16)
                sp.dma_start(tile_start[:, :], dram["c_tilestart"]).then_inc(loaded, 16)
                sp.dma_start(lane[:, :], dram["c_lane"]).then_inc(loaded, 16)
                for to, source in early_loads:
                    sp.dma_start(to, source).then_inc(early_loaded, 16)
                if shared is not None:
                    shared.load(sp)
                if early_loads:
                    sp.wait_ge(early_loaded, len(early_loads) * 16)

            @block.tensor
            def _(pe):
                pe.wait_ge(loaded, 16 * n_loaded)
                if layer == 2:
                    for k in range(KC):
                        last = pe.transpose(ps_count[:, k * E:(k + 1) * E], w_in[:, k * P:(k + 1) * P],
                                            net.ident[0:E, 0:E])
                    last.then_inc(w_turned, 1)
                    pe.wait_ge(w_ready, 1)

                for h in range(2):
                    for k in range(KC):
                        for g in range(4):
                            b = h * 4 + g
                            last = pe.matmul(ps_wide[32 * g:32 * g + 32, h, :], w[:, k, :],
                                             net.xT[:, k, b * S:(b + 1) * S], start=k == 0, stop=k == KC - 1,
                                             tile_position=(0, 32 * g))
                    last.then_inc(z_ready, 1)
                for h in range(2):
                    pe.wait_ge(z_copied, h + 1)
                    for t in range(TB):
                        last = pe.transpose(ps_out[:, 0, h, t * P:(t + 1) * P], z_rows[h][:, t * P:(t + 1) * P],
                                            net.ident[:, :])
                last.then_inc(z_turned, 1)

                def count_pairs():
                    pe.wait_ge(counts_asked, 1)
                    pairs = chosen16[:, :, :].rearrange("p t e -> p (t e)")
                    pe.matmul(ps_count[:, 0:NP], before16[:, :], pairs, start=True, stop=True)
                    pe.matmul(ps_count[:, NP:2 * NP], ones16[:, :], pairs, start=True, stop=True
                              ).then_inc(counted, 1)

                def count_over(i):
                    pe.wait_ge(level_asked, i + 1)
                    net.go_on(pe)
                    pe.matmul(ps_count[:, 0:E], ones16[:, :], count16[:, :], start=True, stop=True
                              ).then_inc(level_counted, 1)

                def count_level():
                    pe.wait_ge(level_asked, BITS + 2)
                    pairs = level16[:, :, :].rearrange("p e t -> p (e t)")
                    pe.matmul(ps_tab[:, 0:NP], before16[:, :], pairs, start=True, stop=True)
                    pe.matmul(ps_tab[:, NP:2 * NP], ones16[:, :], pairs, start=True, stop=True
                              ).then_inc(level_counted, 1)

                def place(t, p, first, last_one):
                    pe.wait_ge(sides_ready, t + 1)
                    for c in range(2):
                        last = pe.matmul(ps_tab[:, 0:2 * SLOT_TILES], lanes[p][:, c, :], valued[p][:, c],
                                         start=first and c == 0, stop=last_one and c == 1)
                    last.then_inc(sides_used, 1)
                if shared is None:
                    count_pairs()
                    place(0, 0, True, False)
                    with pe.Fori(0, NT // 2 - 1) as i:
                        place(i * 2 + 1, 1, False, False)
                        place(i * 2 + 2, 0, False, False)
                    place(NT - 1, 1, False, True)
                else:
                    pe.wait_ge(z_in, 1)
                    shared.turn_weights(pe)
                    count_pairs()
                    shared.up(pe, 0, 0, True)
                    shared.round(pe, 0, 0, True, lambda slot: count_over(slot))
                    shared.round(pe, 1, 1, True, lambda slot: count_over(8 + slot))
                    shared.round(pe, 2, 0, False, lambda slot: count_over(16 + slot))
                    shared.round(pe, 3, 1, False, lambda slot: count_over(24 + slot))
                    count_level()
                    for b in range(4, B - 1):
                        def place_one(slot):
                            t = (b - 4) * 8 + slot
                            place(t, t % 2, t == 0, False)
                        shared.round(pe, b, b % 2, False, place_one)

                    def place_two(slot):
                        for t in (24 + 2 * slot, 25 + 2 * slot):
                            place(t, t % 2, False, t == NT - 1)
                    shared.down(pe, B - 1, 1, False, place_two)

            @block.scalar
            def _(act):
                for h in range(2):
                    act.wait_ge(z_ready, h + 1)
                    act.activation(z_rows[h], ps_wide[:, h, :], ACT.Copy).then_inc(z_copied, 1)
                act.wait_ge(z_in, 1)
                act.activation(sig[:, :, :], z[:, :, :], ACT.Exp, scale=-1.0).then_inc(exp_done, 1)
                if shared is not None:
                    shared.activate(act)

            if shared is not None:
                @block.gpsimd
                def _(pool):
                    shared.add(pool)

            @block.vector
            def _(dve):
                s = Order(dve, step)
                did, wait = s.did, s.wait
                dve.memset(w[:, :, :], 0.0).then_inc(w_zeroed, 1)
                if layer == 2:
                    dve.wait_ge(w_zeroed, 1)
                    dve.wait_ge(w_turned, 1)
                    dve.tensor_copy(w[:, :, 0:E], ps_count[:, 0:KC * E].rearrange("p (k e) -> p k e", k=KC)
                                    ).then_inc(w_ready, 1)
                dve.wait_ge(loaded, 16 * n_loaded)
                did(dve.memset(ones[:, :], 1.0))
                did(dve.memset(ones16[:, :], 1.0))
                did(dve.tensor_copy(before16[:, :], before[:, :]))
                did(dve.tensor_scalar(less8[:, :], expert_no[:, :], float(-E), None, ALU.add))
                def over_experts(column):
                    return column.unsqueeze(2).to_broadcast(by_tile)

                def over_tiles(row):
                    return row.unsqueeze(1).to_broadcast(by_tile)

                def by_e(row):
                    return row.unsqueeze(2).to_broadcast(by_expert)

                did(dve.tensor_reduce(total[:, 0:1], before[:, :], AX.X, ALU.add))
                wait()
                did(dve.tensor_scalar(lane_col[:, :], total[:, 0:1], -1.0, float(P - 1), ALU.mult, ALU.add))
                dve.wait_ge(z_turned, 1)
                half = [P, 4, TB, E]
                for h in range(2):
                    last = dve.tensor_tensor(
                        z[:, h * 4 * TB:(h + 1) * 4 * TB, :].rearrange("p (g t) e -> p g t e", g=4),
                        ps_out[:, 0, h, :].rearrange("p (t g e) -> p g t e", g=4, e=32)[:, :, :, 0:E],
                        bias_z[:, :].unsqueeze(1).unsqueeze(1).to_broadcast(half), ALU.add)
                last.then_inc(z_in, 1)
                dve.wait_ge(z_in, 1)
                dve.wait_ge(exp_done, 1)
                did(dve.tensor_scalar(sig[:, :, :], sig[:, :, :], 1.0, None, ALU.add))
                wait()
                did(dve.reciprocal(sig[:, :, :], sig[:, :, :]))
                wait()
                if layer == 2:
                    did(dve.tensor_tensor(sig[:, :, :], sig[:, :, :], over_tiles(bias_row[:, :]), ALU.add))
                    wait()
                    did(dve.tensor_scalar(sig[:, :, :], sig[:, :, :], 1e-12, None, ALU.max))
                    wait()
                    did(dve.tensor_reduce(total[:, :], sig[:, :, :], AX.X, ALU.add))
                    wait()
                    did(dve.reciprocal(total[:, :], total[:, :]))
                    wait()
                    did(dve.tensor_tensor(sig[:, :, :], sig[:, :, :], over_experts(total[:, :]), ALU.mult))
                    wait()
                    did(dve.tensor_copy(key[:, :, :], sig[:, :, :]))
                else:
                    did(dve.tensor_tensor(key[:, :, :], z[:, :, :], over_tiles(bias_row[:, :]), ALU.add))
                for n, one_hot in enumerate((first, second)):
                    wait()
                    did(dve.tensor_reduce(best[:, :], key[:, :, :], AX.X, ALU.max))
                    wait()
                    did(dve.tensor_tensor(tmp[:, :, :], key[:, :, :], over_experts(best[:, :]), ALU.is_equal))
                    wait()
                    did(dve.tensor_tensor(tmp[:, :, :], tmp[:, :, :], over_tiles(less8[:, :]), ALU.mult))
                    wait()
                    did(dve.tensor_reduce(where_[:, :], tmp[:, :, :], AX.X, ALU.min))
                    wait()
                    did(dve.tensor_tensor(one_hot[:, :, :], over_tiles(less8[:, :]), over_experts(where_[:, :]),
                                          ALU.is_equal))
                    if n == 0:
                        wait()
                        did(dve.scalar_tensor_tensor(key[:, :, :], one_hot[:, :, :], -3e38, key[:, :, :],
                                                     ALU.mult, ALU.add))
                wait()
                did(dve.tensor_tensor(chosen[:, :, :], first[:, :, :], second[:, :, :], ALU.add))
                wait()
                dve.tensor_copy(chosen16[:, :, :], chosen[:, :, :]).then_inc(counts_asked, 1)
                did(dve.tensor_tensor(weights[:, :, :], sig[:, :, :], chosen[:, :, :], ALU.mult))
                wait()
                did(dve.tensor_reduce(total[:, :], weights[:, :, :], AX.X, ALU.add))
                wait()
                if layer == 2:
                    did(dve.tensor_scalar(total[:, :], total[:, :], 1e-12, None, ALU.max))
                    wait()
                did(dve.reciprocal(total[:, :], total[:, :]))
                wait()
                did(dve.tensor_tensor(weights[:, :, :], weights[:, :, :], over_experts(total[:, :]), ALU.mult))

                dve.wait_ge(counted, 1)
                did(dve.tensor_copy(per_tile[:, :, :], ps_count[:, NP:2 * NP].rearrange("p (t e) -> p e t", e=E)))
                wait()

                def running(out, per):
                    for e in range(E):
                        last = dve.tensor_tensor_scan(out[:, e, :], ones[:, :], per[:, e, :], 0.0, ALU.mult, ALU.add)
                        did(last)
                running(upto, per_tile)
                wait()
                did(dve.tensor_tensor(ranks[:, :, :], upto[:, :, :], per_tile[:, :, :], ALU.subtract))
                did(dve.tensor_scalar(small[:, 0, :], upto[:, :, NT - 1], float(P - 1), None, ALU.add))
                wait()
                did(dve.tensor_copy(padded_i[:, :], small[:, 0, :]))
                wait()
                did(dve.tensor_scalar(padded_i[:, :], padded_i[:, :], -P, None, ALU.bitwise_and))
                wait()
                did(dve.tensor_copy(small[:, 1, :], padded_i[:, :]))
                wait()
                did(dve.tensor_tensor_scan(small[:, 2, :], ones[:, 0:E], small[:, 1, :], 0.0, ALU.mult, ALU.add))
                wait()
                did(dve.tensor_tensor(small[:, 3, :], small[:, 2, :], small[:, 1, :], ALU.subtract))
                did(dve.tensor_tensor(tile_cmp[:, :, :], tile_start[:, :].unsqueeze(2).to_broadcast([P, SLOT_TILES, E]),
                                      small[:, 2, :].unsqueeze(1).to_broadcast([P, SLOT_TILES, E]), ALU.is_ge))
                wait()
                did(dve.tensor_tensor(ranks[:, :, :], ranks[:, :, :], by_e(small[:, 3, :]), ALU.add))
                did(dve.tensor_reduce(tile_exp[:, :], tile_cmp[:, :, :], AX.X, ALU.add))
                wait()
                did(dve.tensor_scalar(tile_exp[:, :], tile_exp[:, :], float(E - 1), None, ALU.min))
                did(dve.tensor_tensor(key[:, :, :], ps_count[:, 0:NP].rearrange("p (t e) -> p t e", e=E),
                                      ranks[:, :, :].rearrange("p e t -> p t e"), ALU.add))
                wait()
                did(dve.tensor_copy(tables.expert[:, :], tile_exp[:, :]))
                for c, one_hot in enumerate((first, second)):
                    wait()
                    did(dve.tensor_tensor(tmp[:, :, :], key[:, :, :], one_hot[:, :, :], ALU.mult))
                    wait()
                    did(dve.tensor_reduce(slot[:, c, :], tmp[:, :, :], AX.X, ALU.add))
                wait()
                did(dve.tensor_copy(slot_i[:, :, :], slot[:, :, :]))
                wait()
                did(dve.tensor_scalar(high_i[:, :, :], slot_i[:, :, :], 7, None, ALU.logical_shift_right))
                did(dve.tensor_scalar(low_i[:, :, :], slot_i[:, :, :], P - 1, None, ALU.bitwise_and))
                wait()
                did(dve.tensor_copy(high[:, :, :], high_i[:, :, :]))
                did(dve.tensor_copy(low[:, :, :], low_i[:, :, :]))

                if layer == 2:
                    did(dve.scalar_tensor_tensor(rated[:, :, :], chosen[:, :, :].rearrange("p t e -> p e t"), -1.0,
                                                 weights[:, :, :].rearrange("p t e -> p e t"), ALU.add, ALU.add))
                    did(dve.memset(floor_[:, :], 0))
                    wait()
                    STEPS = 5
                    with dve.Fori(0, BITS) as i:
                        o = Order(dve, loop_step, i * STEPS)
                        o.did(dve.tensor_tensor(candidate[:, :], floor_[:, :], bits[:, ds(i, 1), :], ALU.bitwise_or))
                        o.wait()
                        o.did(dve.tensor_tensor(over[:, :, :], rated[:, :, :], by_e(candidate[:, :].bitcast(F32)),
                                                ALU.is_ge))
                        o.wait()
                        with nc.allow_low_precision(reason="counts up to 32 are exact"):
                            dve.tensor_reduce(count16[:, :], over[:, :, :], AX.X, ALU.add).then_inc(level_asked, 1)
                        dve.wait_ge(level_counted, i + 1)
                        o.did(dve.tensor_scalar(small[:, 4, :], ps_count[:, 0:E], float(CAP), None, ALU.is_ge))
                        o.wait()
                        o.did(dve.tensor_tensor(gain[:, :], small[:, 4, :], bits[:, ds(i, 1), :], ALU.mult))
                        o.wait()
                        o.did(dve.tensor_tensor(floor_[:, :], floor_[:, :], gain[:, :], ALU.bitwise_or))
                        o.wait()
                        assert o.n == STEPS
                    floor_f = by_e(floor_[:, :].bitcast(F32))
                    did(dve.tensor_tensor(over[:, :, :], rated[:, :, :], floor_f, ALU.is_gt))
                    did(dve.tensor_tensor(level[:, :, :], rated[:, :, :], floor_f, ALU.is_equal))
                    wait()
                    with nc.allow_low_precision(reason="counts up to 32 are exact"):
                        dve.tensor_reduce(count16[:, :], over[:, :, :], AX.X, ALU.add).then_inc(level_asked, 1)
                    dve.tensor_copy(level16[:, :, :], level[:, :, :]).then_inc(level_asked, 1)
                    dve.wait_ge(level_counted, BITS + 1)
                    did(dve.tensor_scalar(small[:, 5, :], ps_count[:, 0:E], -1.0, float(CAP), ALU.mult, ALU.add))
                    dve.wait_ge(level_counted, BITS + 2)
                    did(dve.tensor_copy(per_tile[:, :, :], ps_tab[:, NP:2 * NP].rearrange("p (e t) -> p e t", e=E)))
                    wait()
                    running(upto, per_tile)
                    wait()
                    did(dve.tensor_tensor(upto[:, :, :], upto[:, :, :], per_tile[:, :, :], ALU.subtract))
                    wait()
                    did(dve.tensor_tensor(upto[:, :, :], upto[:, :, :], ps_tab[:, 0:NP].rearrange(
                        "p (e t) -> p e t", e=E), ALU.add))
                    wait()
                    did(dve.tensor_tensor(upto[:, :, :], upto[:, :, :], by_e(small[:, 5, :]), ALU.is_lt))
                    wait()
                    did(dve.tensor_tensor(level[:, :, :], level[:, :, :], upto[:, :, :], ALU.mult))
                    wait()
                    did(dve.tensor_tensor(over[:, :, :], over[:, :, :], level[:, :, :], ALU.add))
                    wait()
                    did(dve.tensor_tensor(weights[:, :, :], weights[:, :, :], over[:, :, :].rearrange(
                        "p e t -> p t e"), ALU.mult))
                for c, one_hot in enumerate((first, second)):
                    wait()
                    did(dve.tensor_tensor(tmp[:, :, :], weights[:, :, :], one_hot[:, :, :], ALU.mult))
                    wait()
                    did(dve.tensor_reduce(values[:, :, c, 1], tmp[:, :, :], AX.X, ALU.add))
                wait()

                did(dve.tensor_tensor_scan(token1[:, :], ones[:, :], ones[:, :], -1.0, ALU.mult, ALU.add))
                wait()
                did(dve.tensor_scalar(token1[:, :], token1[:, :], float(P), lane_col[:, 0:1], ALU.mult, ALU.add))
                wait()
                did(dve.tensor_scalar(values[:, :, :, 0], token1[:, :].unsqueeze(2).to_broadcast([P, NT, 2]), 1.0, None,
                                      ALU.add))
                wait()

                def sides(t, p, first_):
                    if not first_:
                        dve.wait_ge(sides_used, t - 1)
                    by_lane, by_slot = [P, 2, P], [P, 2, SLOT_TILES]
                    dve.tensor_tensor(hits[p][:, :, :], lane[:, 0:SLOT_TILES].unsqueeze(1).to_broadcast(by_slot),
                                      high[:, :, ds(t, 1)].to_broadcast(by_slot), ALU.is_equal).then_inc(hits_ready, 1)
                    dve.tensor_tensor(lanes[p][:, :, :], lane[:, :].unsqueeze(1).to_broadcast(by_lane),
                                      low[:, :, ds(t, 1)].to_broadcast(by_lane), ALU.is_equal)
                    dve.wait_ge(hits_ready, t + 1)
                    both = [P, 2, 2, SLOT_TILES]
                    dve.tensor_tensor(valued[p], hits[p][:, :, :].unsqueeze(2).to_broadcast(both),
                                      values[:, ds(t, 1), :, :].rearrange("p t c v -> p (t c) v").unsqueeze(3
                                      ).to_broadcast(both), ALU.mult).then_inc(sides_ready, 1)
                sides(0, 0, True)
                sides(1, 1, True)
                with dve.Fori(1, NT // 2) as i:
                    for p in range(2):
                        sides(i * 2 + p, p, False)
                dve.wait_ge(sides_used, NT)
                did(dve.tensor_copy(table[:, :, :], ps_tab[:, 0:2 * SLOT_TILES].rearrange("p (j t) -> p j t", j=2)))
                wait()
                did(dve.tensor_copy(tables.weight[:, :], table[:, 1, :]))
                did(dve.tensor_scalar(empty[:, :], table[:, 0, :], 0.0, None, ALU.is_equal))
                wait()
                did(dve.tensor_scalar(table[:, 1, :], table[:, 0, :], -1.0, 0.0, ALU.add, ALU.max))
                did(dve.tensor_scalar(tile_exp[:, :], empty[:, :], lane_col[:, 0:1], None, ALU.mult))
                wait()
                did(dve.tensor_copy(tables.take[:, :], table[:, 1, :]))
                did(dve.scalar_tensor_tensor(empty[:, :], empty[:, :], float(TOK), table[:, 1, :],
                                             ALU.mult, ALU.add))
                wait()
                did(dve.tensor_tensor(empty[:, :], empty[:, :], tile_exp[:, :], ALU.add))
                wait()
                did(dve.tensor_copy(tables.give[:, :], empty[:, :]))
                wait()


class SharedExpert:

    SH = 8

    def __init__(self, net, w1, w2, ctx):
        self.net = net
        sb = lambda name, shape: net.sb(f"L2_shared_{name}", shape, F32, ctx)
        sem = lambda name: net.sem(f"L2_shared_{name}")
        self.w1, self.w2 = w1, w2
        self.sh1 = sb("w1", [P, KC, self.SH * P])
        self.sh2 = sb("w2", [P, self.SH, C])
        self.b1 = sb("b1", [P, self.SH])
        self.b2 = sb("b2", [P, C])
        self.active = [sb(f"active{p}", [P, self.SH, S]) for p in range(2)]
        ring = [self.active[0][:, 2 * j:2 * j + 2, :] for j in range(4)]
        self.up_in = [ring[p].rearrange("p a (b c) -> p (a b) c", c=C) for p in range(2)]
        self.down_in = [ring[2 + p] for p in range(2)]
        self.b_in = sem("b_in")
        self.w_in = [sem(f"w_in{p}") for p in range(2)]
        self.turned = sem("turned")
        self.w_copied = sem("w_copied")
        self.hidden_ready = sem("hidden_ready")
        self.gelu_done = sem("gelu_done")
        self.out_ready = sem("out_ready")
        self.part = sb("part", [P, 2, S])
        self.out_copied = sem("out_copied")
        self.b_added = sem("b_added")
        self.added = sem("added")

    def banks(self, wide, out, ctx):
        self.hidden, self.out = wide, out

    def load(self, sp):
        dram, net = self.net.dram, self.net
        fc1 = dram["L2_ffn_fc1_w"].rearrange("e (j p) c -> e p j c", p=P)
        fc2 = dram["L2_ffn_fc2_w"].rearrange("e (k p) h -> e p k h", p=P)
        sh1 = dram["L2_ffn_sh1_w"].rearrange("(u j p) c -> u p j c", p=P, u=2)
        sh2 = dram["L2_ffn_sh2_w"].rearrange("(k p) (u h) -> u p k h", p=P, u=2)

        def load(p, up, down):
            sp.dma_start(self.up_in[p][:, :, :], up).then_inc(self.w_in[p], 16)
            sp.dma_start(self.down_in[p][:, :, :], down).then_inc(self.w_in[p], 16)
        for e in range(2):
            load(e, fc1[e], fc2[e])
        sp.dma_start(self.b2[:, :], dram["L2_ffn_sh2_b"].partition_broadcast(P)).then_inc(self.b_in, 16)
        with net.nc.allow_non_contiguous_dma(reason="bias columns"):
            sp.dma_start(self.b1[:, :], dram["L2_ffn_sh1_b"].rearrange("(j p) -> p j", p=P)
                         ).then_inc(self.b_in, 16)
        with sp.Fori(1, E // 2) as i:
            for p in range(2):
                e = i * 2 + p
                sp.wait_ge(self.turned, e * 2 - 2)
                net.go_on(sp)
                load(p, fc1[ds(e, 1)].rearrange("e p j c -> p (e j) c"),
                     fc2[ds(e, 1)].rearrange("e p k h -> p (e k) h"))
        for h in range(2):
            sp.wait_ge(self.turned, (E + h) * 2 - 2)
            load(h, sh1[h], sh2[h])

    def turn_weights(self, pe):
        ident = self.net.ident

        def turn(u, p, first, earliest):
            pe.wait_ge(self.w_in[p], (u - p) * 16 + 32)
            if not first:
                pe.wait_ge(self.w_copied, u * 2 - 3)
            for k in range(KC):
                for j in range(4):
                    last = pe.transpose(self.out[:, p, k, j * P:(j + 1) * P],
                                        self.up_in[p][:, j, k * P:(k + 1) * P], ident[:, :])
            last.then_inc(self.turned, 1)
            if not earliest:
                pe.wait_ge(self.w_copied, u * 2)
            for j in range(4):
                for k in range(KC):
                    at = (j % 2) * C + k * P
                    last = pe.transpose(self.hidden[:, j // 2, at:at + P],
                                        self.down_in[p][:, k, j * P:(j + 1) * P], ident[:, :])
            last.then_inc(self.turned, 1)
        turn(0, 0, True, True)
        turn(1, 1, True, False)
        with pe.Fori(1, E // 2 + 1) as i:
            for p in range(2):
                turn(i * 2 + p, p, False, False)
        pe.wait_ge(self.w_copied, (E + 2) * 2)

    def up(self, pe, b, p, first, between=None):
        for j in range(self.SH):
            if not (first and j < 2):
                pe.wait_ge(self.gelu_done, b * self.SH + j - 1)
            for k in range(KC):
                last = pe.matmul(self.hidden[:, j % 2, :], self.sh1[:, k, j * P:(j + 1) * P],
                                 self.net.xT[:, k, ds(b * S, S)], start=k == 0, stop=k == KC - 1)
            last.then_inc(self.hidden_ready, 1)
            if between is not None and j % 2 == 1:
                between(j // 2)

    def down(self, pe, b, p, first, between):
        pe.wait_ge(self.gelu_done, b * self.SH + self.SH)
        if not first:
            pe.wait_ge(self.out_copied, b - 1)
        for t in range(TB):
            for j in range(self.SH):
                last = pe.matmul(self.out[:, p, t // 2, (t % 2) * C:(t % 2 + 1) * C],
                                 self.active[p][:, j, t * P:(t + 1) * P], self.sh2[:, j, :],
                                 start=j == 0, stop=j == self.SH - 1)
            if t == TB - 1:
                last.then_inc(self.out_ready, 1)
            between(t)

    def round(self, pe, b, p, first, between):
        self.up(pe, b + 1, 1 - p, False, between)
        self.down(pe, b, p, first, lambda t: between(4 + t))

    def activate(self, act):
        def copy_weights(u, w1, w2, p):
            act.wait_ge(self.turned, u * 2 + 1)
            act.activation(w1, self.out[:, p, :, :], ACT.Copy).then_inc(self.w_copied, 1)
            act.wait_ge(self.turned, u * 2 + 2)
            act.activation(w2, self.hidden[:, :, :].rearrange("p b (j c) -> p (b j) c", c=C), ACT.Copy
                           ).then_inc(self.w_copied, 1)

        def gelus(b, p, first):
            if not first:
                act.wait_ge(self.out_ready, b - 1)
            for j in range(self.SH):
                act.wait_ge(self.hidden_ready, b * self.SH + j + 1)
                act.activation(self.active[p][:, j, :], self.hidden[:, j % 2, :], ACT.Gelu,
                               bias=self.b1[:, j:j + 1]).then_inc(self.gelu_done, 1)

        def copy_out(b, p, first):
            act.wait_ge(self.out_ready, b + 1)
            if not first:
                act.wait_ge(self.added, b)
            act.activation(self.part[:, :, :], self.out[:, p, :, :], ACT.Copy).then_inc(self.out_copied, 1)
        with act.Fori(0, E // 2) as i:
            for p in range(2):
                e = i * 2 + p
                copy_weights(e, self.w1[:, :, ds(e, 1), :].rearrange("p k e h -> p k (e h)"),
                             self.w2[:, ds(e, 1), :, :].rearrange("p e j c -> p (e j) c"), p)
        for h in range(2):
            copy_weights(E + h, self.sh1[:, :, h * 4 * P:(h + 1) * 4 * P], self.sh2[:, h * 4:(h + 1) * 4, :], h)
        act.wait_ge(self.b_in, 32)
        gelus(0, 0, True)
        gelus(1, 1, True)
        copy_out(0, 0, True)
        gelus(2, 0, False)
        with act.Fori(1, B // 2 - 1) as i:
            for p in range(2):
                copy_out(i * 2 + p - 1, 1 - p, False)
                gelus(i * 2 + p + 1, 1 - p, False)
        copy_out(B - 3, 1, False)
        gelus(B - 1, 1, False)
        copy_out(B - 2, 0, False)
        copy_out(B - 1, 1, False)

    def add(self, pool):
        pool.wait_ge(self.b_in, 32)
        with pool.Fori(0, B) as b:
            x_b = self.net.x[:, ds(b * TB, TB), :]
            pool.tensor_tensor(x_b, x_b, self.b2[:, :].unsqueeze(1).to_broadcast([P, TB, C]), ALU.add
                               ).then_inc(self.b_added, 1)
        pool.wait_ge(self.b_added, B)
        with pool.Fori(0, B // 2) as i:
            for p in range(2):
                b = i * 2 + p
                x_b = self.net.x[:, ds(b * TB, TB), :].rearrange("p (b t) c -> p b (t c)", b=2)
                pool.wait_ge(self.out_copied, b + 1)
                self.net.go_on(pool)
                pool.tensor_tensor(x_b, self.part[:, :, :], x_b, ALU.add).then_inc(self.added, 1)


def experts(net, layer, rows, total, w1, w2, tables):
    nc = net.nc
    tag = f"L{layer}_experts"
    FF = w1.shape[3]
    FC = FF // P
    FN = FF // 512
    func = ACT.Gelu if layer == 2 else ACT.Relu
    with ExitStack() as ctx:
        sb = lambda name, shape, dt=F32: net.sb(f"{tag}_{name}", shape, dt, ctx)
        sem = lambda name: net.sem(f"{tag}_{name}")
        token = [sb(f"token{j}", [P, C]) for j in range(4)]
        take = [sb(f"take{j}", [P, 1], I32) for j in range(4)]
        give = [sb(f"give{j}", [P, 1], I32) for j in range(2)]
        tokenT = [sb(f"tokenT{j}", [P, KC, P]) for j in range(2)]
        hidden = sb("hidden", [P, FF])
        hiddenT = sb("hiddenT", [P, FC, P])
        biased = [sb(f"biased{j}", [P, C]) for j in range(2)]
        result = [sb(f"result{j}", [P, C]) for j in range(2)]
        ps_x = net.ps(f"{tag}_ps_x", [P, KC, P], F32, ctx)
        ps_h = net.ps(f"{tag}_ps_h", [P, FN, 512], F32, ctx)
        ps_t = net.ps(f"{tag}_ps_t", [P, FC, P], F32, ctx)
        ps_y = [net.ps(f"{tag}_ps_y{j}", [P, 512], F32, ctx) for j in range(2)]
        take_ready = sem("take_ready")
        give_ready = sem("give_ready")
        zero = sb("zero", [P, C])
        zeroed = sem("zeroed")
        total_stored = sem("total_stored")
        b1, b2 = sb("b1", [P, E, FC]), sb("b2", [P, E, C])
        b_in = sem("b_in")
        b_names = ("L2_ffn_fc1_b", "L2_ffn_fc2_b") if layer == 2 else ("L3_ffn_b1", "L3_ffn_b2")
        gathered = [sem(f"gathered{j}") for j in range(4)]
        added = [sem(f"added{j}") for j in range(2)]
        x_turned = sem("x_turned")
        x_copied = sem("x_copied")
        h_ready = sem("h_ready")
        h_copied = sem("h_copied")
        h_turned = sem("h_turned")
        f_done = sem("f_done")
        y_ready = sem("y_ready")
        biased_ready = sem("biased_ready")
        y_done = sem("y_done")
        NS = SLOT_TILES

        def expert_of(engine, i):
            return engine.value_load(tables.expert[0:1, ds(i, 1)], min_val=0, max_val=E - 1)

        with nc.Block() as block:
            @block.sync
            def _(sp):
                for e in range(E):
                    with nc.allow_non_contiguous_dma(reason="bias columns"):
                        sp.dma_start(b1[:, e, :], net.dram[b_names[0]][e].rearrange("(j p) -> p j", p=P)
                                     ).then_inc(b_in, 16)
                    sp.dma_start(b2[:, e, :], net.dram[b_names[1]][e].partition_broadcast(P)).then_inc(b_in, 16)
                sp.dma_start(total[0:TOK, :].rearrange("(u p) c -> p u c", p=P), net.x[:, :, :]
                             ).then_inc(total_stored, 16)
                sp.wait_ge(zeroed, 1)
                sp.dma_start(total[TOK:TOK + P, :], zero[:, :]).then_inc(total_stored, 16)
                sp.wait_ge(total_stored, 32)

            @block.gpsimd
            def _(pool):
                def gather(i, j, first):
                    if not first:
                        pool.wait_ge(x_turned, i - 3)
                        net.go_on(pool)
                    pool.tensor_copy(take[j][:, :], tables.take[:, ds(i, 1)]).then_inc(take_ready, 1)
                    pool.wait_ge(take_ready, i + 1)
                    net.go_on(pool)
                    pool.indirect_dma_start(out=token[j][:, :], out_offset=None, in_=rows,
                                            in_offset=bass.IndirectOffsetOnAxis(ap=take[j][:, 0:1], axis=0)
                                            ).then_inc(gathered[j], 16)

                def scatter(i, j, first, second=False):
                    if not (first or second):
                        pool.wait_ge(added[j % 2], (i - j % 2) * 8)
                        net.go_on(pool)
                    pool.tensor_copy(give[j % 2][:, :], tables.give[:, ds(i, 1)]).then_inc(give_ready, 1)
                    pool.wait_ge(give_ready, i + 1)
                    pool.wait_ge(y_done, i + 1)
                    if not first:
                        pool.wait_ge(added[(j + 1) % 2], (i - 1 - (j + 1) % 2) * 8 + 16)
                    net.go_on(pool)
                    pool.indirect_dma_start(out=total, out_offset=bass.IndirectOffsetOnAxis(
                        ap=give[j % 2][:, 0:1], axis=0), in_=result[j % 2][:, :], in_offset=None,
                        compute_op=ALU.add).then_inc(added[j % 2], 16)
                for i in range(4):
                    gather(i, i, True)
                pool.wait_ge(total_stored, 32)
                scatter(0, 0, True)
                for i in range(1, 4):
                    gather(i + 3, (i + 3) % 4, False)
                    scatter(i, i, False, i == 1)
                with pool.Fori(1, NS // 4 - 1) as r:
                    for j in range(4):
                        gather(r * 4 + j + 3, (j + 3) % 4, False)
                        scatter(r * 4 + j, j, False)
                gather(NS - 1, 3, False)
                for j in range(4):
                    scatter(NS - 4 + j, j, False)
                for j in range(2):
                    pool.wait_ge(added[j], NS // 2 * 16)

            @block.tensor
            def _(pe):
                def turn_x(i, j, first):
                    pe.wait_ge(gathered[j], (i - j) * 4 + 16)
                    if not first:
                        pe.wait_ge(x_copied, i)
                    for k in range(KC):
                        last = pe.transpose(ps_x[:, k, :], token[j][:, k * P:(k + 1) * P], net.ident[:, :])
                    last.then_inc(x_turned, 1)

                def up(i, j, first):
                    e = expert_of(pe, i)
                    pe.wait_ge(x_copied, i + 1)
                    if not first:
                        pe.wait_ge(h_copied, i)
                    for n in range(FN):
                        for k in range(KC):
                            last = pe.matmul(ps_h[:, n, :], tokenT[j % 2][:, k, :],
                                             w1[:, k, ds(e, 1), n * 512:(n + 1) * 512],
                                             start=k == 0, stop=k == KC - 1)
                    last.then_inc(h_ready, 1)

                def turn_h(i, first):
                    pe.wait_ge(h_copied, i + 1)
                    if not first:
                        pe.wait_ge(f_done, i)
                    for c in range(FC):
                        last = pe.transpose(ps_t[:, c, :], hidden[:, c * P:(c + 1) * P], net.ident[:, :])
                    last.then_inc(h_turned, 1)

                def down(i, j, first):
                    e = expert_of(pe, i)
                    pe.wait_ge(f_done, i + 1)
                    if not first:
                        pe.wait_ge(y_done, i - 1)
                    for c in range(FC):
                        last = pe.matmul(ps_y[j % 2][:, 0:C], hiddenT[:, c, :], w2[:, ds(e, 1), c, :],
                                         start=c == 0, stop=c == FC - 1)
                    last.then_inc(y_ready, 1)

                def tile(i, j, first=False, second=False, more=2):
                    turn_h(i, first)
                    if more >= 1:
                        up(i + 1, j + 1, False)
                    if more >= 2:
                        turn_x(i + 2, (j + 2) % 4, False)
                    down(i, j, first or second)
                turn_x(0, 0, True)
                turn_x(1, 1, False)
                up(0, 0, True)
                for i in range(4):
                    tile(i, i, first=i == 0, second=i == 1)
                with pe.Fori(1, NS // 4 - 1) as r:
                    for j in range(4):
                        tile(r * 4 + j, j)
                for j in range(4):
                    tile(NS - 4 + j, j, more=3 - j)

            @block.scalar
            def _(act):
                def apply(i, first):
                    e = expert_of(act, i)
                    act.wait_ge(h_turned, i + 1)
                    if not first:
                        act.wait_ge(y_ready, i)
                    net.go_on(act)
                    for c in range(FC):
                        last = act.activation(hiddenT[:, c, :], ps_t[:, c, :], func, bias=b1[:, ds(e, 1), c])
                    last.then_inc(f_done, 1)
                act.wait_ge(b_in, 2 * E * 16)
                apply(0, True)
                with act.Fori(1, NS) as i:
                    apply(i, False)

            @block.vector
            def _(dve):
                def copy_x(i, j, first):
                    dve.wait_ge(x_turned, i + 1)
                    if not first:
                        dve.wait_ge(h_ready, i - 1)
                    dve.tensor_copy(tokenT[j % 2][:, :, :], ps_x[:, :, :]).then_inc(x_copied, 1)

                def copy_h(i, first):
                    dve.wait_ge(h_ready, i + 1)
                    if not first:
                        dve.wait_ge(h_turned, i)
                    dve.tensor_copy(hidden[:, :], ps_h[:, :, :].rearrange("p n f -> p (n f)")).then_inc(h_copied, 1)

                def weigh(i, j, first):
                    e = expert_of(dve, i)
                    dve.wait_ge(y_ready, i + 1)
                    dve.tensor_tensor(biased[j % 2][:, :], ps_y[j % 2][:, 0:C], b2[:, ds(e, 1), :], ALU.add
                                      ).then_inc(biased_ready, 1)
                    dve.wait_ge(biased_ready, i + 1)
                    if not first:
                        dve.wait_ge(added[j % 2], (i - j % 2) * 8)
                    dve.tensor_scalar(result[j % 2][:, :], biased[j % 2][:, :], tables.weight[:, ds(i, 1)], None,
                                      ALU.mult).then_inc(y_done, 1)

                def tile(i, j, first=False, more=2):
                    if more >= 1:
                        copy_h(i + 1, False)
                    if more >= 2:
                        copy_x(i + 2, j, False)
                    weigh(i, j, first)
                dve.memset(zero[:, :], 0.0).then_inc(zeroed, 1)
                copy_x(0, 0, True)
                copy_x(1, 1, True)
                copy_h(0, True)
                dve.wait_ge(b_in, 2 * E * 16)
                for i in range(2):
                    tile(i, i, first=True)
                with dve.Fori(1, NS // 2 - 1) as r:
                    for j in range(2):
                        tile(r * 2 + j, j)
                tile(NS - 2, 0, more=1)
                tile(NS - 1, 1, more=0)


def read_back(net, tag, total):
    loaded = [net.sem(f"{tag}_read_back{b}") for b in range(B)]
    stats_step = net.sem(f"{tag}_stats_step")
    with net.nc.Block() as block:
        @block.sync
        def _(sp):
            for b in range(B):
                sp.dma_start(net.x[:, b * TB:(b + 1) * TB, :],
                             total[b * S:(b + 1) * S, :].rearrange("(u p) c -> p u c", p=P)).then_inc(loaded[b], 16)
            for b in range(B):
                sp.wait_ge(loaded[b], 16)

        @block.vector
        def _(dve):
            for b in range(B):
                dve.wait_ge(loaded[b], 16)
                token_stats(net, dve, b, stats_step)


def ffn_block(net, layer, total):
    tag = f"L{layer}_moe"
    rows = net.nc.dram_tensor(f"{tag}_rows", (TOK, C), F32).ap()
    FF = 512 if layer == 2 else 1024
    FC = FF // P
    with ExitStack() as ctx:
        tables = Tables(net, tag, ctx)
        w1 = net.sb(f"{tag}_w1", [P, KC, E, FF], F32, ctx)
        w2 = net.sb(f"{tag}_w2", [P, E, FC, C], F32, ctx)
        with ExitStack() as early:
            net.hold_channels(tag, early)
            layer_norm(net, f"{tag}_ln", rows)
            if layer == 2:
                route(net, layer, tables, shared=SharedExpert(net, w1, w2, early))
            else:
                w1_in = net.dram["L3_ffn_w1"].rearrange("e (k p) f -> k p e f", p=P)
                w2_in = net.dram["L3_ffn_w2"].rearrange("e (j p) c -> e p j c", p=P)
                route(net, layer, tables, early_loads=[(w1[:, k], w1_in[k]) for k in range(KC)]
                      + [(w2[:, e], w2_in[e]) for e in range(E)])
        experts(net, layer, rows, total, w1, w2, tables)


def build(nc, dram, out):
    with ExitStack() as ctx:
        net = Net(nc, ctx, dram)
        conv_layers(net)
        net.clear_semaphores()
        attention_block(net, 2)
        net.clear_semaphores()
        total = nc.dram_tensor("L2_moe_total", (TOK + P, C), F32).ap()
        ffn_block(net, 2, total)
        read_back(net, "L2_moe", total)
        net.clear_semaphores()
        attention_block(net, 3)
        net.clear_semaphores()
        ffn_block(net, 3, out)


def kernel(**inputs):
    import concourse.bacc as _bacc
    from concourse.bass_utils import run_bass_kernel_spmd as _run

    nc = _bacc.Bacc("TRN2", target_bir_lowering=False, num_devices=1)
    arrays = {k: np.ascontiguousarray(v) for k, v in inputs.items()}
    arrays.update(host_constants())
    dram = {k: nc.dram_tensor(k, v.shape, mybir.dt.from_np(v.dtype), kind="ExternalInput").ap()
            for k, v in arrays.items()}
    out = nc.dram_tensor("out", (TOK + P, C), F32, kind="ExternalOutput").ap()
    build(nc, dram, out)
    nc.finalize()
    r = _run(nc, [arrays], core_ids=[0])
    return r.results[0]["out"][:TOK].reshape(B, T, N, C)
```
